# Optimizing a Trainium2 kernel written in Bass

```python
import numpy as np
import jax
import jax.numpy as jnp

def _softmax(x, axis=-1):
    return jax.nn.softmax(x, axis=axis)

def _gelu(x):
    return jax.nn.gelu(x, approximate=True)

def _silu(x):
    return jax.nn.silu(x)

def _sigmoid(x):
    return jax.nn.sigmoid(x)

def _layernorm(x, axis=-1, eps=1e-05):
    m = jnp.mean(x, axis=axis, keepdims=True)
    v = jnp.var(x, axis=axis, keepdims=True)
    return (x - m) / jnp.sqrt(v + eps)

def _scatter_add(tgt, idx, src, axis=0):
    return tgt.at[idx].add(src)

def _segment_sum(src, seg, n):
    return jax.ops.segment_sum(src, seg, n)
kernel_name = 'mk_lm_tower_d1_tok_ids768_r4_d5831c'

def setup_inputs(seed: int=0):
    np.random.seed(seed)
    _w = jnp.asarray

    def _rec_inputs():
        import jax
        import jax.numpy as jnp
        _rk = jax.random.key(seed)
        x = jax.random.randint(jax.random.fold_in(_rk, 1), (16, 128), 0, 30522, jnp.int32)
        mask_BS_i1_0 = jnp.where(jnp.ones((16, 128), dtype=bool), 1, 0).astype(jnp.int32)
        return (x, mask_BS_i1_0)
    x, mask_BS_i1_0 = _rec_inputs()

    def _L0_tok_setup():
        import jax, jax.numpy as jnp
        import numpy as np
        VOCAB = 30522
        HIDDEN = 192
        MAX_POS = 128
        TYPE_VOCAB = 2
        EPS = 1e-05
        key = jax.random.key(seed)
        k1, k2, k3, k4, k5 = jax.random.split(key, 5)
        B, S = (32, 128)
        return {'input_ids': jax.random.randint(k1, (B, S), 0, VOCAB, dtype=jnp.int64 if jax.config.jax_enable_x64 else jnp.int32), 'token_type_ids': jax.random.randint(k2, (B, S), 0, TYPE_VOCAB, dtype=jnp.int32), 'tok_w': jax.random.normal(k3, (VOCAB, HIDDEN), dtype=jnp.float32), 'pos_w': jax.random.normal(k4, (MAX_POS, HIDDEN), dtype=jnp.float32), 'type_w': jax.random.normal(k5, (TYPE_VOCAB, HIDDEN), dtype=jnp.float32), 'gamma': jnp.ones((HIDDEN,), dtype=jnp.float32), 'beta': jnp.zeros((HIDDEN,), dtype=jnp.float32)}
    _L0_tok_all = _L0_tok_setup()
    _L0_tok_in = {k: v for k, v in _L0_tok_all.items() if k in ('tok_w', 'pos_w', 'type_w', 'gamma', 'beta')}
    del _L0_tok_all

    def _L0_attn_setup():
        import jax, jax.numpy as jnp
        import numpy as np
        B, N, C = (8, 1024, 192)
        H, M = (12, 64)
        D = C // H

        def iterative_inv(mat, n_iter=6):
            I = jnp.eye(mat.shape[-1], dtype=mat.dtype)
            K = mat
            scale = jnp.max(jnp.sum(K, axis=-2), axis=-1)[:, :, None, None]
            V = jnp.swapaxes(K, -1, -2) / scale
            for _ in range(n_iter):
                KV = K @ V
                V = 0.25 * V @ (13.0 * I - KV @ (15.0 * I - KV @ (7.0 * I - KV)))
            return V
        key = jax.random.key(seed)
        k1, k2, k3, k4 = jax.random.split(key, 4)
        s = 0.02
        return {'x': jax.random.normal(k1, (B, N, C), dtype=jnp.float32), 'w_qkv': jax.random.normal(k2, (3 * C, C), dtype=jnp.float32) * s, 'w_proj': jax.random.normal(k3, (C, C), dtype=jnp.float32) * s, 'b_proj': jax.random.normal(k4, (C,), dtype=jnp.float32) * s}
    _L0_attn_all = _L0_attn_setup()
    _L0_attn_in = {k: v for k, v in _L0_attn_all.items() if k in ('w_qkv', 'w_proj', 'b_proj')}
    del _L0_attn_all

    def _L0_ffn_setup():
        import jax, jax.numpy as jnp
        import numpy as np
        B, L, D = (4, 256, 192)
        E, S, H = (32, 32, 768)
        EPS = 1e-12

        def _l2norm(v, axis):
            n = jnp.sqrt(jnp.sum(v * v, axis=axis, keepdims=True))
            return v / jnp.maximum(n, EPS)
        key = jax.random.key(seed)
        ks = jax.random.split(key, 6)
        x = jax.random.normal(ks[0], (B, L, D), dtype=jnp.float32)
        phi = jax.random.normal(ks[1], (D, E, S), dtype=jnp.float32) / np.sqrt(D)
        scale = jnp.ones((1,), dtype=jnp.float32)
        w1 = jax.random.normal(ks[2], (E, D, H), dtype=jnp.float32) / np.sqrt(D)
        b1 = jax.random.normal(ks[3], (E, H), dtype=jnp.float32) * 0.01
        w2 = jax.random.normal(ks[4], (E, H, D), dtype=jnp.float32) / np.sqrt(H)
        b2 = jax.random.normal(ks[5], (E, D), dtype=jnp.float32) * 0.01
        return {'x': x, 'phi': phi, 'scale': scale, 'w1': w1, 'b1': b1, 'w2': w2, 'b2': b2}
    _L0_ffn_all = _L0_ffn_setup()
    _L0_ffn_in = {k: v for k, v in _L0_ffn_all.items() if k in ('phi', 'scale', 'w1', 'b1', 'w2', 'b2')}
    del _L0_ffn_all
    return {'x': x, 'mask_BS_i1_0': mask_BS_i1_0, 'L0_tok_tok_w': _L0_tok_in['tok_w'], 'L0_tok_pos_w': _L0_tok_in['pos_w'], 'L0_tok_type_w': _L0_tok_in['type_w'], 'L0_tok_gamma': _L0_tok_in['gamma'], 'L0_tok_beta': _L0_tok_in['beta'], 'L0_attn_w_qkv': _L0_attn_in['w_qkv'], 'L0_attn_w_proj': _L0_attn_in['w_proj'], 'L0_attn_b_proj': _L0_attn_in['b_proj'], 'L0_ffn_phi': _L0_ffn_in['phi'], 'L0_ffn_scale': _L0_ffn_in['scale'], 'L0_ffn_w1': _L0_ffn_in['w1'], 'L0_ffn_b1': _L0_ffn_in['b1'], 'L0_ffn_w2': _L0_ffn_in['w2'], 'L0_ffn_b2': _L0_ffn_in['b2']}

def reference(x, mask_BS_i1_0, L0_tok_tok_w, L0_tok_pos_w, L0_tok_type_w, L0_tok_gamma, L0_tok_beta, L0_attn_w_qkv, L0_attn_w_proj, L0_attn_b_proj, L0_ffn_phi, L0_ffn_scale, L0_ffn_w1, L0_ffn_b1, L0_ffn_w2, L0_ffn_b2):
    import jax
    import jax.numpy as jnp

    def _L0_tok_ref(input_ids, token_type_ids, tok_w, pos_w, type_w, gamma, beta):
        import jax, jax.numpy as jnp
        import numpy as np
        VOCAB = 30522
        HIDDEN = 192
        MAX_POS = 128
        TYPE_VOCAB = 2
        EPS = 1e-05
        S = input_ids.shape[-1]
        emb = tok_w[input_ids] + pos_w[jnp.arange(S)] + type_w[token_type_ids]
        mean = jnp.mean(emb, axis=-1, keepdims=True)
        var = jnp.mean(jnp.square(emb - mean), axis=-1, keepdims=True)
        out = (emb - mean) * gamma * jax.lax.rsqrt(var + EPS) + beta
        return out

    def _L0_attn_ref(x, w_qkv, w_proj, b_proj):
        import jax, jax.numpy as jnp
        import numpy as np
        B, N, C = (8, 1024, 192)
        H, M = (12, 64)
        D = C // H

        def iterative_inv(mat, n_iter=6):
            I = jnp.eye(mat.shape[-1], dtype=mat.dtype)
            K = mat
            scale = jnp.max(jnp.sum(K, axis=-2), axis=-1)[:, :, None, None]
            V = jnp.swapaxes(K, -1, -2) / scale
            for _ in range(n_iter):
                KV = K @ V
                V = 0.25 * V @ (13.0 * I - KV @ (15.0 * I - KV @ (7.0 * I - KV)))
            return V
        b, n, c = x.shape
        qkv = (x @ w_qkv.T).reshape(b, n, 3, H, D).transpose(2, 0, 3, 1, 4)
        Q, K, V = (qkv[0], qkv[1], qkv[2])
        Q = Q / D ** 0.5
        Kl = K.reshape(b, H, M, n // M, D).mean(axis=-2)
        Ql = Q.reshape(b, H, M, n // M, D).mean(axis=-2)
        kernel1 = jax.nn.softmax(jnp.einsum('bhnd,bhmd->bhnm', Q, Kl), axis=-1)
        kernel2 = jax.nn.softmax(jnp.einsum('bhmd,bhld->bhml', Ql, Kl), axis=-1)
        kernel3 = jax.nn.softmax(jnp.einsum('bhmd,bhnd->bhmn', Ql, K), axis=-1)
        SV = kernel1 @ iterative_inv(kernel2) @ (kernel3 @ V)
        SV = SV.transpose(0, 2, 1, 3).reshape(b, n, c)
        out = SV @ w_proj.T + b_proj
        out = out + V.transpose(0, 2, 1, 3).reshape(b, n, c)
        return out

    def _L0_ffn_ref(x, phi, scale, w1, b1, w2, b2):
        import jax, jax.numpy as jnp
        import numpy as np
        B, L, D = (4, 256, 192)
        E, S, H = (32, 32, 768)
        EPS = 1e-12

        def _l2norm(v, axis):
            n = jnp.sqrt(jnp.sum(v * v, axis=axis, keepdims=True))
            return v / jnp.maximum(n, EPS)
        b, l, d = x.shape
        xn = _l2norm(x, axis=2)
        phin = scale * _l2norm(phi, axis=0)
        logits = jnp.einsum('bld,des->bles', xn, phin)
        d_w = jax.nn.softmax(logits, axis=-1)
        c_w = jax.nn.softmax(logits.reshape(b, l, E * S), axis=-1)
        slots = jnp.einsum('bld,bles->besd', xn, d_w)
        h = jax.nn.gelu(jnp.einsum('besd,edh->besh', slots, w1) + b1[:, None, :], approximate=False)
        eo = jnp.einsum('besh,ehd->besd', h, w2) + b2[:, None, :]
        eo = eo.reshape(b, E * S, d)
        return jnp.einsum('bkd,blk->bld', eo, c_w)
    h = _L0_tok_ref(x, mask_BS_i1_0, L0_tok_tok_w, L0_tok_pos_w, L0_tok_type_w, L0_tok_gamma, L0_tok_beta)
    h = h + _L0_attn_ref(_layernorm(h, axis=-1), L0_attn_w_qkv, L0_attn_w_proj, L0_attn_b_proj)
    h = h + _L0_ffn_ref(_layernorm(h, axis=-1), L0_ffn_phi, L0_ffn_scale, L0_ffn_w1, L0_ffn_b1, L0_ffn_w2, L0_ffn_b2)
    return h

_drawn_inputs = setup_inputs


def setup_inputs(seed=0):
    import zlib

    import numpy as np

    out = dict(_drawn_inputs(seed))
    spreads = {'L0_tok_gamma': (1.0, 0.2), 'L0_tok_beta': (0.0, 0.1)}
    factors = {'L0_attn_b_proj': 3.22,
     'L0_ffn_phi': 64.0,
     'L0_ffn_w1': 4.397,
     'L0_ffn_b1': 8.0,
     'L0_ffn_w2': 4.35,
     'L0_ffn_b2': 35.862}
    for name, (base, spread) in spreads.items():
        noise = np.random.default_rng([zlib.crc32(name.encode()), seed]).standard_normal(out[name].shape)
        drawn = base * np.exp(spread * noise) if base else spread * noise
        out[name] = jnp.asarray(drawn.astype(out[name].dtype))
    for name, factor in factors.items():
        out[name] = (out[name] * factor).astype(out[name].dtype)
    return out
```

```python
from contextlib import ExitStack

import concourse.bass as bass
from concourse import mybir

F32 = mybir.dt.float32
F32R = mybir.dt.float32r
I32 = mybir.dt.int32
ALU = mybir.AluOpType
ACT = mybir.ActivationFunctionType
AX = mybir.AxisListType

P = 128
LN_EPS = 1e-5
NORM_EPS2 = 1e-24


def build(nc, x, type_ids, tok_w, pos_w, type_w, gamma, beta, w_qkv, w_proj, b_proj,
          phi, scale, w1, b1, w2, b2, out):
    B, S = x.shape
    C = tok_w.shape[1]
    C0, C1 = P, C - P
    H, M = 12, 64
    D = C // H
    NP = H // 2
    GH = P // D
    E, SL = phi.shape[1], phi.shape[2]
    ES = E * SL
    HID = w1.shape[2]
    HC = HID // P
    R = B * SL
    GE = P // SL
    NG = E // GE
    ITERS = 6
    SW = M + D
    assert S == P and B % 4 == 0 and M == 64 and C1 == 64 and R == 512

    slots_dram = nc.dram_tensor("slots_dram", [E, C, R], F32).ap()
    comb_dram = nc.dram_tensor("comb_dram", [NG, P, B, S], F32).ap()

    with ExitStack() as ctx:
        def sb(name, shape, dt=F32, where=ctx):
            return where.enter_context(nc.sbuf_tensor(name, shape, dt))

        h = sb("h", [P, B, C])
        ident = sb("ident", [P, P])
        b1T = sb("b1T", [P, E * HC])
        w1raw = [sb(f"w1raw{q}", [P, 2, HID]) for q in range(2)]
        w2raw = [sb(f"w2raw{q}", [P, HC, C]) for q in range(2)]
        b2row = [sb(f"b2row{q}", [P, C]) for q in range(2)]

        front = ExitStack()
        fb = lambda name, shape, dt=F32: sb(name, shape, dt, front)
        ids = fb("ids", [P, B], I32)
        tids = fb("tids", [P, B], I32)
        tidf = fb("tidf", [P, B])
        pos = fb("pos", [P, C])
        ty = fb("ty", [P, 2, C])
        gam = fb("gam", [P, C])
        bet = fb("bet", [P, C])
        bpr = fb("bpr", [P, C])
        scl = fb("scl", [P, 1])
        expo = fb("expo", [P, 1])
        ones = fb("ones", [P, P])
        mask8 = fb("mask8", [P, GH, M])
        mask2 = fb("mask2", [P, 2, M])
        eye15 = fb("eye15", [P, NP, SW])
        wn = fb("wn", [96, 8, C])
        b1n = fb("b1n", [96, 2, P])
        wT = fb("wT", [P, 2, 256 + 256 + C])
        pT = fb("pT", [P, 2, C])
        phraw = fb("phraw", [P, 2, ES])
        phn = fb("phn", [P, ES])
        pht = fb("pht", [P, ES])
        ph_hi = fb("ph_hi", [P, ES], F32R)
        ph_lo = fb("ph_lo", [P, ES], F32R)
        ph_st = fb("ph_st", [P, ES], F32R)

        att = ExitStack()
        two = lambda name, shape, dt=F32, w=att: [sb(f"{name}{l}", shape, dt, w) for l in range(2)]
        xn = two("xn", [P, C])
        st6 = two("st6", [P, 6])
        mv = two("mv", [P, 2])
        ve = two("ve", [P, 1])
        rs = two("rs", [P, 1])
        xT = two("xT", [P, 2, P])
        qT = two("qT", [P, 2, P])
        kk = two("kk", [P, 2, P + M])
        v33 = two("v33", [P, NP, 2 * D + 1])
        ql = two("ql", [P, 2, M])
        kl = two("kl", [P, 2, M])
        qbd = two("qbd", [P, H, M])
        kbd = two("kbd", [P, H, M])
        m3 = two("m3", [P, NP])
        m2 = two("m2", [P, NP])
        m1 = two("m1", [P, H])
        e3 = two("e3", [P, NP, P])
        e2 = two("e2", [P, NP, M])
        e1 = two("e1", [P, H, M])
        s2 = two("s2", [P, NP])
        r2 = two("r2", [P, NP])
        k2 = two("k2", [P, NP, P])
        k2T = two("k2T", [P, NP, P])
        k3T = two("k3T", [P, NP, P])
        k1T = two("k1T", [P, NP, P])
        cs = two("cs", [P, NP])
        csm = two("csm", [NP, 2])
        csr = two("csr", [NP, 2])
        csb = two("csb", [NP, 2, M])
        r4 = two("r4", [P, NP])
        r25 = two("r25", [P, NP])
        u4 = two("u4", [P, NP])
        g = two("g", [P, NP, SW])
        gbd = two("gbd", [P, NP, P])
        ybd = two("ybd", [P, NP, P])
        tt = two("tt", [P, NP, SW])
        wf = two("wf", [P, NP, SW])
        aw = two("aw", [P, NP, D])
        wbd = two("wbd", [P, NP, 2 * D + 2])
        ro = two("ro", [P, NP, 2])
        sv = two("sv", [P, C])
        svT = two("svT", [P, 2, P])
        hb = two("hb", [P, C])
        att.close()

        rt = ExitStack()
        rx = two("rx", [P, C], w=rt)
        rst6 = two("rst6", [P, 6], w=rt)
        rmv = two("rmv", [P, 2], w=rt)
        rve = two("rve", [P, 1], w=rt)
        rrs = two("rrs", [P, 1], w=rt)
        rsq = two("rsq", [P, C], w=rt)
        rss = two("rss", [P, 1], w=rt)
        rsm = two("rsm", [P, 1], w=rt)
        rrn = two("rrn", [P, 1], w=rt)
        xe = two("xe", [P, 2 * P], w=rt)
        xe_hi = two("xe_hi", [P, 2 * P], F32R, rt)
        xe_lo = two("xe_lo", [P, 2 * P], F32R, rt)
        xt_hi = two("xt_hi", [P, 2, P], F32R, rt)
        xt_lo = two("xt_lo", [P, 2, P], F32R, rt)
        mx = two("mx", [P, E], w=rt)
        nm = two("nm", [P, 1], w=rt)
        fe = two("fe", [P, E], w=rt)
        ze = two("ze", [P, E], w=rt)
        rz = two("rz", [P, E], w=rt)
        zf = two("zf", [P, E], w=rt)
        zt = two("zt", [P, 1], w=rt)
        rzt = two("rzt", [P, 1], w=rt)
        fz = two("fz", [P, E], w=rt)
        lg = two("lg", [P, E, SL], w=rt)
        dw = two("dw", [P, E, SL], w=rt)
        dw_hi = two("dw_hi", [P, ES], F32R, rt)
        dw_lo = two("dw_lo", [P, ES], F32R, rt)
        cw = two("cw", [P, E, SL], w=rt)
        cwT = two("cwT", [P, 2, NG, P], w=rt)
        slm = sb("slm", [P, E, 4, SL], F32, rt)
        slr = sb("slr", [C1, E, 4, SL], F32, rt)
        rt.close()
        front.close()

        xsm = two("xsm", [P, 2, R], w=ctx)
        w1_hi = two("w1_hi", [P, HID], F32R, ctx)
        w1_lo = two("w1_lo", [P, HID], F32R, ctx)
        w1_st = two("w1_st", [P, HID], F32R, ctx)
        w2_hi = two("w2_hi", [P, HC, C], F32R, ctx)
        w2_lo = two("w2_lo", [P, HC, C], F32R, ctx)
        xs_hi = two("xs_hi", [P, 2, R], F32R, ctx)
        xs_lo = two("xs_lo", [P, 2, R], F32R, ctx)
        hraw = two("hraw", [P, R], w=ctx)
        h_hi = [sb(f"h_hi{k}", [P, R], F32R) for k in range(3)]
        h_lo = [sb(f"h_lo{k}", [P, R], F32R) for k in range(3)]
        eo = two("eo", [P, 4, C], w=ctx)
        eog = sb("eog", [P, B, C])
        cwg = sb("cwg", [P, B, S])

        ps = ctx.enter_context(nc.psum_tensor("ps", [P, 8, 512], F32))
        bank = [[ps[:, 4 * l + k, :] for k in range(4)] for l in range(2)]

        def sems(text):
            return [ctx.enter_context(nc.semaphore(n)) for n in text.split()]

        (ids_in, consts_in, tokens_in, phi_in, wn_in, comb_out0, comb_out1, slots_out, w1_in0, w1_in1,
         w2_in0, w2_in1, slots_in0, slots_in1, eog_in0, eog_in1, comb_in, y_out) = sems(
            "ids_in consts_in tokens_in phi_in wn_in comb_out0 comb_out1 slots_out w1_in0 w1_in1 w2_in0 "
            "w2_in1 slots_in0 slots_in1 eog_in0 eog_in1 comb_in y_out ")
        (i_zero, i_ident, i_const, i_pool, i_mask2, i_ty, i_wnT, i_wT, i_b1n, i_b1T, i_sq, i_ss, i_n, i_sqrt,
         i_phi) = sems(
            "i_zero i_ident i_const i_pool i_mask2 i_ty i_wnT i_wT i_b1n i_b1T i_sq i_ss i_n i_sqrt "
            "i_phi ")
        (a_emb, a_stat, a_mv, a_ve, a_rs, a_cen, a_h0, a_xn, a_xTp, a_xT, a_qkp, a_vp, a_q, a_k, a_v, a_ql,
         a_kl, a_qbd, a_kbd, a_kk, a_s3, a_s1, a_m3, a_m2, a_d3, a_d2, a_m1, a_d1, a_e3, a_e2, a_e1, a_sum2,
         a_r2, a_k2, a_k3p, a_k3T, a_k2p, a_k2T, a_csT, a_csm, a_csr, a_csb, a_sb, a_r4, a_res, a_hv, a_x0,
         a_up, a_u4, a_gw, a_g0, a_gbd, a_wf, a_A, a_y, a_T, a_Z, a_G, a_fix, a_k1p, a_k1T, a_v0, a_wbd, a_o,
         a_ro, a_sv, a_svp, a_svT, a_pr, a_hb, a_h1) = sems(
            "a_emb a_stat a_mv a_ve a_rs a_cen a_h0 a_xn a_xTp a_xT a_qkp a_vp a_q a_k a_v a_ql a_kl "
            "a_qbd a_kbd a_kk a_s3 a_s1 a_m3 a_m2 a_d3 a_d2 a_m1 a_d1 a_e3 a_e2 a_e1 a_sum2 a_r2 a_k2 "
            "a_k3p a_k3T a_k2p a_k2T a_csT a_csm a_csr a_csb a_sb a_r4 a_res a_hv a_x0 a_up a_u4 a_gw "
            "a_g0 a_gbd a_wf a_A a_y a_T a_Z a_G a_fix a_k1p a_k1T a_v0 a_wbd a_o a_ro a_sv a_svp a_svT "
            "a_pr a_hb a_h1 ")
        (r_stat, r_mv, r_ve, r_rs, r_x, r_ss, r_sm, r_rn, r_xe, r_xtp, r_xth, r_xtl, r_xeh, r_xel, r_lg,
         r_mx, r_nm, r_f, r_d, r_exp, r_z, r_rz, r_zf, r_zt, r_rzt, r_fz, r_dw, r_dh, r_dl, r_sm_p, r_sr_p,
         r_slm, r_slr, r_cw, r_cwp, r_cwT) = sems(
            "r_stat r_mv r_ve r_rs r_x r_ss r_sm r_rn r_xe r_xtp r_xth r_xtl r_xeh r_xel r_lg r_mx r_nm "
            "r_f r_d r_exp r_z r_rz r_zf r_zt r_rzt r_fz r_dw r_dh r_dl r_sm_p r_sr_p r_slm r_slr r_cw "
            "r_cwp r_cwT ")
        (c_hi, c_lo_w1, c_lo_xs, c_lo_w2, c_hidden, c_gelu, c_hhi, c_hlo, c_output, c_eo, c_comb_ps, c_comb) = sems(
            "c_hi c_lo_w1 c_lo_xs c_lo_w2 c_hidden c_gelu c_hhi c_hlo c_output c_eo c_comb_ps c_comb ")
        comb_out = [comb_out0, comb_out1]
        w1_in, w2_in = [w1_in0, w1_in1], [w2_in0, w2_in1]
        slots_in, eog_in = [slots_in0, slots_in1], [eog_in0, eog_in1]

        stage_free = ctx.enter_context(nc.semaphore("stage_free"))
        waited = ctx.enter_context(nc.semaphore("waited"))

        block = ctx.enter_context(nc.Block())

        def half(t, lane_half):
            return t[64 * lane_half:64 * lane_half + 64]

        def bc(ap, shape):
            return ap.to_broadcast(shape)

        @block.sync
        def _(sp):
            sp.dma_start(ids[:, :], x.rearrange("b s -> s b"), allow_slow_non_contiguous=True).then_inc(ids_in, 16)
            sp.dma_start(tids[:, :], type_ids.rearrange("b s -> s b"), allow_slow_non_contiguous=True).then_inc(consts_in, 16)
            sp.dma_start(pos[:, :], pos_w).then_inc(consts_in, 16)
            sp.dma_start(ty[:, :, :], type_w.rearrange("(o t) c -> o t c", o=1).to_broadcast([P, 2, C])).then_inc(consts_in, 16)
            for t, v in ((gam, gamma), (bet, beta), (bpr, b_proj)):
                sp.dma_start(t[:, :], v.rearrange("(o c) -> o c", o=1).to_broadcast([P, C])).then_inc(consts_in, 16)
            sp.dma_start(scl[:, :], scale.rearrange("(o c) -> o c", o=1).to_broadcast([P, 1])).then_inc(consts_in, 16)
            sp.dma_start(wn[:, 0:6, :], w_qkv.rearrange("(t p) c -> p t c", p=96)).then_inc(wn_in, 16)
            sp.dma_start(wn[:, 6:8, :], w_proj.rearrange("(t p) c -> p t c", p=96)).then_inc(wn_in, 16)
            sp.dma_start(b1n[:, :, :], b1.rearrange("e (c q) -> (e c) q", q=P).rearrange("(t p) q -> p t q", p=96)).then_inc(wn_in, 16)
            phv = phi.rearrange("d e s -> d (e s)")
            sp.dma_start(phraw[:, 0, :], phv[0:C0, :]).then_inc(phi_in, 16)
            for q in range(2):
                sp.dma_start(half(phraw, q)[:, 1, :], phv[C0:C, :]).then_inc(phi_in, 16)

            def load_weights(e, q):
                sp.dma_start(w1raw[q][:, 0, :], w1[bass.ds(e, 1), 0:C0, :].rearrange("o d h -> d (o h)")).then_inc(w1_in[q], 16)
                for k in range(2):
                    sp.dma_start(half(w1raw[q], k)[:, 1, :], w1[bass.ds(e, 1), C0:C, :].rearrange("o d h -> d (o h)")).then_inc(w1_in[q], 16)
                sp.dma_start(w2raw[q][:, :, :], w2[bass.ds(e, 1), :, :].rearrange("o (c p) d -> p (o c) d", p=P)).then_inc(w2_in[q], 16)
                sp.dma_start(b2row[q][:, :], b2[bass.ds(e, 1), :].to_broadcast([P, C])).then_inc(w2_in[q], 16)

            def load_slots(e, q):
                sp.dma_start(xsm[q][:, 0, :], slots_dram[bass.ds(e, 1), 0:C0, :].rearrange("o d h -> d (o h)")).then_inc(slots_in[q], 16)
                for k in range(2):
                    sp.dma_start(half(xsm[q], k)[:, 1, :], slots_dram[bass.ds(e, 1), C0:C, :].rearrange("o d h -> d (o h)")).then_inc(slots_in[q], 16)

            for q in range(2):
                load_weights(q, q)

            sp.sem_inc(stage_free, 1)
            with sp.Fori(0, B // 4) as i:
                for hf in range(2):
                    for l in range(2):
                        sp.wait_ge(r_cwT, 4 * i + 2 * hf + l + 1)
                        sp.sem_inc(waited, 1)
                        sp.dma_start(comb_dram[:, :, bass.ds(4 * i + 2 * hf + l, 1), :].rearrange("g p o l -> p g (o l)"),
                                     cwT[l][:, hf, :, :]).then_inc(comb_out[l], 16)
                sp.wait_ge(r_slm, 4 * i + 4)
                sp.wait_ge(r_slr, 4 * i + 4)
                sp.sem_inc(waited, 1)
                sp.dma_start(slots_dram[:, 0:C0, bass.ds(i * (4 * SL), 4 * SL)].rearrange("e d r -> d e r"),
                             slm[:, :, :, :].rearrange("d e b s -> d e (b s)")).then_inc(slots_out, 16)
                sp.dma_start(slots_dram[:, C0:C, bass.ds(i * (4 * SL), 4 * SL)].rearrange("e d r -> d e r"),
                             slr[:, :, :, :].rearrange("d e b s -> d e (b s)")).then_inc(slots_out, 16)
                sp.wait_ge(slots_out, 32 * i + 32)
                for l in range(2):
                    sp.wait_ge(comb_out[l], 32 * i + 32)
                sp.sem_inc(stage_free, 1)
            sp.wait_ge(slots_out, 32 * (B // 4))
            for l in range(2):
                sp.wait_ge(comb_out[l], 16 * (B // 2))
            for q in range(2):
                load_slots(q, q)

            def group(gr, last):
                for j in range(GE):
                    e, q = gr * GE + j, j % 2
                    if not (last and j >= 2):
                        sp.wait_ge(c_hi, 5 * e + 5)
                        sp.sem_inc(waited, 1)
                        sp.wait_ge(c_lo_w1, 2 * e + 2)
                        sp.sem_inc(waited, 1)
                        sp.wait_ge(c_lo_w2, e + 1)
                        sp.wait_ge(c_lo_xs, e + 1)
                        sp.sem_inc(waited, 1)
                        load_slots(e + 2, q)
                        sp.wait_ge(c_eo, e + 1)
                        sp.sem_inc(waited, 1)
                        load_weights(e + 2, q)
                    if j == 0:
                        if not (isinstance(gr, int) and gr == 0):
                            sp.wait_ge(c_comb_ps, gr * (B // 2))
                        sp.sem_inc(waited, 1)
                        sp.dma_start(cwg[:, :, :], comb_dram[bass.ds(gr, 1), :, :, :].rearrange("o p b l -> p (o b) l")).then_inc(comb_in, 16)
                    sp.wait_ge(c_eo, e + 1)
                    for k in range(4):
                        sp.dma_start(eog[SL * j:SL * j + SL, :, :].rearrange("p (t k) d -> p t k d", k=4)[:, :, k, :],
                                     eo[q][SL * k:SL * k + SL, :, :]).then_inc(eog_in[q], 16)

            group(0, False)
            with sp.Fori(1, NG - 1) as gr:
                group(gr, False)
            group(NG - 1, True)
            sp.wait_ge(c_comb, (NG) * (B // 2))
            sp.dma_start(out.rearrange("b s c -> s b c"), h[:, :, :]).then_inc(y_out, 16)
            sp.wait_ge(y_out, 16)

        @block.gpsimd
        def _(pool):
            pool.memset(ident[:, :], 0.0).then_inc(i_zero, 1)
            pool.memset(mask8[:, :, :], 0.5).then_inc(i_zero, 1)
            pool.memset(eye15[:, :, :], 0.0).then_inc(i_zero, 1)
            pool.memset(ones[:, :], 1.0).then_inc(i_pool, 1)
            pool.memset(expo[:, :], -0.5).then_inc(i_pool, 1)
            pool.wait_ge(i_zero, 3)
            pool.affine_select(out=ident[:, :], in_=ident[:, :], compare_op=ALU.not_equal, fill=1.0, base=0,
                               pattern=[[-1, P]], channel_multiplier=1).then_inc(i_ident, 1)
            pool.affine_select(out=mask8[:, :, :], in_=mask8[:, :, :], compare_op=ALU.is_ge, fill=0.0, base=0,
                               pattern=[[-D, GH], [0, M]], channel_multiplier=1).then_inc(i_const, 1)
            pool.wait_ge(i_const, 1)
            pool.affine_select(out=mask8[:, :, :], in_=mask8[:, :, :], compare_op=ALU.is_ge, fill=0.0, base=D - 1,
                               pattern=[[D, GH], [0, M]], channel_multiplier=-1).then_inc(i_const, 1)
            for q in range(2):
                pool.wait_ge(i_const, 2 + q)
                v = eye15[64 * q:64 * q + 64, :, 0:M]
                pool.affine_select(out=v, in_=v, compare_op=ALU.not_equal, fill=15.0, base=0,
                                   pattern=[[0, NP], [-1, M]], channel_multiplier=1).then_inc(i_const, 1)
            pool.wait_ge(i_const, 4)
            for q in range(2):
                pool.memset(half(mask2, q)[:, 1 - q, :], 0.0).then_inc(i_const, 1)
                pool.wait_ge(i_const, 5 + q)
                pool.memset(half(mask2, q)[:, q, :], 1.0).then_inc(i_mask2, 1)
                pool.wait_ge(i_mask2, 1 + q)
            pool.wait_ge(ids_in, 16)
            for b in range(B):
                pool.indirect_dma_start(h[:, b, :], None, tok_w, bass.IndirectOffsetOnAxis(ap=ids[:, b:b + 1], axis=0)).then_inc(tokens_in, 16)
            for l in range(2):
                for t in (k2[l], ybd[l]):
                    pool.memset(t[:, :, :], 0.0).then_inc(i_pool, 1)
                pool.memset(wbd[l][:, :, :], 0.0).then_inc(i_pool, 1)
                pool.memset(v33[l][:, :, 2 * D:2 * D + 1], 1.0).then_inc(i_pool, 1)
            for l in range(2):
                for q in range(2):
                    pool.wait_ge(i_pool, 10 + 2 * l + q)
                    pool.memset(half(wbd[l], q)[:, :, 2 * D + q:2 * D + q + 1], 1.0).then_inc(i_pool, 1)

            pool.wait_ge(i_pool, 14)
            with pool.Fori(0, B // 2) as i:
                now = lambda l: 2 * i + (l + 1)
                first = lambda l: 4 * i + (l + 1)
                second = lambda l: 4 * i + (l + 3)
                for l in range(2):
                    pool.wait_ge(a_ve, first(l))
                    pool.tensor_tensor(rs[l][:, :], ve[l][:, :], expo[:, :], ALU.pow).then_inc(a_rs, 1)
                for l in range(2):
                    pool.wait_ge(a_ve, second(l))
                    pool.tensor_tensor(rs[l][:, :], ve[l][:, :], expo[:, :], ALU.pow).then_inc(a_rs, 1)
                for l in range(2):
                    pool.wait_ge(a_k, now(l))
                    pool.tensor_tensor(kl[l][:, :, :], kk[l][:, :, 0:P:2], kk[l][:, :, 1:P:2], ALU.add).then_inc(a_kl, 1)
                for l in range(2):
                    pool.wait_ge(a_kl, now(l))
                    pool.sem_inc(waited, 1)
                    pool.tensor_scalar(kk[l][:, :, P:P + M], kl[l][:, :, :], 0.5, 0.0, ALU.mult, ALU.add).then_inc(a_kk, 1)
                for l in range(2):
                    pool.tensor_tensor(kbd[l][:, 0:GH, :], bc(kl[l][:, 0:1, :], [P, GH, M]), mask8[:, :, :], ALU.mult)
                    pool.tensor_tensor(kbd[l][:, GH:H, :], bc(kl[l][:, 1:2, :], [P, H - GH, M]), mask8[:, 0:H - GH, :], ALU.mult).then_inc(a_kbd, 1)
                for k in range(ITERS):
                    for l in range(2):
                        if k == 0:
                            pool.wait_ge(a_g0, 4 * i + 2 * l + 2)
                            pool.wait_ge(a_gw, 4 * i + 2 * l + 2)
                        else:
                            pool.wait_ge(a_fix, i * (2 * ITERS) + 2 * (k - 1) + l + 1)
                        pool.tensor_tensor(gbd[l][:, :, :].rearrange("p a (q n) -> p a q n", q=2),
                                           bc(g[l][:, :, 0:M].rearrange("p a (o n) -> p a o n", o=1), [P, NP, 2, M]),
                                           bc(mask2[:, :, :].rearrange("p (o q) n -> p o q n", o=1), [P, NP, 2, M]), ALU.mult).then_inc(a_gbd, 1)
                        pool.tensor_scalar(wf[l][:, :, :], g[l][:, :, :], 1.75, 0.0, ALU.mult, ALU.add).then_inc(a_wf, 1)
                        pool.wait_ge(a_wf, i * (4 * ITERS) + 4 * k + 2 * l + 1)
                        pool.tensor_tensor(wf[l][:, :, :], wf[l][:, :, :], eye15[:, :, :], ALU.subtract).then_inc(a_wf, 1)

            with pool.Fori(0, B // 4) as i:
                for hf in range(2):
                    now = lambda l: 4 * i + (2 * hf + l + 1)
                    for l in range(2):
                        pool.wait_ge(r_ve, now(l))
                        pool.tensor_tensor(rrs[l][:, :], rve[l][:, :], expo[:, :], ALU.pow).then_inc(r_rs, 1)
                    for l in range(2):
                        pool.wait_ge(r_ss, now(l))
                        pool.sem_inc(waited, 1)
                        pool.tensor_scalar(rsm[l][:, :], rss[l][:, :], NORM_EPS2, 0.0, ALU.max, ALU.add).then_inc(r_sm, 1)
                    for l in range(2):
                        pool.wait_ge(r_sm, now(l))
                        pool.tensor_tensor(rrn[l][:, :], rsm[l][:, :], expo[:, :], ALU.pow).then_inc(r_rn, 1)
                    for l in range(2):
                        pool.wait_ge(r_xeh, now(l))
                        pool.tensor_tensor(xe_lo[l][:, :], xe[l][:, :], xe_hi[l][:, :].bitcast(F32), ALU.subtract).then_inc(r_xel, 1)
                    for l in range(2):
                        pool.wait_ge(r_fz, now(l))
                        pool.tensor_tensor(cw[l][:, :, :], lg[l][:, :, :], bc(fz[l][:, :].rearrange("p (e o) -> p e o", o=1), [P, E, SL]), ALU.mult).then_inc(r_cw, 1)

            def hi(e, m, q):
                if not (isinstance(e, int) and e < 2):
                    pool.wait_ge(c_hidden, HC * (e - 1))
                pool.wait_ge(w1_in[q], 48 * (m + 1))
                pool.sem_inc(waited, 1)
                pool.tensor_copy(w1_hi[q][:, :], w1raw[q][:, 0, :]).then_inc(c_hi, 1)
                pool.tensor_copy(w1_st[q][:, :], w1raw[q][:, 1, :]).then_inc(c_hi, 1)
                pool.wait_ge(slots_in[q], 48 * (m + 1))
                pool.sem_inc(waited, 1)
                pool.tensor_copy(xs_hi[q][:, 0, :], xsm[q][:, 0, :]).then_inc(c_hi, 1)
                pool.tensor_copy(xs_hi[q][:, 1, :], xsm[q][:, 1, :]).then_inc(c_hi, 1)
                if not (isinstance(e, int) and e < 2):
                    pool.wait_ge(c_output, HC * (e - 1))
                pool.wait_ge(w2_in[q], 32 * (m + 1))
                pool.sem_inc(waited, 1)
                pool.tensor_copy(w2_hi[q][:, :, :], w2raw[q][:, :, :]).then_inc(c_hi, 1)

            pool.wait_ge(slots_out, 32 * (B // 4))
            for l in range(2):
                pool.wait_ge(comb_out[l], 16 * (B // 2))
            hi(0, 0, 0)

            def group(gr, last):
                for j in range(GE):
                    if not (last and j == GE - 1):
                        hi(gr * GE + (j + 1), gr * 2 + (j + 1) // 2, (j + 1) % 2)

            group(0, False)
            with pool.Fori(1, NG - 1) as gr:
                group(gr, False)
            group(NG - 1, True)

        @block.scalar
        def _(act):
            act.wait_ge(phi_in, 48)
            act.activation(phn[:, :], phraw[:, 0, :], ACT.Square).then_inc(i_sq, 1)
            act.activation(pht[0:64, :], phraw[0:64, 1, :], ACT.Square).then_inc(i_sq, 1)
            act.wait_ge(i_n, 1)
            act.activation(pht[:, :], phn[:, :], ACT.Sqrt).then_inc(i_sqrt, 1)

            with act.Fori(0, B // 2) as i:
                now = lambda l: 2 * i + (l + 1)
                first = lambda l: 4 * i + (l + 1)
                second = lambda l: 4 * i + (l + 3)
                for l in range(2):
                    act.wait_ge(a_xTp, now(l))
                    act.activation(xT[l][:, 0, :], bank[l][0][:, 0:P], ACT.Copy)
                    act.activation(xT[l][0:64, 1, :], bank[l][0][0:64, P:2 * P], ACT.Copy).then_inc(a_xT, 1)
                for l in range(2):
                    act.wait_ge(a_qkp, now(l))
                    act.activation(qT[l][:, :, :], bank[l][1][:, 0:2 * P].rearrange("p (a n) -> p a n", a=2), ACT.Copy, scale=D ** -0.5).then_inc(a_q, 1)
                    act.activation(kk[l][:, :, 0:P], bank[l][1][:, 2 * P:4 * P].rearrange("p (a n) -> p a n", a=2), ACT.Copy).then_inc(a_k, 1)
                for l in range(2):
                    act.wait_ge(a_vp, now(l))
                    act.activation(v33[l][:, :, 0:2 * D], bank[l][2][:, 0:C].rearrange("p (a n) -> p a n", a=NP), ACT.Copy).then_inc(a_v, 1)
                for l in range(2):
                    act.wait_ge(a_d2, now(l))
                    act.activation(e2[l][:, :, :], e2[l][:, :, :], ACT.Exp).then_inc(a_e2, 1)
                for l in range(2):
                    act.wait_ge(a_d3, now(l))
                    act.activation(e3[l][:, :, :], e3[l][:, :, :], ACT.Exp).then_inc(a_e3, 1)
                for l in range(2):
                    act.wait_ge(a_k2p, now(l))
                    act.activation(k2T[l][:, 0:4, :], bank[l][1].rearrange("p (a n) -> p a n", a=4), ACT.Copy)
                    act.activation(k2T[l][:, 4:6, :], bank[l][0][:, 0:2 * P].rearrange("p (a n) -> p a n", a=2), ACT.Copy)
                    act.activation(cs[l][:, :], bank[l][0][:, 2 * P:2 * P + NP], ACT.Copy).then_inc(a_k2T, 1)
                for l in range(2):
                    act.wait_ge(a_k3p, now(l))
                    act.activation(k3T[l][:, 0:4, :], bank[l][2].rearrange("p (a n) -> p a n", a=4), ACT.Copy)
                    act.activation(k3T[l][:, 4:6, :], bank[l][3][:, 0:2 * P].rearrange("p (a n) -> p a n", a=2), ACT.Copy).then_inc(a_k3T, 1)
                for l in range(2):
                    act.wait_ge(a_d1, second(l))
                    act.activation(e1[l][:, :, :], e1[l][:, :, :], ACT.Exp).then_inc(a_e1, 1)
                for k in range(ITERS):
                    for l in range(2):
                        act.wait_ge(a_A, i * (2 * ITERS) + 2 * k + l + 1)
                        for q in range(2):
                            act.activation(half(ybd[l], q)[:, :, M * q:M * q + M],
                                           half(bank[l][0], q)[:, 0:NP * SW].rearrange("p (a n) -> p a n", a=NP)[:, :, 0:M],
                                           ACT.Copy, scale=1.0 / 16).then_inc(a_y, 1)
                    if k == 0:
                        for l in range(2):
                            act.wait_ge(a_k1p, now(l))
                            act.activation(k1T[l][:, 0:4, :], bank[l][2].rearrange("p (a n) -> p a n", a=4), ACT.Copy)
                            act.activation(k1T[l][:, 4:6, :], bank[l][3][:, 0:2 * P].rearrange("p (a n) -> p a n", a=2), ACT.Copy).then_inc(a_k1T, 1)
                for l in range(2):
                    act.wait_ge(a_svp, now(l))
                    act.activation(svT[l][:, 0, :], bank[l][1][:, 0:P], ACT.Copy)
                    act.activation(svT[l][0:64, 1, :], bank[l][1][0:64, P:2 * P], ACT.Copy).then_inc(a_svT, 1)

            with act.Fori(0, B // 4) as i:
                for hf in range(2):
                    now = lambda l: 4 * i + (2 * hf + l + 1)
                    for l in range(2):
                        act.wait_ge(r_x, now(l))
                        act.activation(rsq[l][:, :], rx[l][:, :], ACT.Square, accum_out=rss[l][:, :]).then_inc(r_ss, 1)
                    for l in range(2):
                        act.wait_ge(r_xtp, now(l))
                        act.activation(xt_hi[l][:, :, :], bank[l][2][:, 0:2 * P].rearrange("p (a n) -> p a n", a=2), ACT.Copy).then_inc(r_xth, 1)
                    for l in range(2):
                        act.wait_ge(r_xe, 2 * now(l))
                        act.activation(xe_hi[l][:, :], xe[l][:, :], ACT.Copy).then_inc(r_xeh, 1)
                    for l in range(2):
                        act.wait_ge(r_nm, now(l))
                        act.activation(fe[l][:, :], mx[l][:, :], ACT.Exp, bias=nm[l][:, :]).then_inc(r_f, 1)
                        act.wait_ge(r_d, now(l))
                        act.activation(lg[l][:, :, :], lg[l][:, :, :], ACT.Exp).then_inc(r_exp, 1)
                    for l in range(2):
                        act.wait_ge(r_dw, now(l))
                        act.activation(dw_hi[l][:, :], dw[l][:, :, :].rearrange("p e s -> p (e s)"), ACT.Copy).then_inc(r_dh, 1)
                    for l in range(2):
                        act.wait_ge(r_sr_p, now(l))
                        if hf == 0:
                            act.wait_ge(stage_free, i + 1)
                        act.activation(slr[:, :, 2 * hf + l, :], ps[0:64, 4 * l:4 * l + 2, :].rearrange("p a (e s) -> p (a e) s", s=SL), ACT.Copy).then_inc(r_slr, 1)
                    for l in range(2):
                        act.wait_ge(r_cwp, now(l))
                        act.activation(cwT[l][:, hf, :, :], ps[:, 4 * l + 2:4 * l + 4, :].rearrange("p a (g n) -> p (a g) n", n=P), ACT.Copy).then_inc(r_cwT, 1)

            def group(gr, last):
                first = isinstance(gr, int) and gr == 0
                for t in range(GE * HC):
                    n = gr * (GE * HC) + t
                    if not (first and t < 2):
                        act.wait_ge(c_hlo, n - 1)
                    act.wait_ge(c_hidden, n + 1)
                    act.activation(hraw[t % 2][:, :], ps[:, t % 2, :], ACT.Gelu, bias=b1T[:, bass.ds(n, 1)]).then_inc(c_gelu, 1)
                    if not (first and t < 3):
                        act.wait_ge(c_output, n - 2)
                    act.wait_ge(c_gelu, n + 1)
                    act.activation(h_hi[t % 3][:, :], hraw[t % 2][:, :], ACT.Copy).then_inc(c_hhi, 1)

            act.wait_ge(slots_out, 32 * (B // 4))
            for l in range(2):
                act.wait_ge(comb_out[l], 16 * (B // 2))
            group(0, False)
            with act.Fori(1, NG - 1) as gr:
                group(gr, False)
            group(NG - 1, True)

        @block.vector
        def _(dve):
            dve.wait_ge(consts_in, 16 * 7)
            dve.tensor_copy(tidf[:, :], tids[:, :]).then_inc(i_ty, 1)
            dve.tensor_tensor(pos[:, :], pos[:, :], ty[:, 0, :], ALU.add).then_inc(i_ty, 1)
            dve.tensor_tensor(ty[:, 1, :], ty[:, 1, :], ty[:, 0, :], ALU.subtract).then_inc(i_ty, 1)
            dve.memset(wT[:, :, C:256], 0.0)
            dve.memset(wT[:, :, 256 + C:512], 0.0)
            dve.wait_ge(i_wnT, 1)
            for k in range(2):
                rows = P if k == 0 else 64
                dve.tensor_copy(wT[0:rows, k, 0:512].rearrange("p (a n) -> p a n", a=2)[:, :, 0:C],
                                bank[0][2 * k][0:rows, 0:384].rearrange("p (a n) -> p a n", a=2)).then_inc(i_wT, 1)
                dve.tensor_copy(wT[0:rows, k, 512:704], bank[0][2 * k + 1][0:rows, 0:C]).then_inc(i_wT, 1)
                dve.tensor_copy(pT[0:rows, k, :], bank[0][2 * k + 1][0:rows, C:2 * C]).then_inc(i_wT, 1)
            dve.wait_ge(i_b1n, 1)
            dve.tensor_copy(b1T[:, :], bank[1][0][:, 0:E * HC]).then_inc(i_b1T, 1)
            dve.wait_ge(i_ss, 1)
            dve.tensor_scalar(phn[:, :], ps[:, 5:7, :].rearrange("p a n -> p (a n)"), NORM_EPS2, 0.0, ALU.max, ALU.add).then_inc(i_n, 1)
            dve.wait_ge(i_sqrt, 1)
            steps = [0]

            def link(ins):
                steps[0] += 1
                ins.then_inc(i_phi, 1)
                dve.wait_ge(i_phi, steps[0])

            link(dve.reciprocal(pht[:, :], pht[:, :]))
            link(dve.tensor_tensor(phn[:, :], phn[:, :], pht[:, :], ALU.mult))
            link(dve.tensor_tensor(phn[:, :], phn[:, :], pht[:, :], ALU.mult))
            link(dve.tensor_scalar(phn[:, :], phn[:, :], -0.5, 1.5, ALU.mult, ALU.add))
            link(dve.tensor_tensor(phn[:, :], phn[:, :], pht[:, :], ALU.mult))
            link(dve.tensor_scalar(phn[:, :], phn[:, :], scl[:, :], None, ALU.mult))
            for k in range(2):
                link(dve.tensor_tensor(phraw[:, k, :], phraw[:, k, :], phn[:, :], ALU.mult))
            link(dve.tensor_copy(ph_hi[:, :], phraw[:, 0, :]))
            link(dve.tensor_copy(ph_st[:, :], phraw[:, 1, :]))
            link(dve.tensor_tensor(ph_lo[:, :], phraw[:, 0, :], ph_hi[:, :].bitcast(F32), ALU.subtract))
            link(dve.tensor_tensor(ph_st[64:128, :], phraw[64:128, 1, :], ph_st[64:128, :].bitcast(F32), ALU.subtract))
            dve.wait_ge(tokens_in, 16 * B)
            dve.wait_ge(i_ty, 3)
            dve.wait_ge(i_const, 6)
            dve.wait_ge(i_pool, 14)

            def col(ap):
                return ap.rearrange("p (a o) -> p a o", o=1)

            with dve.Fori(0, B // 2) as i:
                now = lambda l: 2 * i + (l + 1)
                first = lambda l: 4 * i + (l + 1)
                second = lambda l: 4 * i + (l + 3)
                hrow = lambda l: h[:, bass.ds(2 * i + l, 1), :].rearrange("p o c -> p (o c)")
                for l in range(2):
                    dve.tensor_tensor(xn[l][:, :], hrow(l), pos[:, :], ALU.add).then_inc(a_emb, 1)
                for l in range(2):
                    dve.wait_ge(a_emb, now(l))
                    dve.scalar_tensor_tensor(hb[l][:, :], ty[:, 1, :], tidf[:, bass.ds(2 * i + l, 1)], xn[l][:, :], ALU.mult, ALU.add).then_inc(a_cen, 1)
                for l in range(2):
                    dve.wait_ge(a_cen, now(l))
                    dve.sem_inc(waited, 1)
                    dve.bn_stats(st6[l][:, :], hb[l][:, :]).then_inc(a_stat, 1)
                for l in range(2):
                    dve.wait_ge(a_stat, first(l))
                    dve.sem_inc(waited, 1)
                    dve.bn_aggr(mv[l][:, :], st6[l][:, :]).then_inc(a_mv, 1)
                for l in range(2):
                    dve.wait_ge(a_mv, first(l))
                    dve.tensor_scalar(ve[l][:, :], mv[l][:, 1:2], LN_EPS, 0.0, ALU.add, ALU.add).then_inc(a_ve, 1)
                for l in range(2):
                    dve.scalar_tensor_tensor(xn[l][:, :], hb[l][:, :], mv[l][:, 0:1], gam[:, :], ALU.subtract, ALU.mult).then_inc(a_hb, 1)
                for l in range(2):
                    dve.wait_ge(a_rs, first(l))
                    dve.wait_ge(a_hb, now(l))
                    dve.scalar_tensor_tensor(hrow(l), xn[l][:, :], rs[l][:, :], bet[:, :], ALU.mult, ALU.add).then_inc(a_h0, 1)
                for l in range(2):
                    dve.wait_ge(a_h0, now(l))
                    dve.sem_inc(waited, 1)
                    dve.bn_stats(st6[l][:, :], hrow(l)).then_inc(a_stat, 1)
                for l in range(2):
                    dve.wait_ge(a_stat, second(l))
                    dve.sem_inc(waited, 1)
                    dve.bn_aggr(mv[l][:, :], st6[l][:, :]).then_inc(a_mv, 1)
                for l in range(2):
                    dve.wait_ge(a_mv, second(l))
                    dve.tensor_scalar(ve[l][:, :], mv[l][:, 1:2], LN_EPS, 0.0, ALU.add, ALU.add).then_inc(a_ve, 1)
                for l in range(2):
                    dve.wait_ge(a_rs, second(l))
                    dve.tensor_scalar(xn[l][:, :], hrow(l), mv[l][:, 0:1], rs[l][:, :], ALU.subtract, ALU.mult).then_inc(a_xn, 1)
                for l in range(2):
                    dve.wait_ge(a_q, now(l))
                    dve.tensor_tensor(ql[l][:, :, :], qT[l][:, :, 0:P:2], qT[l][:, :, 1:P:2], ALU.add).then_inc(a_ql, 1)
                for l in range(2):
                    dve.wait_ge(a_ql, now(l))
                    dve.tensor_tensor(qbd[l][:, 0:GH, :], bc(ql[l][:, 0:1, :], [P, GH, M]), mask8[:, :, :], ALU.mult)
                    dve.tensor_tensor(qbd[l][:, GH:H, :], bc(ql[l][:, 1:2, :], [P, H - GH, M]), mask8[:, 0:H - GH, :], ALU.mult).then_inc(a_qbd, 1)
                s32 = lambda l: ps[:, 4 * l + 1:4 * l + 4, 0:2 * (P + M)].rearrange("p a (q c) -> p a q c", q=2)
                for l in range(2):
                    dve.wait_ge(a_s3, now(l))
                    dve.tensor_reduce(m2[l][:, :], s32(l)[:, :, :, P:P + M], AX.X, ALU.max).then_inc(a_m2, 1)
                    dve.tensor_reduce(m3[l][:, :], s32(l)[:, :, :, 0:P], AX.X, ALU.max).then_inc(a_m3, 1)
                for l in range(2):
                    dve.wait_ge(a_m2, now(l))
                    dve.tensor_tensor(e2[l][:, :, :].rearrange("p (a q) c -> p a q c", q=2), s32(l)[:, :, :, P:P + M],
                                      bc(m2[l][:, :].rearrange("p (a q o) -> p a q o", q=2, o=1), [P, 3, 2, M]), ALU.subtract).then_inc(a_d2, 1)
                    dve.wait_ge(a_m3, now(l))
                    dve.tensor_tensor(e3[l][:, :, :].rearrange("p (a q) c -> p a q c", q=2), s32(l)[:, :, :, 0:P],
                                      bc(m3[l][:, :].rearrange("p (a q o) -> p a q o", q=2, o=1), [P, 3, 2, P]), ALU.subtract).then_inc(a_d3, 1)
                for l in range(2):
                    dve.wait_ge(a_e2, now(l))
                    dve.tensor_reduce(s2[l][:, :], e2[l][:, :, :], AX.X, ALU.add).then_inc(a_sum2, 1)
                for l in range(2):
                    dve.wait_ge(a_sum2, now(l))
                    dve.reciprocal(r2[l][:, :], s2[l][:, :]).then_inc(a_r2, 1)
                for l in range(2):
                    dve.wait_ge(a_r2, now(l))
                    for q in range(2):
                        dve.tensor_tensor(half(k2[l], q)[:, :, M * q:M * q + M], half(e2[l], q)[:, :, :],
                                          bc(col(half(r2[l], q)[:, :]), [64, NP, M]), ALU.mult).then_inc(a_k2, 1)
                v1 = lambda l, k, n: bank[l][k][:, 0:n * M].rearrange("p (a n) -> p a n", a=n)
                for l in range(2):
                    dve.wait_ge(a_s1, first(l))
                    dve.tensor_reduce(m1[l][:, 0:GH], v1(l, 0, GH), AX.X, ALU.max).then_inc(a_m1, 1)
                for l in range(2):
                    dve.wait_ge(a_m1, first(l))
                    dve.tensor_tensor(e1[l][:, 0:GH, :], v1(l, 0, GH), bc(col(m1[l][:, 0:GH]), [P, GH, M]), ALU.subtract).then_inc(a_d1, 1)
                for l in range(2):
                    dve.wait_ge(a_s1, second(l))
                    dve.tensor_reduce(m1[l][:, GH:H], v1(l, 1, H - GH), AX.X, ALU.max).then_inc(a_m1, 1)
                for l in range(2):
                    dve.wait_ge(a_m1, second(l))
                    dve.tensor_tensor(e1[l][:, GH:H, :], v1(l, 1, H - GH), bc(col(m1[l][:, GH:H]), [P, H - GH, M]), ALU.subtract).then_inc(a_d1, 1)
                for l in range(2):
                    dve.wait_ge(a_csT, now(l))
                    dve.tensor_reduce(csm[l][:, :], bank[l][0][0:NP, 0:P].rearrange("p (a n) -> p a n", a=2), AX.X, ALU.max).then_inc(a_csm, 1)
                for l in range(2):
                    dve.wait_ge(a_csm, now(l))
                    dve.reciprocal(csr[l][:, :], csm[l][:, :]).then_inc(a_csr, 1)
                for l in range(2):
                    dve.wait_ge(a_csr, now(l))
                    dve.tensor_copy(csb[l][:, :, :], bc(col(csr[l][:, :]), [NP, 2, M])).then_inc(a_csb, 1)
                for l in range(2):
                    dve.wait_ge(a_sb, now(l))
                    dve.tensor_scalar(r4[l][:, :], bank[l][0][:, 0:NP], 4.0, None, ALU.mult)
                    dve.tensor_scalar(r25[l][:, :], bank[l][0][:, 0:NP], 0.25, None, ALU.mult).then_inc(a_r4, 1)
                for l in range(2):
                    dve.wait_ge(a_up, now(l))
                    dve.reciprocal(u4[l][:, :], bank[l][3][:, 0:NP * 33].rearrange("p (a n) -> p a n", a=NP)[:, :, 32]).then_inc(a_u4, 1)
                for l in range(2):
                    dve.wait_ge(a_u4, now(l))
                    for q in range(2):
                        dve.scalar_tensor_tensor(half(g[l], q)[:, :, M:SW],
                                                 half(bank[l][3], q)[:, 0:NP * 33].rearrange("p (a n) -> p a n", a=NP)[:, :, D * q:D * q + D],
                                                 4.0, bc(col(half(u4[l], q)[:, :]), [64, NP, D]), ALU.mult, ALU.mult).then_inc(a_gw, 1)
                for l in range(2):
                    dve.wait_ge(a_x0, now(l))
                    dve.wait_ge(a_r4, now(l))
                    for q in range(2):
                        dve.tensor_tensor(half(g[l], q)[:, 0:4, 0:M], half(bank[l][1], q).rearrange("p (a n) -> p a n", a=4)[:, :, M * q:M * q + M],
                                          bc(col(half(r4[l], q)[:, 0:4]), [64, 4, M]), ALU.mult)
                        dve.tensor_tensor(half(g[l], q)[:, 4:6, 0:M], half(bank[l][2], q)[:, 0:2 * P].rearrange("p (a n) -> p a n", a=2)[:, :, M * q:M * q + M],
                                          bc(col(half(r4[l], q)[:, 4:6]), [64, 2, M]), ALU.mult).then_inc(a_g0, 1)
                pA = lambda l: bank[l][0][:, 0:NP * SW].rearrange("p (a n) -> p a n", a=NP)
                pZ = lambda l: bank[l][1][:, 0:NP * SW].rearrange("p (a n) -> p a n", a=NP)
                for k in range(ITERS):
                    at = lambda l: i * (2 * ITERS) + 2 * k + l + 1
                    for l in range(2):
                        dve.wait_ge(a_y, 2 * at(l))
                        dve.wait_ge(a_wf, 2 * at(l))
                        dve.scalar_tensor_tensor(tt[l][:, :, :], pA(l), -1.0 / 16, wf[l][:, :, :], ALU.mult, ALU.add).then_inc(a_T, 1)
                        dve.tensor_scalar(aw[l][:, :, :], pA(l)[:, :, M:SW], 15.0 / 16, None, ALU.mult).then_inc(a_T, 1)
                    for l in range(2):
                        dve.wait_ge(a_Z, at(l))
                        dve.wait_ge(a_gbd, at(l))
                        dve.scalar_tensor_tensor(g[l][:, :, :], g[l][:, :, :], 3.25, pZ(l), ALU.mult, ALU.add).then_inc(a_G, 1)
                    for l in range(2):
                        dve.wait_ge(a_G, at(l))
                        dve.wait_ge(a_T, 2 * at(l))
                        dve.tensor_tensor(g[l][:, :, M:SW], g[l][:, :, M:SW], aw[l][:, :, :], ALU.subtract).then_inc(a_fix, 1)
                for l in range(2):
                    dve.wait_ge(a_v0, now(l))
                    for q in range(2):
                        dve.tensor_tensor(half(wbd[l], q)[:, :, D * q:D * q + D], half(bank[l][0], q)[:, 0:NP * D].rearrange("p (a n) -> p a n", a=NP),
                                          bc(col(half(r25[l], q)[:, :]), [64, NP, D]), ALU.mult).then_inc(a_wbd, 1)
                po = lambda l: bank[l][2][:, 0:NP * 34].rearrange("p (a n) -> p a n", a=NP)
                for l in range(2):
                    dve.wait_ge(a_o, now(l))
                    dve.reciprocal(ro[l][:, :, :], po(l)[:, :, 32:34]).then_inc(a_ro, 1)
                for l in range(2):
                    dve.wait_ge(a_ro, now(l))
                    dve.tensor_tensor(sv[l][:, :].rearrange("p (a q d) -> p a q d", q=2, d=D),
                                      po(l)[:, :, 0:32].rearrange("p a (q d) -> p a q d", q=2),
                                      bc(ro[l][:, :, :].rearrange("p a (q o) -> p a q o", o=1), [P, NP, 2, D]), ALU.mult).then_inc(a_sv, 1)
                for l in range(2):
                    dve.tensor_tensor(xn[l][:, :], hrow(l), bpr[:, :], ALU.add).then_inc(a_res, 1)
                for l in range(2):
                    dve.wait_ge(a_res, now(l))
                    dve.tensor_tensor(hb[l][:, :].rearrange("p (a n) -> p a n", a=NP), xn[l][:, :].rearrange("p (a n) -> p a n", a=NP),
                                      v33[l][:, :, 0:2 * D], ALU.add).then_inc(a_hv, 1)
                for l in range(2):
                    dve.wait_ge(a_pr, now(l))
                    dve.wait_ge(a_hv, now(l))
                    dve.tensor_tensor(hrow(l), hb[l][:, :], bank[l][3][:, 0:C], ALU.add).then_inc(a_h1, 1)

            dve.wait_ge(a_h1, B)
            with dve.Fori(0, B // 4) as i:
                for hf in range(2):
                    now = lambda l: 4 * i + (2 * hf + l + 1)
                    hrow = lambda l: h[:, bass.ds(4 * i + (2 * hf + l), 1), :].rearrange("p o c -> p (o c)")
                    lgp = lambda l: ps[:, 4 * l:4 * l + 2, :].rearrange("p a (e s) -> p (a e) s", s=SL)
                    for l in range(2):
                        dve.bn_stats(rst6[l][:, :], hrow(l)).then_inc(r_stat, 1)
                    for l in range(2):
                        dve.wait_ge(r_stat, now(l))
                        dve.sem_inc(waited, 1)
                        dve.bn_aggr(rmv[l][:, :], rst6[l][:, :]).then_inc(r_mv, 1)
                    for l in range(2):
                        dve.wait_ge(r_mv, now(l))
                        dve.tensor_scalar(rve[l][:, :], rmv[l][:, 1:2], LN_EPS, 0.0, ALU.add, ALU.add).then_inc(r_ve, 1)
                    for l in range(2):
                        dve.wait_ge(r_rs, now(l))
                        dve.tensor_scalar(rx[l][:, :], hrow(l), rmv[l][:, 0:1], rrs[l][:, :], ALU.subtract, ALU.mult).then_inc(r_x, 1)
                    for l in range(2):
                        dve.wait_ge(r_rn, now(l))
                        dve.tensor_scalar(xe[l][:, 0:C], rx[l][:, :], rrn[l][:, :], None, ALU.mult).then_inc(r_xe, 1)
                        dve.tensor_scalar(xe[l][:, C:2 * P], rx[l][:, C0:C], rrn[l][:, :], None, ALU.mult).then_inc(r_xe, 1)
                    for l in range(2):
                        dve.wait_ge(r_xth, now(l))
                        dve.tensor_tensor(xt_lo[l][:, :, :], bank[l][2][:, 0:2 * P].rearrange("p (a n) -> p a n", a=2), xt_hi[l][:, :, :].bitcast(F32), ALU.subtract).then_inc(r_xtl, 1)
                    for l in range(2):
                        dve.wait_ge(r_lg, now(l))
                        dve.tensor_reduce(mx[l][:, :], lgp(l), AX.X, ALU.max).then_inc(r_mx, 1)
                    for l in range(2):
                        dve.wait_ge(r_mx, now(l))
                        dve.tensor_reduce(nm[l][:, :], mx[l][:, :], AX.X, ALU.max, negate=True).then_inc(r_nm, 1)
                        dve.tensor_tensor(lg[l][:, :, :], lgp(l), bc(col(mx[l][:, :]), [P, E, SL]), ALU.subtract).then_inc(r_d, 1)
                    for l in range(2):
                        dve.wait_ge(r_exp, now(l))
                        dve.tensor_reduce(ze[l][:, :], lg[l][:, :, :], AX.X, ALU.add).then_inc(r_z, 1)
                    for l in range(2):
                        dve.wait_ge(r_z, now(l))
                        dve.reciprocal(rz[l][:, :], ze[l][:, :]).then_inc(r_rz, 1)
                        dve.wait_ge(r_f, now(l))
                        dve.tensor_tensor(zf[l][:, :], ze[l][:, :], fe[l][:, :], ALU.mult).then_inc(r_zf, 1)
                    for l in range(2):
                        dve.wait_ge(r_rz, now(l))
                        dve.tensor_tensor(dw[l][:, :, :], lg[l][:, :, :], bc(col(rz[l][:, :]), [P, E, SL]), ALU.mult).then_inc(r_dw, 1)
                    for l in range(2):
                        dve.wait_ge(r_zf, now(l))
                        dve.tensor_reduce(zt[l][:, :], zf[l][:, :], AX.X, ALU.add).then_inc(r_zt, 1)
                    for l in range(2):
                        dve.wait_ge(r_zt, now(l))
                        dve.reciprocal(rzt[l][:, :], zt[l][:, :]).then_inc(r_rzt, 1)
                    for l in range(2):
                        dve.wait_ge(r_rzt, now(l))
                        dve.tensor_scalar(fz[l][:, :], fe[l][:, :], rzt[l][:, :], None, ALU.mult).then_inc(r_fz, 1)
                    for l in range(2):
                        dve.wait_ge(r_dh, now(l))
                        dve.tensor_tensor(dw_lo[l][:, :], dw[l][:, :, :].rearrange("p e s -> p (e s)"), dw_hi[l][:, :].bitcast(F32), ALU.subtract).then_inc(r_dl, 1)
                    for l in range(2):
                        dve.wait_ge(r_sm_p, now(l))
                        if hf == 0:
                            dve.wait_ge(stage_free, i + 1)
                        dve.tensor_copy(slm[:, :, 2 * hf + l, :], ps[:, 4 * l + 2:4 * l + 4, :].rearrange("p a (e s) -> p (a e) s", s=SL)).then_inc(r_slm, 1)

            def lo(e, m, q, part):
                if part == 0:
                    dve.wait_ge(w1_in[q], 48 * (m + 1))
                    dve.wait_ge(c_hi, 5 * e + 2)
                    dve.tensor_tensor(w1_lo[q][:, :], w1raw[q][:, 0, :], w1_hi[q][:, :].bitcast(F32), ALU.subtract).then_inc(c_lo_w1, 1)
                    dve.tensor_tensor(w1_st[q][64:128, :], w1raw[q][64:128, 1, :], w1_st[q][64:128, :].bitcast(F32), ALU.subtract).then_inc(c_lo_w1, 1)
                elif part == 1:
                    dve.wait_ge(slots_in[q], 48 * (m + 1))
                    dve.wait_ge(c_hi, 5 * e + 4)
                    dve.tensor_tensor(xs_lo[q][:, :, :], xsm[q][:, :, :], xs_hi[q][:, :, :].bitcast(F32), ALU.subtract).then_inc(c_lo_xs, 1)
                else:
                    dve.wait_ge(w2_in[q], 32 * (m + 1))
                    dve.wait_ge(c_hi, 5 * e + 5)
                    dve.tensor_tensor(w2_lo[q][:, :, :], w2raw[q][:, :, :], w2_hi[q][:, :, :].bitcast(F32), ALU.subtract).then_inc(c_lo_w2, 1)

            def combine(gr, k):
                dve.wait_ge(c_comb_ps, gr * (B // 2) + (k + 1))
                dve.tensor_tensor(h[:, 2 * k:2 * k + 2, :], h[:, 2 * k:2 * k + 2, :],
                                  ps[:, 6 + k % 2, 0:2 * C].rearrange("p (b d) -> p b d", b=2), ALU.add).then_inc(c_comb, 1)

            dve.wait_ge(slots_out, 32 * (B // 4))
            for l in range(2):
                dve.wait_ge(comb_out[l], 16 * (B // 2))
            for part in range(3):
                lo(0, 0, 0, part)

            def group(gr, last):
                first = isinstance(gr, int) and gr == 0
                for j in range(GE):
                    e, q = gr * GE + j, j % 2
                    for k in range(HC):
                        t = j * HC + k
                        n = gr * (GE * HC) + t
                        dve.wait_ge(c_hhi, n + 1)
                        dve.tensor_tensor(h_lo[t % 3][:, :], hraw[t % 2][:, :], h_hi[t % 3][:, :].bitcast(F32), ALU.subtract).then_inc(c_hlo, 1)
                        if k < 3 and not (last and j == GE - 1):
                            lo(gr * GE + (j + 1), gr * 2 + (j + 1) // 2, (j + 1) % 2, k)
                        if j == 0 and not first and k == 3:
                            for b in range(B // 2):
                                combine(gr - 1, b)
                    dve.wait_ge(c_output, HC * (e + 1))
                    dve.wait_ge(w2_in[q], 32 * (gr * 2 + j // 2 + 1))
                    if not (first and j < 2):
                        dve.wait_ge(eog_in[q], 64 * (gr * 2 + j // 2))
                    dve.tensor_tensor(eo[q][:, :, :], ps[:, 2:6, 0:C], bc(b2row[q][:, :].rearrange("p (o d) -> p o d", o=1), [P, 4, C]), ALU.add).then_inc(c_eo, 1)

            group(0, False)
            with dve.Fori(1, NG - 1) as gr:
                group(gr, False)
            group(NG - 1, True)
            for b in range(B // 2):
                combine(NG - 1, b)

        @block.tensor
        def _(pe):
            mm = pe.matmul
            pe.wait_ge(i_ident, 1)
            pe.wait_ge(wn_in, 48)
            for k in range(2):
                rows = P if k == 0 else 64
                for t in range(8):
                    last = pe.transpose(bank[0][2 * k + t // 4][0:rows, 96 * (t % 4):96 * (t % 4) + 96], wn[:, t, P * k:P * k + rows], ident[0:96, 0:96])
            last.then_inc(i_wnT, 1)
            for t in range(2):
                last = pe.transpose(bank[1][0][:, 96 * t:96 * t + 96], b1n[:, t, :], ident[0:96, 0:96])
            last.then_inc(i_b1n, 1)
            pe.wait_ge(i_sq, 2)
            pe.wait_ge(i_pool, 1)
            for a in range(2):
                mm(bank[1][1 + a], ones[:, :], phn[:, 512 * a:512 * a + 512], start=True, stop=False)
                last = mm(bank[1][1 + a], ones[0:64, :], pht[0:64, 512 * a:512 * a + 512], start=False, stop=True)
            last.then_inc(i_ss, 1)
            pe.wait_ge(i_wT, 6)
            pe.wait_ge(i_b1T, 1)
            pe.wait_ge(i_n, 1)
            pe.wait_ge(i_pool, 14)

            with pe.Fori(0, B // 2) as i:
                now = lambda l: 2 * i + (l + 1)
                first = lambda l: 4 * i + (l + 1)
                second = lambda l: 4 * i + (l + 3)
                for l in range(2):
                    pe.wait_ge(a_xn, now(l))
                    pe.transpose(bank[l][0][:, 0:P], xn[l][:, 0:P], ident[:, :])
                    pe.transpose(bank[l][0][0:64, P:2 * P], xn[l][:, P:C], ident[:, :]).then_inc(a_xTp, 1)
                for l in range(2):
                    pe.wait_ge(a_xT, now(l))
                    for a in range(4):
                        mm(bank[l][1][:, P * a:P * a + P], wT[:, 0, P * a:P * a + P], xT[l][:, 0, :], start=True, stop=False)
                        last = mm(bank[l][1][:, P * a:P * a + P], wT[0:64, 1, P * a:P * a + P], xT[l][0:64, 1, :], start=False, stop=True)
                    last.then_inc(a_qkp, 1)
                    mm(bank[l][2][:, 0:C], xT[l][:, 0, :], wT[:, 0, 512:704], start=True, stop=False)
                    mm(bank[l][2][:, 0:C], xT[l][0:64, 1, :], wT[0:64, 1, 512:704], start=False, stop=True).then_inc(a_vp, 1)
                for l in range(2):
                    pe.wait_ge(a_qbd, now(l))
                    pe.wait_ge(a_kk, now(l))
                    pe.wait_ge(a_k, now(l))
                    pe.wait_ge(a_v, now(l))
                    for p in range(NP):
                        last = mm(bank[l][1 + p // 2][:, (P + M) * (p % 2):(P + M) * (p % 2 + 1)],
                                  qbd[l][:, 2 * p:2 * p + 2, :].rearrange("p a n -> p (a n)"), kk[l][:, p // 4, :], start=True, stop=True)
                    last.then_inc(a_s3, 1)
                for l in range(2):
                    pe.wait_ge(a_kbd, now(l))
                    mm(bank[l][0], qT[l][:, 0, :], kbd[l][:, 0:GH, :].rearrange("p a n -> p (a n)"), start=True, stop=True).then_inc(a_s1, 1)
                for l in range(2):
                    pe.wait_ge(a_d3, now(l))
                    pe.wait_ge(a_d2, now(l))
                    mm(bank[l][1][:, 0:256], qT[l][:, 1, :], kbd[l][:, GH:H, :].rearrange("p a n -> p (a n)"), start=True, stop=True).then_inc(a_s1, 1)
                for l in range(2):
                    pe.wait_ge(a_e3, now(l))
                    for p in range(NP):
                        last = pe.transpose(bank[l][2 + p // 4][:, P * (p % 4):P * (p % 4) + P], e3[l][:, p, :], ident[:, :])
                    last.then_inc(a_k3p, 1)
                for l in range(2):
                    pe.wait_ge(a_k2, 2 * now(l))
                    pe.wait_ge(a_d1, first(l))
                    pe.wait_ge(a_d1, second(l))
                    for p in range(NP):
                        pe.transpose(bank[l][1 - p // 4][:, P * (p % 4):P * (p % 4) + P], k2[l][:, p, :], ident[:, :])
                    for p in range(NP):
                        last = mm(bank[l][0][:, 2 * P + p:2 * P + p + 1], k2[l][:, p, :], ones[:, 0:1], start=True, stop=True)
                    last.then_inc(a_k2p, 1)
                for l in range(2):
                    pe.wait_ge(a_k2T, now(l))
                    pe.transpose(bank[l][0][0:NP, 0:P], cs[l][:, :], ident[:, :]).then_inc(a_csT, 1)
                for l in range(2):
                    pe.wait_ge(a_k3T, now(l))
                    for p in range(NP):
                        last = mm(bank[l][3][:, 33 * p:33 * p + 33], k3T[l][:, p, :], v33[l][:, p, :], start=True, stop=True)
                    last.then_inc(a_up, 1)
                for l in range(2):
                    for p in range(NP):
                        last = mm(bank[l][1 + p // 4][:, P * (p % 4):P * (p % 4) + P], k2T[l][:, p, :], k2T[l][:, p, :], start=True, stop=True)
                    last.then_inc(a_x0, 1)
                for l in range(2):
                    pe.wait_ge(a_csb, now(l))
                    mm(bank[l][0][:, 0:NP], csb[l][:, :, :].rearrange("p a n -> p (a n)"), ident[0:NP, 0:NP], start=True, stop=True).then_inc(a_sb, 1)
                for k in range(ITERS):
                    at = lambda l: i * (2 * ITERS) + 2 * k + l + 1
                    for l in range(2):
                        pe.wait_ge(a_gbd, at(l))
                        if k == 0:
                            pe.wait_ge(a_gw, 4 * i + 2 * l + 2)
                            pe.wait_ge(a_g0, 4 * i + 2 * l + 2)
                        for p in range(NP):
                            last = mm(bank[l][0][:, SW * p:SW * p + SW], gbd[l][:, p, :], g[l][:, p, :], start=True, stop=True)
                        last.then_inc(a_A, 1)
                    if k == 0:
                        for l in range(2):
                            pe.wait_ge(a_e1, now(l))
                            for p in range(NP):
                                last = pe.transpose(bank[l][2 + p // 4][:, P * (p % 4):P * (p % 4) + P],
                                                    e1[l][:, 2 * p:2 * p + 2, :].rearrange("p a n -> p (a n)"), ident[:, :])
                            last.then_inc(a_k1p, 1)
                    for l in range(2):
                        pe.wait_ge(a_T, 2 * at(l))
                        for p in range(NP):
                            last = mm(bank[l][1][:, SW * p:SW * p + SW], ybd[l][:, p, :], tt[l][:, p, :], start=True, stop=True)
                        last.then_inc(a_Z, 1)
                for l in range(2):
                    pe.wait_ge(a_fix, i * (2 * ITERS) + 2 * (ITERS - 1) + l + 1)
                    for p in range(NP):
                        last = mm(bank[l][0][:, D * p:D * p + D], k2[l][:, p, :], g[l][:, p, M:SW], start=True, stop=True)
                    last.then_inc(a_v0, 1)
                for l in range(2):
                    pe.wait_ge(a_wbd, 2 * now(l))
                    pe.wait_ge(a_k1T, now(l))
                    for p in range(NP):
                        last = mm(bank[l][2][:, 34 * p:34 * p + 34], k1T[l][:, p, :], wbd[l][:, p, :], start=True, stop=True)
                    last.then_inc(a_o, 1)
                for l in range(2):
                    pe.wait_ge(a_sv, now(l))
                    pe.transpose(bank[l][1][:, 0:P], sv[l][:, 0:P], ident[:, :])
                    pe.transpose(bank[l][1][0:64, P:2 * P], sv[l][:, P:C], ident[:, :]).then_inc(a_svp, 1)
                for l in range(2):
                    pe.wait_ge(a_svT, now(l))
                    mm(bank[l][3][:, 0:C], svT[l][:, 0, :], pT[:, 0, :], start=True, stop=False)
                    mm(bank[l][3][:, 0:C], svT[l][0:64, 1, :], pT[0:64, 1, :], start=False, stop=True).then_inc(a_pr, 1)

            pe.wait_ge(a_h1, B)
            pe.wait_ge(i_phi, 12)
            with pe.Fori(0, B // 4) as i:
                for hf in range(2):
                    now = lambda l: 4 * i + (2 * hf + l + 1)
                    for l in range(2):
                        pe.wait_ge(r_xe, 2 * now(l))
                        for a in range(2):
                            last = pe.transpose(bank[l][2][:, P * a:P * a + P], xe[l][:, P * a:P * a + P], ident[:, :])
                        last.then_inc(r_xtp, 1)
                    for l in range(2):
                        pe.wait_ge(r_xth, now(l))
                        pe.wait_ge(r_xtl, now(l))
                        for a in range(2):
                            cols = slice(512 * a, 512 * a + 512)
                            mm(bank[l][a], xt_hi[l][:, 0, :], ph_hi[:, cols], start=True, stop=False)
                            mm(bank[l][a], xt_hi[l][:, 0, :], ph_lo[:, cols], start=False, stop=False)
                            mm(bank[l][a], xt_lo[l][:, 0, :], ph_hi[:, cols], start=False, stop=False)
                            mm(bank[l][a], xt_hi[l][:, 1, :], ph_st[:, cols], start=False, stop=False)
                            last = mm(bank[l][a], xt_lo[l][:, 1, :], ph_st[:, cols], start=False, stop=True)
                        last.then_inc(r_lg, 1)
                    for l in range(2):
                        pe.wait_ge(r_xel, now(l))
                        pe.wait_ge(r_dl, now(l))
                        for part, first_bank in ((0, 2), (1, 0)):
                            for a in range(2):
                                cols = slice(512 * a, 512 * a + 512)
                                chans = slice(P * part, P * part + P)
                                mm(bank[l][first_bank + a], xe_hi[l][:, chans], dw_hi[l][:, cols], start=True, stop=False)
                                mm(bank[l][first_bank + a], xe_hi[l][:, chans], dw_lo[l][:, cols], start=False, stop=False)
                                last = mm(bank[l][first_bank + a], xe_lo[l][:, chans], dw_hi[l][:, cols], start=False, stop=True)
                            last.then_inc(r_sm_p if part == 0 else r_sr_p, 1)
                    for l in range(2):
                        pe.wait_ge(r_cw, now(l))
                        pe.wait_ge(r_slm, now(l))
                        for gq in range(NG):
                            last = pe.transpose(bank[l][2 + gq // 4][:, P * (gq % 4):P * (gq % 4) + P],
                                                cw[l][:, GE * gq:GE * gq + GE, :].rearrange("p e s -> p (e s)"), ident[:, :])
                        last.then_inc(r_cwp, 1)
                    pe.wait_ge(r_slr, now(1))
                    pe.wait_ge(r_cwT, now(1))

            def hidden(gr, t):
                j, k = t // HC, t % HC
                e, q = gr * GE + j, j % 2
                n = gr * (GE * HC) + t
                cols = slice(P * k, P * k + P)
                if k == 0:
                    pe.wait_ge(c_hi, 5 * e + 4)
                    pe.wait_ge(c_lo_w1, 2 * e + 2)
                    pe.wait_ge(c_lo_xs, e + 1)
                if not (isinstance(gr, int) and gr == 0 and t < 2):
                    pe.wait_ge(c_gelu, n - 1)
                dst = ps[:, t % 2, :]
                mm(dst, w1_hi[q][:, cols], xs_hi[q][:, 0, :], start=True, stop=False)
                mm(dst, w1_hi[q][:, cols], xs_lo[q][:, 0, :], start=False, stop=False)
                mm(dst, w1_lo[q][:, cols], xs_hi[q][:, 0, :], start=False, stop=False)
                mm(dst, w1_st[q][:, cols], xs_hi[q][:, 1, :], start=False, stop=False)
                mm(dst, w1_st[q][:, cols], xs_lo[q][:, 1, :], start=False, stop=True).then_inc(c_hidden, 1)

            def output(gr, t):
                j, k = t // HC, t % HC
                e, q = gr * GE + j, j % 2
                n = gr * (GE * HC) + t
                if k == 0:
                    pe.wait_ge(c_hi, 5 * e + 5)
                    pe.wait_ge(c_lo_w2, e + 1)
                    if not (isinstance(e, int) and e == 0):
                        pe.wait_ge(c_eo, e)
                pe.wait_ge(c_hlo, n + 1)
                for a in range(4):
                    rows = slice(P * a, P * a + P)
                    dst = ps[:, 2 + a, 0:C]
                    mm(dst, h_hi[t % 3][:, rows], w2_hi[q][:, k, :], start=(k == 0), stop=False)
                    mm(dst, h_hi[t % 3][:, rows], w2_lo[q][:, k, :], start=False, stop=False)
                    last = mm(dst, h_lo[t % 3][:, rows], w2_hi[q][:, k, :], start=False, stop=(k == HC - 1))
                last.then_inc(c_output, 1)

            def combine(gr):
                pe.wait_ge(comb_in, 16 * (gr + 1))
                for q in range(2):
                    pe.wait_ge(eog_in[q], 128 * (gr + 1))
                for k in range(B // 2):
                    if k >= 2:
                        pe.wait_ge(c_comb, gr * (B // 2) + (k - 1))
                    for b in range(2):
                        last = mm(ps[:, 6 + k % 2, C * b:C * b + C], cwg[:, 2 * k + b, :], eog[:, 2 * k + b, :], start=True, stop=True)
                    last.then_inc(c_comb_ps, 1)

            pe.wait_ge(slots_out, 32 * (B // 4))
            for l in range(2):
                pe.wait_ge(comb_out[l], 16 * (B // 2))
            hidden(0, 0)
            hidden(0, 1)

            def group(gr, last):
                first = isinstance(gr, int) and gr == 0
                nt = GE * HC
                for t in range(nt):
                    if t + 2 < nt:
                        hidden(gr, t + 2)
                    elif not last:
                        hidden(gr + 1, t + 2 - nt)
                    output(gr, t)
                    if t == 3 and not first:
                        combine(gr - 1)

            group(0, False)
            with pe.Fori(1, NG - 1) as gr:
                group(gr, False)
            group(NG - 1, True)
            combine(NG - 1)


_INS = ['x', 'mask_BS_i1_0', 'L0_tok_tok_w', 'L0_tok_pos_w', 'L0_tok_type_w', 'L0_tok_gamma', 'L0_tok_beta',
        'L0_attn_w_qkv', 'L0_attn_w_proj', 'L0_attn_b_proj', 'L0_ffn_phi', 'L0_ffn_scale', 'L0_ffn_w1',
        'L0_ffn_b1', 'L0_ffn_w2', 'L0_ffn_b2']
_OUTS = [((16, 128, 192), 'float32')]


def kernel(**inputs):
    import numpy as _np
    import concourse.bacc as _bacc
    from concourse.bass_utils import run_bass_kernel_spmd as _run

    nc = _bacc.Bacc("TRN2", target_bir_lowering=False, num_devices=1)
    arrays, args = {}, []
    for name in _INS:
        a = _np.ascontiguousarray(inputs[name])
        arrays[f"in_{name}_dram"] = a
        args.append(nc.dram_tensor(f"in_{name}_dram", a.shape, mybir.dt.from_np(a.dtype), kind="ExternalInput").ap())
    for i, (shape, dtype) in enumerate(_OUTS):
        args.append(nc.dram_tensor(f"out_{i}_dram", shape, mybir.dt.from_np(_np.dtype(dtype)), kind="ExternalOutput").ap())
    build(nc, *args)
    r = _run(nc, [arrays], core_ids=[0])
    return r.results[0]["out_0_dram"]
```

```python
from contextlib import ExitStack

import concourse.bass as bass
from concourse import mybir

F32 = mybir.dt.float32
F32R = mybir.dt.float32r
I32 = mybir.dt.int32
ALU = mybir.AluOpType
ACT = mybir.ActivationFunctionType
AX = mybir.AxisListType

P = 128
LN_EPS = 1e-5
NORM_EPS2 = 1e-24


def build(nc, x, type_ids, tok_w, pos_w, type_w, gamma, beta, w_qkv, w_proj, b_proj,
          phi, scale, w1, b1, w2, b2, out):
    B, S = x.shape
    C = tok_w.shape[1]
    C0, C1 = P, C - P
    H, M = 12, 64
    D = C // H
    NP = H // 2
    GH = P // D
    E, SL = phi.shape[1], phi.shape[2]
    ES = E * SL
    HID = w1.shape[2]
    HC = HID // P
    R = B * SL
    GE = P // SL
    NG = E // GE
    ITERS = 6
    COMB_AT = 5
    SW = M + D
    assert S == P and B % 4 == 0 and M == 64 and C1 == 64 and R == 512

    slots_dram = nc.dram_tensor("slots_dram", [E, C, R], F32).ap()
    comb_dram = nc.dram_tensor("comb_dram", [NG, P, B, S], F32).ap()

    with ExitStack() as ctx:
        def sb(name, shape, dt=F32, where=ctx):
            return where.enter_context(nc.sbuf_tensor(name, shape, dt))

        h = sb("h", [P, B, C])
        ident = sb("ident", [P, P + 1])
        b1T = sb("b1T", [P, E * HC])
        w1raw = [sb(f"w1raw{q}", [P, 2, HID]) for q in range(2)]
        w2raw = [sb(f"w2raw{q}", [P, HC, C]) for q in range(2)]
        b2row = [sb(f"b2row{q}", [P, C]) for q in range(2)]

        front = ExitStack()
        fb = lambda name, shape, dt=F32: sb(name, shape, dt, front)
        ids = fb("ids", [P, B], I32)
        tids = fb("tids", [P, B], I32)
        tidf = fb("tidf", [P, B])
        pos = fb("pos", [P, C])
        ty = fb("ty", [P, 2, C])
        gam = fb("gam", [P, C])
        bet = fb("bet", [P, C])
        bpr = fb("bpr", [P, C])
        scl = fb("scl", [P, 1])
        expo = fb("expo", [P, 1])
        ones = fb("ones", [P, P])
        mask8 = fb("mask8", [P, GH, M])
        eye15 = fb("eye15", [P, NP, SW])
        wn = fb("wn", [96, 8, C])
        b1n = fb("b1n", [96, 2, P])
        wT = fb("wT", [P, 2, 256 + 256 + C])
        pT = fb("pT", [P, 2, C])
        phraw = fb("phraw", [P, 2, ES])
        phn = fb("phn", [P, ES])
        pht = fb("pht", [P, ES])
        ph_hi = fb("ph_hi", [P, ES], F32R)
        ph_lo = fb("ph_lo", [P, ES], F32R)
        ph_st = fb("ph_st", [P, ES], F32R)

        att = ExitStack()
        two = lambda name, shape, dt=F32, w=att: [sb(f"{name}{l}", shape, dt, w) for l in range(2)]
        xn = two("xn", [P, C])
        st6 = two("st6", [P, 6])
        mv = two("mv", [P, 2])
        ve = two("ve", [P, 1])
        rs = two("rs", [P, 1])
        xT = two("xT", [P, 2, P])
        qT = two("qT", [P, 2, P])
        kk = two("kk", [P, 2, P + M])
        v33 = two("v33", [P, NP, 2 * D + 1])
        ql = two("ql", [P, 2, M])
        kl = two("kl", [P, 2, M])
        qbd = two("qbd", [P, H, M])
        kbd = two("kbd", [P, H, M])
        m3 = two("m3", [P, NP])
        m2 = two("m2", [P, NP])
        m1 = two("m1", [P, H])
        e3 = two("e3", [P, NP, P])
        e2 = two("e2", [P, NP, M])
        e1 = two("e1", [P, H, M])
        s2 = two("s2", [P, NP])
        r2 = two("r2", [P, NP])
        k2 = two("k2", [P, NP, P])
        k2T = two("k2T", [P, NP, P + 1])
        k3T = two("k3T", [P, NP, P])
        k1T = two("k1T", [P, NP, P])
        csm = two("csm", [NP, 2])
        csr = two("csr", [NP, 2])
        csb = two("csb", [NP, 2, M])
        r4 = two("r4", [P, NP])
        r25 = two("r25", [P, NP])
        u4 = two("u4", [P, NP])
        g = two("g", [P, NP, SW])
        gbd = two("gbd", [P, NP, P])
        ybd = two("ybd", [P, NP, P])
        tt = two("tt", [P, NP, SW])
        wf = two("wf", [P, NP, SW])
        aw = two("aw", [P, NP, D])
        wbd = two("wbd", [P, NP, 2 * D + 2])
        ro = two("ro", [P, NP, 2])
        sv = two("sv", [P, C])
        svT = two("svT", [P, 2, P])
        hb = two("hb", [P, C])
        att.close()

        rt = ExitStack()
        rx = two("rx", [P, C], w=rt)
        rst6 = two("rst6", [P, 6], w=rt)
        rmv = two("rmv", [P, 2], w=rt)
        rve = two("rve", [P, 1], w=rt)
        rrs = two("rrs", [P, 1], w=rt)
        rsq = two("rsq", [P, C], w=rt)
        rss = two("rss", [P, 1], w=rt)
        rsm = two("rsm", [P, 1], w=rt)
        rrn = two("rrn", [P, 1], w=rt)
        xe = two("xe", [P, 2 * P], w=rt)
        xe_hi = two("xe_hi", [P, 2 * P], F32R, rt)
        xe_lo = two("xe_lo", [P, 2 * P], F32R, rt)
        xt_hi = two("xt_hi", [P, 2, P], F32R, rt)
        xt_lo = two("xt_lo", [P, 2, P], F32R, rt)
        mx = two("mx", [P, E], w=rt)
        nm = two("nm", [P, 1], w=rt)
        fe = two("fe", [P, E], w=rt)
        ze = two("ze", [P, E], w=rt)
        rz = two("rz", [P, E], w=rt)
        zf = two("zf", [P, E], w=rt)
        zt = two("zt", [P, 1], w=rt)
        rzt = two("rzt", [P, 1], w=rt)
        fz = two("fz", [P, E], w=rt)
        lg = two("lg", [P, E, SL], w=rt)
        dw = two("dw", [P, E, SL], w=rt)
        dw_hi = two("dw_hi", [P, ES], F32R, rt)
        dw_lo = two("dw_lo", [P, ES], F32R, rt)
        cw = two("cw", [P, E, SL], w=rt)
        cwT = two("cwT", [P, 2, NG, P], w=rt)
        slm = sb("slm", [P, E, 4, SL], F32, rt)
        slr = sb("slr", [C1, E, 4, SL], F32, rt)
        rt.close()
        front.close()

        xsm = two("xsm", [P, 2, R], w=ctx)
        w1_hi = two("w1_hi", [P, HID], F32R, ctx)
        w1_lo = two("w1_lo", [P, HID], F32R, ctx)
        w1_st = two("w1_st", [P, HID], F32R, ctx)
        w2_hl = two("w2_hl", [P, HC, 2 * C], F32R, ctx)
        eos = sb("eos", [P, 4, C])
        xs_hi = two("xs_hi", [P, 2, R], F32R, ctx)
        xs_lo = two("xs_lo", [P, 2, R], F32R, ctx)
        hraw = two("hraw", [P, R], w=ctx)
        h_hi = [sb(f"h_hi{k}", [P, R], F32R) for k in range(3)]
        h_lo = [sb(f"h_lo{k}", [P, R], F32R) for k in range(3)]
        eo = two("eo", [P, 4, C], w=ctx)
        eog = [sb(f"eog{k}", [P, B, C]) for k in range(2)]
        cwg = [sb(f"cwg{k}", [P, B, S]) for k in range(2)]

        ps = ctx.enter_context(nc.psum_tensor("ps", [P, 8, 512], F32))
        bank = [[ps[:, 4 * l + k, :] for k in range(4)] for l in range(2)]

        def sems(text):
            return [ctx.enter_context(nc.semaphore(n)) for n in text.split()]

        (ids_in, consts_in, tokens_in, phi_in, wn_in, comb_out0, comb_out1, slots_out, w1_in0, w1_in1,
         w2_in0, w2_in1, b2_in0, b2_in1, slots_in0, slots_in1, eog_in0, eog_in1, comb_in, y_out) = sems(
            "ids_in consts_in tokens_in phi_in wn_in comb_out0 comb_out1 slots_out w1_in0 w1_in1 w2_in0 "
            "w2_in1 b2_in0 b2_in1 slots_in0 slots_in1 eog_in0 eog_in1 comb_in y_out ")
        (i_zero, i_ident, i_const, i_pool, i_ty, i_wnT, i_wT, i_b1n, i_b1T, i_sq, i_ss, i_n, i_sqrt,
         i_phi) = sems(
            "i_zero i_ident i_const i_pool i_ty i_wnT i_wT i_b1n i_b1T i_sq i_ss i_n i_sqrt "
            "i_phi ")
        (a_emb, a_stat, a_mv, a_ve, a_rs, a_cen, a_h0, a_xn, a_xTp, a_xT, a_qkp, a_vp, a_q, a_k, a_v, a_ql,
         a_kl, a_qbd, a_kbd, a_kk, a_s3, a_s1, a_m3, a_m2, a_d3, a_d2, a_m1, a_d1, a_e3, a_e2, a_e1, a_sum2,
         a_r2, a_k2, a_k3p, a_k3T, a_k2p, a_k2T, a_csT, a_csm, a_csr, a_csb, a_sb, a_r4, a_res, a_hv, a_x0,
         a_up, a_u4, a_gw, a_g0, a_gbd, a_wf, a_A, a_y, a_T, a_Z, a_G, a_fix, a_k1p, a_k1T, a_v0, a_wbd, a_o,
         a_ro, a_sv, a_svp, a_svT, a_pr, a_hb, a_h1) = sems(
            "a_emb a_stat a_mv a_ve a_rs a_cen a_h0 a_xn a_xTp a_xT a_qkp a_vp a_q a_k a_v a_ql a_kl "
            "a_qbd a_kbd a_kk a_s3 a_s1 a_m3 a_m2 a_d3 a_d2 a_m1 a_d1 a_e3 a_e2 a_e1 a_sum2 a_r2 a_k2 "
            "a_k3p a_k3T a_k2p a_k2T a_csT a_csm a_csr a_csb a_sb a_r4 a_res a_hv a_x0 a_up a_u4 a_gw "
            "a_g0 a_gbd a_wf a_A a_y a_T a_Z a_G a_fix a_k1p a_k1T a_v0 a_wbd a_o a_ro a_sv a_svp a_svT "
            "a_pr a_hb a_h1 ")
        (r_stat, r_mv, r_ve, r_rs, r_x, r_ss, r_sm, r_rn, r_xe, r_xtp, r_xth, r_xtl, r_xeh, r_xel, r_lg,
         r_mx, r_nm, r_f, r_d, r_exp, r_z, r_rz, r_zf, r_zt, r_rzt, r_fz, r_dw, r_dh, r_dl, r_sm_p, r_sr_p,
         r_slm, r_slr, r_cw, r_cwp, r_cwT) = sems(
            "r_stat r_mv r_ve r_rs r_x r_ss r_sm r_rn r_xe r_xtp r_xth r_xtl r_xeh r_xel r_lg r_mx r_nm "
            "r_f r_d r_exp r_z r_rz r_zf r_zt r_rzt r_fz r_dw r_dh r_dl r_sm_p r_sr_p r_slm r_slr r_cw "
            "r_cwp r_cwT ")
        (c_hi, c_lo_w1, c_lo_xs, c_lo_w2, c_hidden, c_gelu, c_hhi, c_hlo, c_output, c_eos, c_eo, c_comb_ps, c_comb) = sems(
            "c_hi c_lo_w1 c_lo_xs c_lo_w2 c_hidden c_gelu c_hhi c_hlo c_output c_eos c_eo c_comb_ps c_comb ")
        comb_out = [comb_out0, comb_out1]
        w1_in, w2_in, b2_in = [w1_in0, w1_in1], [w2_in0, w2_in1], [b2_in0, b2_in1]
        slots_in, eog_in = [slots_in0, slots_in1], [eog_in0, eog_in1]

        stage_free = ctx.enter_context(nc.semaphore("stage_free"))
        waited = ctx.enter_context(nc.semaphore("waited"))

        block = ctx.enter_context(nc.Block())

        def half(t, lane_half):
            return t[64 * lane_half:64 * lane_half + 64]

        OC = HC + 3

        def outputs_done(t):
            return OC * (t // HC) + (OC if t % HC == HC - 1 else t % HC + 1)

        def bc(ap, shape):
            return ap.to_broadcast(shape)

        @block.sync
        def _(sp):
            sp.dma_start(ids[:, :], x.rearrange("b s -> s b"), allow_slow_non_contiguous=True).then_inc(ids_in, 16)
            sp.dma_start(tids[:, :], type_ids.rearrange("b s -> s b"), allow_slow_non_contiguous=True).then_inc(consts_in, 16)
            sp.dma_start(pos[:, :], pos_w).then_inc(consts_in, 16)
            sp.dma_start(ty[:, :, :], type_w.rearrange("(o t) c -> o t c", o=1).to_broadcast([P, 2, C])).then_inc(consts_in, 16)
            for t, v in ((gam, gamma), (bet, beta), (bpr, b_proj)):
                sp.dma_start(t[:, :], v.rearrange("(o c) -> o c", o=1).to_broadcast([P, C])).then_inc(consts_in, 16)
            sp.dma_start(scl[:, :], scale.rearrange("(o c) -> o c", o=1).to_broadcast([P, 1])).then_inc(consts_in, 16)
            sp.dma_start(wn[:, 0:6, :], w_qkv.rearrange("(t p) c -> p t c", p=96)).then_inc(wn_in, 16)
            sp.dma_start(wn[:, 6:8, :], w_proj.rearrange("(t p) c -> p t c", p=96)).then_inc(wn_in, 16)
            sp.dma_start(b1n[:, :, :], b1.rearrange("e (c q) -> (e c) q", q=P).rearrange("(t p) q -> p t q", p=96)).then_inc(wn_in, 16)
            phv = phi.rearrange("d e s -> d (e s)")
            sp.dma_start(phraw[:, 0, :], phv[0:C0, :]).then_inc(phi_in, 16)
            for q in range(2):
                sp.dma_start(half(phraw, q)[:, 1, :], phv[C0:C, :]).then_inc(phi_in, 16)

            def load_weights(e, q):
                sp.dma_start(w1raw[q][:, 0, :], w1[bass.ds(e, 1), 0:C0, :].rearrange("o d h -> d (o h)")).then_inc(w1_in[q], 16)
                for k in range(2):
                    sp.dma_start(half(w1raw[q], k)[:, 1, :], w1[bass.ds(e, 1), C0:C, :].rearrange("o d h -> d (o h)")).then_inc(w1_in[q], 16)
                sp.dma_start(w2raw[q][:, :, :], w2[bass.ds(e, 1), :, :].rearrange("o (c p) d -> p (o c) d", p=P)).then_inc(w2_in[q], 16)

            def load_bias(e, q):
                sp.dma_start(b2row[q][:, :], b2[bass.ds(e, 1), :].to_broadcast([P, C])).then_inc(b2_in[q], 16)

            def load_slots(e, q):
                sp.dma_start(xsm[q][:, 0, :], slots_dram[bass.ds(e, 1), 0:C0, :].rearrange("o d h -> d (o h)")).then_inc(slots_in[q], 16)
                for k in range(2):
                    sp.dma_start(half(xsm[q], k)[:, 1, :], slots_dram[bass.ds(e, 1), C0:C, :].rearrange("o d h -> d (o h)")).then_inc(slots_in[q], 16)

            for q in range(2):
                load_weights(q, q)
                load_bias(q, q)

            sp.sem_inc(stage_free, 1)
            with sp.Fori(0, B // 4) as i:
                for hf in range(2):
                    for l in range(2):
                        sp.wait_ge(r_cwT, 4 * i + 2 * hf + l + 1)
                        sp.sem_inc(waited, 1)
                        sp.dma_start(comb_dram[:, :, bass.ds(4 * i + 2 * hf + l, 1), :].rearrange("g p o l -> p g (o l)"),
                                     cwT[l][:, hf, :, :]).then_inc(comb_out[l], 16)
                sp.wait_ge(r_slm, 4 * i + 4)
                sp.wait_ge(r_slr, 4 * i + 4)
                sp.sem_inc(waited, 1)
                sp.dma_start(slots_dram[:, 0:C0, bass.ds(i * (4 * SL), 4 * SL)].rearrange("e d r -> d e r"),
                             slm[:, :, :, :].rearrange("d e b s -> d e (b s)")).then_inc(slots_out, 16)
                sp.dma_start(slots_dram[:, C0:C, bass.ds(i * (4 * SL), 4 * SL)].rearrange("e d r -> d e r"),
                             slr[:, :, :, :].rearrange("d e b s -> d e (b s)")).then_inc(slots_out, 16)
                sp.wait_ge(slots_out, 32 * i + 32)
                for l in range(2):
                    sp.wait_ge(comb_out[l], 32 * i + 32)
                sp.sem_inc(stage_free, 1)
            sp.wait_ge(slots_out, 32 * (B // 4))
            for l in range(2):
                sp.wait_ge(comb_out[l], 16 * (B // 2))
            for q in range(2):
                load_slots(q, q)

            def prefetch(e, q):
                sp.wait_ge(c_hi, 5 * e + 5)
                sp.sem_inc(waited, 1)
                sp.wait_ge(c_lo_w1, 2 * e + 2)
                sp.sem_inc(waited, 1)
                sp.wait_ge(c_lo_xs, e + 1)
                sp.sem_inc(waited, 1)
                load_slots(e + 2, q)
                sp.wait_ge(c_lo_w2, e + 1)
                sp.sem_inc(waited, 1)
                load_weights(e + 2, q)

            prefetch(0, 0)

            def group(gr, last, par):
                for j in range(GE):
                    e, q = gr * GE + j, j % 2
                    if not (last and j >= 1):
                        prefetch(gr * GE + (j + 1), (j + 1) % 2)
                    if j == 0:
                        if not (isinstance(gr, int) and gr == 0):
                            sp.wait_ge(c_comb, (gr - 1) * (B // 2) + 2)
                        sp.sem_inc(waited, 1)
                        sp.dma_start(cwg[par][:, :, :], comb_dram[bass.ds(gr, 1), :, :, :].rearrange("o p b l -> p (o b) l")).then_inc(comb_in, 16)
                    sp.wait_ge(c_eo, 4 * (e + 1))
                    for k in range(4):
                        sp.dma_start(eog[par][SL * j:SL * j + SL, :, :].rearrange("p (t k) d -> p t k d", k=4)[:, :, k, :],
                                     eo[q][SL * k:SL * k + SL, :, :]).then_inc(eog_in[q], 16)
                    if not (last and j >= 2):
                        sp.sem_inc(waited, 1)
                        load_bias(e + 2, q)

            group(0, False, 0)
            with sp.Fori(0, NG // 2 - 1) as i:
                for k in range(2):
                    group(2 * i + (k + 1), False, (k + 1) % 2)
            group(NG - 1, True, (NG - 1) % 2)
            sp.wait_ge(c_comb, NG * (B // 2) + 2)
            sp.dma_start(out.rearrange("b s c -> s b c"), h[:, :, :]).then_inc(y_out, 16)
            sp.wait_ge(y_out, 16)

        @block.gpsimd
        def _(pool):
            pool.memset(ident[:, 0:P], 0.0).then_inc(i_zero, 1)
            pool.memset(mask8[:, :, :], 0.5).then_inc(i_zero, 1)
            pool.memset(eye15[:, :, :], 0.0).then_inc(i_zero, 1)
            pool.memset(ones[:, :], 1.0).then_inc(i_pool, 1)
            pool.memset(ident[:, P:P + 1], 1.0).then_inc(i_pool, 1)
            pool.memset(expo[:, :], -0.5).then_inc(i_pool, 1)
            pool.wait_ge(i_zero, 3)
            pool.affine_select(out=ident[:, 0:P], in_=ident[:, 0:P], compare_op=ALU.not_equal, fill=1.0, base=0,
                               pattern=[[-1, P]], channel_multiplier=1).then_inc(i_ident, 1)
            pool.affine_select(out=mask8[:, :, :], in_=mask8[:, :, :], compare_op=ALU.is_ge, fill=0.0, base=0,
                               pattern=[[-D, GH], [0, M]], channel_multiplier=1).then_inc(i_const, 1)
            pool.wait_ge(i_const, 1)
            pool.affine_select(out=mask8[:, :, :], in_=mask8[:, :, :], compare_op=ALU.is_ge, fill=0.0, base=D - 1,
                               pattern=[[D, GH], [0, M]], channel_multiplier=-1).then_inc(i_const, 1)
            for q in range(2):
                pool.wait_ge(i_const, 2 + q)
                v = eye15[64 * q:64 * q + 64, :, 0:M]
                pool.affine_select(out=v, in_=v, compare_op=ALU.not_equal, fill=15.0, base=0,
                                   pattern=[[0, NP], [-1, M]], channel_multiplier=1).then_inc(i_const, 1)
            pool.wait_ge(i_const, 4)
            pool.wait_ge(ids_in, 16)
            for b in range(B):
                pool.indirect_dma_start(h[:, b, :], None, tok_w, bass.IndirectOffsetOnAxis(ap=ids[:, b:b + 1], axis=0)).then_inc(tokens_in, 16)
            for l in range(2):
                for t in (k2[l], gbd[l], ybd[l]):
                    pool.memset(t[:, :, :], 0.0).then_inc(i_pool, 1)
                pool.memset(wbd[l][:, :, :], 0.0).then_inc(i_pool, 1)
                pool.memset(v33[l][:, :, 2 * D:2 * D + 1], 1.0).then_inc(i_pool, 1)
            for l in range(2):
                for q in range(2):
                    pool.wait_ge(i_pool, 13 + 2 * l + q)
                    pool.memset(half(wbd[l], q)[:, :, 2 * D + q:2 * D + q + 1], 1.0).then_inc(i_pool, 1)

            pool.wait_ge(i_pool, 17)
            with pool.Fori(0, B // 2) as i:
                now = lambda l: 2 * i + (l + 1)
                first = lambda l: 4 * i + (l + 1)
                second = lambda l: 4 * i + (l + 3)
                for l in range(2):
                    pool.wait_ge(a_ve, first(l))
                    pool.tensor_tensor(rs[l][:, :], ve[l][:, :], expo[:, :], ALU.pow).then_inc(a_rs, 1)
                for l in range(2):
                    pool.wait_ge(a_ve, second(l))
                    pool.tensor_tensor(rs[l][:, :], ve[l][:, :], expo[:, :], ALU.pow).then_inc(a_rs, 1)
                for l in range(2):
                    pool.wait_ge(a_k, now(l))
                    pool.tensor_tensor(kl[l][:, :, :], kk[l][:, :, 0:P:2], kk[l][:, :, 1:P:2], ALU.add).then_inc(a_kl, 1)
                for l in range(2):
                    pool.wait_ge(a_kl, now(l))
                    pool.sem_inc(waited, 1)
                    pool.tensor_scalar(kk[l][:, :, P:P + M], kl[l][:, :, :], 0.5, 0.0, ALU.mult, ALU.add).then_inc(a_kk, 1)
                for l in range(2):
                    pool.tensor_tensor(kbd[l][:, 0:GH, :], bc(kl[l][:, 0:1, :], [P, GH, M]), mask8[:, :, :], ALU.mult)
                    pool.tensor_tensor(kbd[l][:, GH:H, :], bc(kl[l][:, 1:2, :], [P, H - GH, M]), mask8[:, 0:H - GH, :], ALU.mult).then_inc(a_kbd, 1)

            with pool.Fori(0, B // 4) as i:
                for hf in range(2):
                    now = lambda l: 4 * i + (2 * hf + l + 1)
                    for l in range(2):
                        pool.wait_ge(r_ve, now(l))
                        pool.tensor_tensor(rrs[l][:, :], rve[l][:, :], expo[:, :], ALU.pow).then_inc(r_rs, 1)
                    for l in range(2):
                        pool.wait_ge(r_ss, now(l))
                        pool.sem_inc(waited, 1)
                        pool.tensor_scalar(rsm[l][:, :], rss[l][:, :], NORM_EPS2, 0.0, ALU.max, ALU.add).then_inc(r_sm, 1)
                    for l in range(2):
                        pool.wait_ge(r_sm, now(l))
                        pool.tensor_tensor(rrn[l][:, :], rsm[l][:, :], expo[:, :], ALU.pow).then_inc(r_rn, 1)
                    for l in range(2):
                        pool.wait_ge(r_xeh, now(l))
                        pool.tensor_tensor(xe_lo[l][:, :], xe[l][:, :], xe_hi[l][:, :].bitcast(F32), ALU.subtract).then_inc(r_xel, 1)
                    for l in range(2):
                        pool.wait_ge(r_fz, now(l))
                        pool.tensor_tensor(cw[l][:, :, :], lg[l][:, :, :], bc(fz[l][:, :].rearrange("p (e o) -> p e o", o=1), [P, E, SL]), ALU.mult).then_inc(r_cw, 1)

            def hi(e, m, q):
                if not (isinstance(e, int) and e < 2):
                    pool.wait_ge(c_hidden, HC * (e - 1))
                pool.wait_ge(w1_in[q], 48 * (m + 1))
                pool.sem_inc(waited, 1)
                pool.tensor_scalar(w1_hi[q][:, :], w1raw[q][:, 0, :], 1.0, 0.0, ALU.mult, ALU.add).then_inc(c_hi, 1)
                pool.tensor_scalar(w1_st[q][:, :], w1raw[q][:, 1, :], 1.0, 0.0, ALU.mult, ALU.add).then_inc(c_hi, 1)
                pool.wait_ge(slots_in[q], 48 * (m + 1))
                pool.sem_inc(waited, 1)
                pool.tensor_scalar(xs_hi[q][:, 0, :], xsm[q][:, 0, :], 1.0, 0.0, ALU.mult, ALU.add).then_inc(c_hi, 1)
                pool.tensor_scalar(xs_hi[q][:, 1, :], xsm[q][:, 1, :], 1.0, 0.0, ALU.mult, ALU.add).then_inc(c_hi, 1)
                if not (isinstance(e, int) and e < 2):
                    pool.wait_ge(c_output, OC * (e - 1))
                pool.wait_ge(w2_in[q], 16 * (m + 1))
                pool.sem_inc(waited, 1)
                pool.tensor_scalar(w2_hl[q][:, :, 0:C], w2raw[q][:, :, :], 1.0, 0.0, ALU.mult, ALU.add).then_inc(c_hi, 1)

            pool.wait_ge(slots_out, 32 * (B // 4))
            for l in range(2):
                pool.wait_ge(comb_out[l], 16 * (B // 2))
            hi(0, 0, 0)

            def group(gr, last, par):
                for j in range(GE):
                    if not (last and j == GE - 1):
                        hi(gr * GE + (j + 1), gr * 2 + (j + 1) // 2, (j + 1) % 2)

            group(0, False, 0)
            with pool.Fori(0, NG // 2 - 1) as i:
                for k in range(2):
                    group(2 * i + (k + 1), False, (k + 1) % 2)
            group(NG - 1, True, (NG - 1) % 2)

        @block.scalar
        def _(act):
            act.wait_ge(phi_in, 48)
            act.activation(phn[:, :], phraw[:, 0, :], ACT.Square).then_inc(i_sq, 1)
            act.activation(pht[0:64, :], phraw[0:64, 1, :], ACT.Square).then_inc(i_sq, 1)
            act.wait_ge(i_n, 1)
            act.activation(pht[:, :], phn[:, :], ACT.Sqrt).then_inc(i_sqrt, 1)

            with act.Fori(0, B // 2) as i:
                now = lambda l: 2 * i + (l + 1)
                first = lambda l: 4 * i + (l + 1)
                second = lambda l: 4 * i + (l + 3)
                for l in range(2):
                    act.wait_ge(a_xTp, now(l))
                    act.activation(xT[l][:, 0, :], bank[l][0][:, 0:P], ACT.Copy)
                    act.activation(xT[l][0:64, 1, :], bank[l][0][0:64, P:2 * P], ACT.Copy).then_inc(a_xT, 1)
                for l in range(2):
                    act.wait_ge(a_qkp, now(l))
                    act.activation(qT[l][:, :, :], bank[l][1][:, 0:2 * P].rearrange("p (a n) -> p a n", a=2), ACT.Copy, scale=D ** -0.5).then_inc(a_q, 1)
                    act.activation(kk[l][:, :, 0:P], bank[l][1][:, 2 * P:4 * P].rearrange("p (a n) -> p a n", a=2), ACT.Copy).then_inc(a_k, 1)
                for l in range(2):
                    act.wait_ge(a_vp, now(l))
                    act.activation(v33[l][:, :, 0:2 * D], bank[l][2][:, 0:C].rearrange("p (a n) -> p a n", a=NP), ACT.Copy).then_inc(a_v, 1)
                for l in range(2):
                    act.wait_ge(a_d2, now(l))
                    act.activation(e2[l][:, :, :], e2[l][:, :, :], ACT.Exp).then_inc(a_e2, 1)
                for l in range(2):
                    act.wait_ge(a_d3, now(l))
                    act.activation(e3[l][:, :, :], e3[l][:, :, :], ACT.Exp).then_inc(a_e3, 1)
                for l in range(2):
                    act.wait_ge(a_k2p, now(l))
                    act.activation(k2T[l][:, :, :].rearrange("p (a q) n -> p a q n", a=2),
                                   ps[:, 4 * l:4 * l + 2, 0:3 * (P + 1)].rearrange("p a (q n) -> p a q n", q=3), ACT.Copy).then_inc(a_k2T, 1)
                for l in range(2):
                    act.wait_ge(a_k3p, now(l))
                    act.activation(k3T[l][:, 0:4, :], bank[l][2].rearrange("p (a n) -> p a n", a=4), ACT.Copy)
                    act.activation(k3T[l][:, 4:6, :], bank[l][3][:, 0:2 * P].rearrange("p (a n) -> p a n", a=2), ACT.Copy).then_inc(a_k3T, 1)
                for l in range(2):
                    act.wait_ge(a_d1, second(l))
                    act.activation(e1[l][:, :, :], e1[l][:, :, :], ACT.Exp).then_inc(a_e1, 1)
                def state_bd(k, l):
                    if k == 0:
                        act.wait_ge(a_g0, 4 * i + 2 * l + 2)
                    else:
                        act.wait_ge(a_G, i * (2 * ITERS) + 2 * (k - 1) + l + 1)
                    for q in range(2):
                        act.activation(half(gbd[l], q)[:, :, M * q:M * q + M], half(g[l], q)[:, :, 0:M], ACT.Copy).then_inc(a_gbd, 1)

                for l in range(2):
                    state_bd(0, l)
                for k in range(ITERS):
                    for l in range(2):
                        act.wait_ge(a_A, i * (2 * ITERS) + 2 * k + l + 1)
                        for q in range(2):
                            act.activation(half(ybd[l], q)[:, :, M * q:M * q + M],
                                           half(bank[l][0], q)[:, 0:NP * SW].rearrange("p (a n) -> p a n", a=NP)[:, :, 0:M],
                                           ACT.Copy, scale=1.0 / 16).then_inc(a_y, 1)
                    if k < ITERS - 1:
                        for l in range(2):
                            state_bd(k + 1, l)
                    if k == 0:
                        for l in range(2):
                            act.wait_ge(a_k1p, now(l))
                            act.activation(k1T[l][:, 0:4, :], bank[l][2].rearrange("p (a n) -> p a n", a=4), ACT.Copy)
                            act.activation(k1T[l][:, 4:6, :], bank[l][3][:, 0:2 * P].rearrange("p (a n) -> p a n", a=2), ACT.Copy).then_inc(a_k1T, 1)
                for l in range(2):
                    act.wait_ge(a_svp, now(l))
                    act.activation(svT[l][:, 0, :], bank[l][1][:, 0:P], ACT.Copy)
                    act.activation(svT[l][0:64, 1, :], bank[l][1][0:64, P:2 * P], ACT.Copy).then_inc(a_svT, 1)

            with act.Fori(0, B // 4) as i:
                for hf in range(2):
                    now = lambda l: 4 * i + (2 * hf + l + 1)
                    for l in range(2):
                        act.wait_ge(r_x, now(l))
                        act.activation(rsq[l][:, :], rx[l][:, :], ACT.Square, accum_out=rss[l][:, :]).then_inc(r_ss, 1)
                    for l in range(2):
                        act.wait_ge(r_xtp, now(l))
                        act.activation(xt_hi[l][:, :, :], bank[l][2][:, 0:2 * P].rearrange("p (a n) -> p a n", a=2), ACT.Copy).then_inc(r_xth, 1)
                    for l in range(2):
                        act.wait_ge(r_xe, 2 * now(l))
                        act.activation(xe_hi[l][:, :], xe[l][:, :], ACT.Copy).then_inc(r_xeh, 1)
                    for l in range(2):
                        act.wait_ge(r_nm, now(l))
                        act.activation(fe[l][:, :], mx[l][:, :], ACT.Exp, bias=nm[l][:, :]).then_inc(r_f, 1)
                        act.wait_ge(r_d, now(l))
                        act.activation(lg[l][:, :, :], lg[l][:, :, :], ACT.Exp).then_inc(r_exp, 1)
                    for l in range(2):
                        act.wait_ge(r_dw, now(l))
                        act.activation(dw_hi[l][:, :], dw[l][:, :, :].rearrange("p e s -> p (e s)"), ACT.Copy).then_inc(r_dh, 1)
                    for l in range(2):
                        act.wait_ge(r_sr_p, now(l))
                        if hf == 0:
                            act.wait_ge(stage_free, i + 1)
                        act.activation(slr[:, :, 2 * hf + l, :], ps[0:64, 4 * l:4 * l + 2, :].rearrange("p a (e s) -> p (a e) s", s=SL), ACT.Copy).then_inc(r_slr, 1)
                    for l in range(2):
                        act.wait_ge(r_cwp, now(l))
                        act.activation(cwT[l][:, hf, :, :], ps[:, 4 * l + 2:4 * l + 4, :].rearrange("p a (g n) -> p (a g) n", n=P), ACT.Copy).then_inc(r_cwT, 1)

            def group(gr, last, par):
                first = isinstance(gr, int) and gr == 0
                for t in range(GE * HC):
                    n = gr * (GE * HC) + t
                    if not (first and t < 2):
                        act.wait_ge(c_hlo, n - 1)
                    act.wait_ge(c_hidden, n + 1)
                    act.activation(hraw[t % 2][:, :], ps[:, t % 2, :], ACT.Gelu, bias=b1T[:, bass.ds(n, 1)]).then_inc(c_gelu, 1)
                    if not (first and t < 3):
                        act.wait_ge(c_output, OC * (gr * GE) + outputs_done(t - 3))
                    act.wait_ge(c_gelu, n + 1)
                    act.activation(h_hi[t % 3][:, :], hraw[t % 2][:, :], ACT.Copy).then_inc(c_hhi, 1)

            act.wait_ge(slots_out, 32 * (B // 4))
            for l in range(2):
                act.wait_ge(comb_out[l], 16 * (B // 2))
            group(0, False, 0)
            with act.Fori(0, NG // 2 - 1) as i:
                for k in range(2):
                    group(2 * i + (k + 1), False, (k + 1) % 2)
            group(NG - 1, True, (NG - 1) % 2)

        @block.vector
        def _(dve):
            dve.wait_ge(consts_in, 16 * 7)
            dve.tensor_copy(tidf[:, :], tids[:, :]).then_inc(i_ty, 1)
            dve.tensor_tensor(pos[:, :], pos[:, :], ty[:, 0, :], ALU.add).then_inc(i_ty, 1)
            dve.tensor_tensor(ty[:, 1, :], ty[:, 1, :], ty[:, 0, :], ALU.subtract).then_inc(i_ty, 1)
            dve.memset(wT[:, :, C:256], 0.0)
            dve.memset(wT[:, :, 256 + C:512], 0.0)
            dve.wait_ge(i_wnT, 1)
            for k in range(2):
                rows = P if k == 0 else 64
                dve.tensor_copy(wT[0:rows, k, 0:512].rearrange("p (a n) -> p a n", a=2)[:, :, 0:C],
                                bank[0][2 * k][0:rows, 0:384].rearrange("p (a n) -> p a n", a=2)).then_inc(i_wT, 1)
                dve.tensor_copy(wT[0:rows, k, 512:704], bank[0][2 * k + 1][0:rows, 0:C]).then_inc(i_wT, 1)
                dve.tensor_copy(pT[0:rows, k, :], bank[0][2 * k + 1][0:rows, C:2 * C]).then_inc(i_wT, 1)
            dve.wait_ge(i_b1n, 1)
            dve.tensor_copy(b1T[:, :], bank[1][0][:, 0:E * HC]).then_inc(i_b1T, 1)
            dve.wait_ge(i_ss, 1)
            dve.tensor_scalar(phn[:, :], ps[:, 5:7, :].rearrange("p a n -> p (a n)"), NORM_EPS2, 0.0, ALU.max, ALU.add).then_inc(i_n, 1)
            dve.wait_ge(i_sqrt, 1)
            steps = [0]

            def link(ins):
                steps[0] += 1
                ins.then_inc(i_phi, 1)
                dve.wait_ge(i_phi, steps[0])

            link(dve.reciprocal(pht[:, :], pht[:, :]))
            link(dve.tensor_tensor(phn[:, :], phn[:, :], pht[:, :], ALU.mult))
            link(dve.tensor_tensor(phn[:, :], phn[:, :], pht[:, :], ALU.mult))
            link(dve.tensor_scalar(phn[:, :], phn[:, :], -0.5, 1.5, ALU.mult, ALU.add))
            link(dve.tensor_tensor(phn[:, :], phn[:, :], pht[:, :], ALU.mult))
            link(dve.tensor_scalar(phn[:, :], phn[:, :], scl[:, :], None, ALU.mult))
            for k in range(2):
                link(dve.tensor_tensor(phraw[:, k, :], phraw[:, k, :], phn[:, :], ALU.mult))
            link(dve.tensor_copy(ph_hi[:, :], phraw[:, 0, :]))
            link(dve.tensor_copy(ph_st[:, :], phraw[:, 1, :]))
            link(dve.tensor_tensor(ph_lo[:, :], phraw[:, 0, :], ph_hi[:, :].bitcast(F32), ALU.subtract))
            link(dve.tensor_tensor(ph_st[64:128, :], phraw[64:128, 1, :], ph_st[64:128, :].bitcast(F32), ALU.subtract))
            dve.wait_ge(tokens_in, 16 * B)
            dve.wait_ge(i_ty, 3)
            dve.wait_ge(i_const, 4)
            dve.wait_ge(i_pool, 17)

            def col(ap):
                return ap.rearrange("p (a o) -> p a o", o=1)

            with dve.Fori(0, B // 2) as i:
                now = lambda l: 2 * i + (l + 1)
                first = lambda l: 4 * i + (l + 1)
                second = lambda l: 4 * i + (l + 3)
                hrow = lambda l: h[:, bass.ds(2 * i + l, 1), :].rearrange("p o c -> p (o c)")
                for l in range(2):
                    dve.tensor_tensor(xn[l][:, :], hrow(l), pos[:, :], ALU.add).then_inc(a_emb, 1)
                for l in range(2):
                    dve.wait_ge(a_emb, now(l))
                    dve.scalar_tensor_tensor(hb[l][:, :], ty[:, 1, :], tidf[:, bass.ds(2 * i + l, 1)], xn[l][:, :], ALU.mult, ALU.add).then_inc(a_cen, 1)
                for l in range(2):
                    dve.wait_ge(a_cen, now(l))
                    dve.sem_inc(waited, 1)
                    dve.bn_stats(st6[l][:, :], hb[l][:, :]).then_inc(a_stat, 1)
                for l in range(2):
                    dve.wait_ge(a_stat, first(l))
                    dve.sem_inc(waited, 1)
                    dve.bn_aggr(mv[l][:, :], st6[l][:, :]).then_inc(a_mv, 1)
                for l in range(2):
                    dve.wait_ge(a_mv, first(l))
                    dve.tensor_scalar(ve[l][:, :], mv[l][:, 1:2], LN_EPS, 0.0, ALU.add, ALU.add).then_inc(a_ve, 1)
                for l in range(2):
                    dve.scalar_tensor_tensor(xn[l][:, :], hb[l][:, :], mv[l][:, 0:1], gam[:, :], ALU.subtract, ALU.mult).then_inc(a_hb, 1)
                for l in range(2):
                    dve.wait_ge(a_rs, first(l))
                    dve.wait_ge(a_hb, now(l))
                    dve.scalar_tensor_tensor(hrow(l), xn[l][:, :], rs[l][:, :], bet[:, :], ALU.mult, ALU.add).then_inc(a_h0, 1)
                for l in range(2):
                    dve.wait_ge(a_h0, now(l))
                    dve.sem_inc(waited, 1)
                    dve.bn_stats(st6[l][:, :], hrow(l)).then_inc(a_stat, 1)
                for l in range(2):
                    dve.wait_ge(a_stat, second(l))
                    dve.sem_inc(waited, 1)
                    dve.bn_aggr(mv[l][:, :], st6[l][:, :]).then_inc(a_mv, 1)
                for l in range(2):
                    dve.wait_ge(a_mv, second(l))
                    dve.tensor_scalar(ve[l][:, :], mv[l][:, 1:2], LN_EPS, 0.0, ALU.add, ALU.add).then_inc(a_ve, 1)
                for l in range(2):
                    dve.wait_ge(a_rs, second(l))
                    dve.tensor_scalar(xn[l][:, :], hrow(l), mv[l][:, 0:1], rs[l][:, :], ALU.subtract, ALU.mult).then_inc(a_xn, 1)
                for l in range(2):
                    dve.wait_ge(a_q, now(l))
                    dve.tensor_tensor(ql[l][:, :, :], qT[l][:, :, 0:P:2], qT[l][:, :, 1:P:2], ALU.add).then_inc(a_ql, 1)
                for l in range(2):
                    dve.wait_ge(a_ql, now(l))
                    dve.tensor_tensor(qbd[l][:, 0:GH, :], bc(ql[l][:, 0:1, :], [P, GH, M]), mask8[:, :, :], ALU.mult)
                    dve.tensor_tensor(qbd[l][:, GH:H, :], bc(ql[l][:, 1:2, :], [P, H - GH, M]), mask8[:, 0:H - GH, :], ALU.mult).then_inc(a_qbd, 1)
                s32 = lambda l: ps[:, 4 * l + 1:4 * l + 4, 0:2 * (P + M)].rearrange("p a (q c) -> p a q c", q=2)
                for l in range(2):
                    dve.wait_ge(a_s3, now(l))
                    dve.tensor_reduce(m2[l][:, :], s32(l)[:, :, :, P:P + M], AX.X, ALU.max).then_inc(a_m2, 1)
                    dve.tensor_reduce(m3[l][:, :], s32(l)[:, :, :, 0:P], AX.X, ALU.max).then_inc(a_m3, 1)
                for l in range(2):
                    dve.wait_ge(a_m2, now(l))
                    dve.tensor_tensor(e2[l][:, :, :].rearrange("p (a q) c -> p a q c", q=2), s32(l)[:, :, :, P:P + M],
                                      bc(m2[l][:, :].rearrange("p (a q o) -> p a q o", q=2, o=1), [P, 3, 2, M]), ALU.subtract).then_inc(a_d2, 1)
                    dve.wait_ge(a_m3, now(l))
                    dve.tensor_tensor(e3[l][:, :, :].rearrange("p (a q) c -> p a q c", q=2), s32(l)[:, :, :, 0:P],
                                      bc(m3[l][:, :].rearrange("p (a q o) -> p a q o", q=2, o=1), [P, 3, 2, P]), ALU.subtract).then_inc(a_d3, 1)
                for l in range(2):
                    dve.wait_ge(a_e2, now(l))
                    dve.tensor_reduce(s2[l][:, :], e2[l][:, :, :], AX.X, ALU.add).then_inc(a_sum2, 1)
                for l in range(2):
                    dve.wait_ge(a_sum2, now(l))
                    dve.reciprocal(r2[l][:, :], s2[l][:, :]).then_inc(a_r2, 1)
                for l in range(2):
                    dve.wait_ge(a_r2, now(l))
                    for q in range(2):
                        dve.tensor_tensor(half(k2[l], q)[:, :, M * q:M * q + M], half(e2[l], q)[:, :, :],
                                          bc(col(half(r2[l], q)[:, :]), [64, NP, M]), ALU.mult).then_inc(a_k2, 1)
                v1 = lambda l, k, n: bank[l][k][:, 0:n * M].rearrange("p (a n) -> p a n", a=n)
                for l in range(2):
                    dve.wait_ge(a_s1, first(l))
                    dve.tensor_reduce(m1[l][:, 0:GH], v1(l, 0, GH), AX.X, ALU.max).then_inc(a_m1, 1)
                for l in range(2):
                    dve.wait_ge(a_m1, first(l))
                    dve.tensor_tensor(e1[l][:, 0:GH, :], v1(l, 0, GH), bc(col(m1[l][:, 0:GH]), [P, GH, M]), ALU.subtract).then_inc(a_d1, 1)
                for l in range(2):
                    dve.wait_ge(a_s1, second(l))
                    dve.tensor_reduce(m1[l][:, GH:H], v1(l, 1, H - GH), AX.X, ALU.max).then_inc(a_m1, 1)
                for l in range(2):
                    dve.wait_ge(a_m1, second(l))
                    dve.tensor_tensor(e1[l][:, GH:H, :], v1(l, 1, H - GH), bc(col(m1[l][:, GH:H]), [P, H - GH, M]), ALU.subtract).then_inc(a_d1, 1)
                for l in range(2):
                    dve.wait_ge(a_csT, now(l))
                    dve.tensor_reduce(csm[l][:, :], bank[l][0][0:NP, 0:P].rearrange("p (a n) -> p a n", a=2), AX.X, ALU.max).then_inc(a_csm, 1)
                for l in range(2):
                    dve.wait_ge(a_csm, now(l))
                    dve.reciprocal(csr[l][:, :], csm[l][:, :]).then_inc(a_csr, 1)
                for l in range(2):
                    dve.wait_ge(a_csr, now(l))
                    dve.tensor_copy(csb[l][:, :, :], bc(col(csr[l][:, :]), [NP, 2, M])).then_inc(a_csb, 1)
                for l in range(2):
                    dve.wait_ge(a_sb, now(l))
                    dve.tensor_scalar(r4[l][:, :], bank[l][0][:, 0:NP], 4.0, None, ALU.mult)
                    dve.tensor_scalar(r25[l][:, :], bank[l][0][:, 0:NP], 0.25, None, ALU.mult).then_inc(a_r4, 1)
                for l in range(2):
                    dve.wait_ge(a_up, now(l))
                    dve.reciprocal(u4[l][:, :], bank[l][3][:, 0:NP * 33].rearrange("p (a n) -> p a n", a=NP)[:, :, 32]).then_inc(a_u4, 1)
                for l in range(2):
                    dve.wait_ge(a_u4, now(l))
                    for q in range(2):
                        dve.scalar_tensor_tensor(half(g[l], q)[:, :, M:SW],
                                                 half(bank[l][3], q)[:, 0:NP * 33].rearrange("p (a n) -> p a n", a=NP)[:, :, D * q:D * q + D],
                                                 4.0, bc(col(half(u4[l], q)[:, :]), [64, NP, D]), ALU.mult, ALU.mult).then_inc(a_gw, 1)
                for l in range(2):
                    dve.wait_ge(a_x0, now(l))
                    dve.wait_ge(a_r4, now(l))
                    for q in range(2):
                        dve.tensor_tensor(half(g[l], q)[:, 0:4, 0:M], half(bank[l][1], q).rearrange("p (a n) -> p a n", a=4)[:, :, M * q:M * q + M],
                                          bc(col(half(r4[l], q)[:, 0:4]), [64, 4, M]), ALU.mult)
                        dve.tensor_tensor(half(g[l], q)[:, 4:6, 0:M], half(bank[l][2], q)[:, 0:2 * P].rearrange("p (a n) -> p a n", a=2)[:, :, M * q:M * q + M],
                                          bc(col(half(r4[l], q)[:, 4:6]), [64, 2, M]), ALU.mult).then_inc(a_g0, 1)
                pA = lambda l: bank[l][0][:, 0:NP * SW].rearrange("p (a n) -> p a n", a=NP)
                pZ = lambda l: bank[l][1][:, 0:NP * SW].rearrange("p (a n) -> p a n", a=NP)
                for k in range(ITERS):
                    at = lambda l: i * (2 * ITERS) + 2 * k + l + 1
                    for l in range(2):
                        if k == 0:
                            dve.wait_ge(a_g0, 4 * i + 2 * l + 2)
                            dve.wait_ge(a_gw, 4 * i + 2 * l + 2)
                        else:
                            dve.wait_ge(a_fix, i * (2 * ITERS) + 2 * (k - 1) + l + 1)
                        dve.scalar_tensor_tensor(wf[l][:, :, :], g[l][:, :, :], 1.75, eye15[:, :, :], ALU.mult, ALU.subtract).then_inc(a_wf, 1)
                    for l in range(2):
                        dve.wait_ge(a_y, 2 * at(l))
                        dve.wait_ge(a_wf, at(l))
                        dve.scalar_tensor_tensor(tt[l][:, :, :], pA(l), -1.0 / 16, wf[l][:, :, :], ALU.mult, ALU.add).then_inc(a_T, 1)
                        dve.tensor_scalar(aw[l][:, :, :], pA(l)[:, :, M:SW], 15.0 / 16, None, ALU.mult).then_inc(a_T, 1)
                    for l in range(2):
                        dve.wait_ge(a_Z, at(l))
                        dve.wait_ge(a_wf, at(l))
                        dve.scalar_tensor_tensor(g[l][:, :, :], g[l][:, :, :], 3.25, pZ(l), ALU.mult, ALU.add).then_inc(a_G, 1)
                    for l in range(2):
                        dve.wait_ge(a_G, at(l))
                        dve.wait_ge(a_T, 2 * at(l))
                        dve.tensor_tensor(g[l][:, :, M:SW], g[l][:, :, M:SW], aw[l][:, :, :], ALU.subtract).then_inc(a_fix, 1)
                for l in range(2):
                    dve.wait_ge(a_v0, now(l))
                    for q in range(2):
                        dve.tensor_tensor(half(wbd[l], q)[:, :, D * q:D * q + D], half(bank[l][0], q)[:, 0:NP * D].rearrange("p (a n) -> p a n", a=NP),
                                          bc(col(half(r25[l], q)[:, :]), [64, NP, D]), ALU.mult).then_inc(a_wbd, 1)
                po = lambda l: bank[l][2][:, 0:NP * 34].rearrange("p (a n) -> p a n", a=NP)
                for l in range(2):
                    dve.wait_ge(a_o, now(l))
                    dve.reciprocal(ro[l][:, :, :], po(l)[:, :, 32:34]).then_inc(a_ro, 1)
                for l in range(2):
                    dve.wait_ge(a_ro, now(l))
                    dve.tensor_tensor(sv[l][:, :].rearrange("p (a q d) -> p a q d", q=2, d=D),
                                      po(l)[:, :, 0:32].rearrange("p a (q d) -> p a q d", q=2),
                                      bc(ro[l][:, :, :].rearrange("p a (q o) -> p a q o", o=1), [P, NP, 2, D]), ALU.mult).then_inc(a_sv, 1)
                for l in range(2):
                    dve.tensor_tensor(xn[l][:, :], hrow(l), bpr[:, :], ALU.add).then_inc(a_res, 1)
                for l in range(2):
                    dve.wait_ge(a_res, now(l))
                    dve.tensor_tensor(hb[l][:, :].rearrange("p (a n) -> p a n", a=NP), xn[l][:, :].rearrange("p (a n) -> p a n", a=NP),
                                      v33[l][:, :, 0:2 * D], ALU.add).then_inc(a_hv, 1)
                for l in range(2):
                    dve.wait_ge(a_pr, now(l))
                    dve.wait_ge(a_hv, now(l))
                    dve.tensor_tensor(hrow(l), hb[l][:, :], bank[l][3][:, 0:C], ALU.add).then_inc(a_h1, 1)

            dve.wait_ge(a_h1, B)
            with dve.Fori(0, B // 4) as i:
                for hf in range(2):
                    now = lambda l: 4 * i + (2 * hf + l + 1)
                    hrow = lambda l: h[:, bass.ds(4 * i + (2 * hf + l), 1), :].rearrange("p o c -> p (o c)")
                    lgp = lambda l: ps[:, 4 * l:4 * l + 2, :].rearrange("p a (e s) -> p (a e) s", s=SL)
                    for l in range(2):
                        dve.bn_stats(rst6[l][:, :], hrow(l)).then_inc(r_stat, 1)
                    for l in range(2):
                        dve.wait_ge(r_stat, now(l))
                        dve.sem_inc(waited, 1)
                        dve.bn_aggr(rmv[l][:, :], rst6[l][:, :]).then_inc(r_mv, 1)
                    for l in range(2):
                        dve.wait_ge(r_mv, now(l))
                        dve.tensor_scalar(rve[l][:, :], rmv[l][:, 1:2], LN_EPS, 0.0, ALU.add, ALU.add).then_inc(r_ve, 1)
                    for l in range(2):
                        dve.wait_ge(r_rs, now(l))
                        dve.tensor_scalar(rx[l][:, :], hrow(l), rmv[l][:, 0:1], rrs[l][:, :], ALU.subtract, ALU.mult).then_inc(r_x, 1)
                    for l in range(2):
                        dve.wait_ge(r_rn, now(l))
                        dve.tensor_scalar(xe[l][:, 0:C], rx[l][:, :], rrn[l][:, :], None, ALU.mult).then_inc(r_xe, 1)
                        dve.tensor_scalar(xe[l][:, C:2 * P], rx[l][:, C0:C], rrn[l][:, :], None, ALU.mult).then_inc(r_xe, 1)
                    for l in range(2):
                        dve.wait_ge(r_xth, now(l))
                        dve.tensor_tensor(xt_lo[l][:, :, :], bank[l][2][:, 0:2 * P].rearrange("p (a n) -> p a n", a=2), xt_hi[l][:, :, :].bitcast(F32), ALU.subtract).then_inc(r_xtl, 1)
                    for l in range(2):
                        dve.wait_ge(r_lg, now(l))
                        dve.tensor_reduce(mx[l][:, :], lgp(l), AX.X, ALU.max).then_inc(r_mx, 1)
                    for l in range(2):
                        dve.wait_ge(r_mx, now(l))
                        dve.tensor_reduce(nm[l][:, :], mx[l][:, :], AX.X, ALU.max, negate=True).then_inc(r_nm, 1)
                        dve.tensor_tensor(lg[l][:, :, :], lgp(l), bc(col(mx[l][:, :]), [P, E, SL]), ALU.subtract).then_inc(r_d, 1)
                    for l in range(2):
                        dve.wait_ge(r_exp, now(l))
                        dve.tensor_reduce(ze[l][:, :], lg[l][:, :, :], AX.X, ALU.add).then_inc(r_z, 1)
                    for l in range(2):
                        dve.wait_ge(r_z, now(l))
                        dve.reciprocal(rz[l][:, :], ze[l][:, :]).then_inc(r_rz, 1)
                        dve.wait_ge(r_f, now(l))
                        dve.tensor_tensor(zf[l][:, :], ze[l][:, :], fe[l][:, :], ALU.mult).then_inc(r_zf, 1)
                    for l in range(2):
                        dve.wait_ge(r_rz, now(l))
                        dve.tensor_tensor(dw[l][:, :, :], lg[l][:, :, :], bc(col(rz[l][:, :]), [P, E, SL]), ALU.mult).then_inc(r_dw, 1)
                    for l in range(2):
                        dve.wait_ge(r_zf, now(l))
                        dve.tensor_reduce(zt[l][:, :], zf[l][:, :], AX.X, ALU.add).then_inc(r_zt, 1)
                    for l in range(2):
                        dve.wait_ge(r_zt, now(l))
                        dve.reciprocal(rzt[l][:, :], zt[l][:, :]).then_inc(r_rzt, 1)
                    for l in range(2):
                        dve.wait_ge(r_rzt, now(l))
                        dve.tensor_scalar(fz[l][:, :], fe[l][:, :], rzt[l][:, :], None, ALU.mult).then_inc(r_fz, 1)
                    for l in range(2):
                        dve.wait_ge(r_dh, now(l))
                        dve.tensor_tensor(dw_lo[l][:, :], dw[l][:, :, :].rearrange("p e s -> p (e s)"), dw_hi[l][:, :].bitcast(F32), ALU.subtract).then_inc(r_dl, 1)
                    for l in range(2):
                        dve.wait_ge(r_sm_p, now(l))
                        if hf == 0:
                            dve.wait_ge(stage_free, i + 1)
                        dve.tensor_copy(slm[:, :, 2 * hf + l, :], ps[:, 4 * l + 2:4 * l + 4, :].rearrange("p a (e s) -> p (a e) s", s=SL)).then_inc(r_slm, 1)

            def lo(e, m, q, part):
                if part == 0:
                    dve.wait_ge(w1_in[q], 48 * (m + 1))
                    dve.wait_ge(c_hi, 5 * e + 2)
                    dve.tensor_tensor(w1_lo[q][:, :], w1raw[q][:, 0, :], w1_hi[q][:, :].bitcast(F32), ALU.subtract).then_inc(c_lo_w1, 1)
                    dve.tensor_tensor(w1_st[q][64:128, :], w1raw[q][64:128, 1, :], w1_st[q][64:128, :].bitcast(F32), ALU.subtract).then_inc(c_lo_w1, 1)
                elif part == 1:
                    dve.wait_ge(slots_in[q], 48 * (m + 1))
                    dve.wait_ge(c_hi, 5 * e + 4)
                    dve.tensor_tensor(xs_lo[q][:, :, :], xsm[q][:, :, :], xs_hi[q][:, :, :].bitcast(F32), ALU.subtract).then_inc(c_lo_xs, 1)
                else:
                    dve.wait_ge(w2_in[q], 16 * (m + 1))
                    dve.wait_ge(c_hi, 5 * e + 5)
                    dve.tensor_tensor(w2_hl[q][:, :, C:2 * C], w2raw[q][:, :, :], w2_hl[q][:, :, 0:C].bitcast(F32), ALU.subtract).then_inc(c_lo_w2, 1)

            def combine(gr, k):
                dve.wait_ge(c_comb_ps, gr * (B // 2) + (k + 1))
                dve.tensor_tensor(h[:, 2 * k:2 * k + 2, :], h[:, 2 * k:2 * k + 2, :],
                                  ps[:, 6 + k % 2, 0:2 * C].rearrange("p (b d) -> p b d", b=2), ALU.add).then_inc(c_comb, 1)

            def biased(e, m, q, fresh):
                dve.wait_ge(b2_in[q], 16 * (m + 1))
                if not fresh:
                    dve.wait_ge(eog_in[q], 64 * m)
                for a in range(4):
                    dve.wait_ge(c_output, OC * (e + 1) - 3 + a)
                    dve.tensor_tensor(eos[:, a, :], ps[:, 2 + a, 0:C], b2row[q][:, :], ALU.add).then_inc(c_eos, 1)
                for a in range(4):
                    dve.wait_ge(c_eos, 4 * e + a + 1)
                    dve.tensor_tensor(eo[q][:, a, :], eos[:, a, :], ps[:, 2 + a, C:2 * C], ALU.add).then_inc(c_eo, 1)

            dve.wait_ge(slots_out, 32 * (B // 4))
            for l in range(2):
                dve.wait_ge(comb_out[l], 16 * (B // 2))
            dve.sem_inc(c_comb, 2)
            for part in range(3):
                lo(0, 0, 0, part)

            def group(gr, last, par):
                first = isinstance(gr, int) and gr == 0
                for j in range(GE):
                    e, q = gr * GE + j, j % 2
                    for k in range(HC):
                        t = j * HC + k
                        n = gr * (GE * HC) + t
                        dve.wait_ge(c_hhi, n + 1)
                        dve.tensor_tensor(h_lo[t % 3][:, :], hraw[t % 2][:, :], h_hi[t % 3][:, :].bitcast(F32), ALU.subtract).then_inc(c_hlo, 1)
                        if k == 0 and not (first and j == 0):
                            biased(e - 1, gr * 2 + (j - 1) // 2, (j - 1) % 2, first and j - 1 < 2)
                        if not first and COMB_AT < t <= COMB_AT + B // 2:
                            combine(gr - 1, t - COMB_AT - 1)
                        if 1 <= k <= 3 and not (last and j == GE - 1):
                            lo(gr * GE + (j + 1), gr * 2 + (j + 1) // 2, (j + 1) % 2, k - 1)

            group(0, False, 0)
            with dve.Fori(0, NG // 2 - 1) as i:
                for k in range(2):
                    group(2 * i + (k + 1), False, (k + 1) % 2)
            group(NG - 1, True, (NG - 1) % 2)
            biased(E - 1, E // 2 - 1, (E - 1) % 2, False)
            for b in range(B // 2):
                combine(NG - 1, b)

        @block.tensor
        def _(pe):
            mm = pe.matmul
            pe.wait_ge(i_ident, 1)
            pe.wait_ge(wn_in, 48)
            for k in range(2):
                rows = P if k == 0 else 64
                for t in range(8):
                    last = pe.transpose(bank[0][2 * k + t // 4][0:rows, 96 * (t % 4):96 * (t % 4) + 96], wn[:, t, P * k:P * k + rows], ident[0:96, 0:96])
            last.then_inc(i_wnT, 1)
            for t in range(2):
                last = pe.transpose(bank[1][0][:, 96 * t:96 * t + 96], b1n[:, t, :], ident[0:96, 0:96])
            last.then_inc(i_b1n, 1)
            pe.wait_ge(i_sq, 2)
            pe.wait_ge(i_pool, 1)
            for a in range(2):
                mm(bank[1][1 + a], ones[:, :], phn[:, 512 * a:512 * a + 512], start=True, stop=False)
                last = mm(bank[1][1 + a], ones[0:64, :], pht[0:64, 512 * a:512 * a + 512], start=False, stop=True)
            last.then_inc(i_ss, 1)
            pe.wait_ge(i_wT, 6)
            pe.wait_ge(i_b1T, 1)
            pe.wait_ge(i_n, 1)
            pe.wait_ge(i_pool, 17)

            with pe.Fori(0, B // 2) as i:
                now = lambda l: 2 * i + (l + 1)
                first = lambda l: 4 * i + (l + 1)
                second = lambda l: 4 * i + (l + 3)
                for l in range(2):
                    pe.wait_ge(a_xn, now(l))
                    pe.transpose(bank[l][0][:, 0:P], xn[l][:, 0:P], ident[:, 0:P])
                    pe.transpose(bank[l][0][0:64, P:2 * P], xn[l][:, P:C], ident[:, 0:P]).then_inc(a_xTp, 1)
                for l in range(2):
                    pe.wait_ge(a_xT, now(l))
                    for a in range(4):
                        mm(bank[l][1][:, P * a:P * a + P], wT[:, 0, P * a:P * a + P], xT[l][:, 0, :], start=True, stop=False)
                        last = mm(bank[l][1][:, P * a:P * a + P], wT[0:64, 1, P * a:P * a + P], xT[l][0:64, 1, :], start=False, stop=True)
                    last.then_inc(a_qkp, 1)
                    mm(bank[l][2][:, 0:C], xT[l][:, 0, :], wT[:, 0, 512:704], start=True, stop=False)
                    mm(bank[l][2][:, 0:C], xT[l][0:64, 1, :], wT[0:64, 1, 512:704], start=False, stop=True).then_inc(a_vp, 1)
                for l in range(2):
                    pe.wait_ge(a_qbd, now(l))
                    pe.wait_ge(a_kk, now(l))
                    pe.wait_ge(a_k, now(l))
                    pe.wait_ge(a_v, now(l))
                    for p in range(NP):
                        last = mm(bank[l][1 + p // 2][:, (P + M) * (p % 2):(P + M) * (p % 2 + 1)],
                                  qbd[l][:, 2 * p:2 * p + 2, :].rearrange("p a n -> p (a n)"), kk[l][:, p // 4, :], start=True, stop=True)
                    last.then_inc(a_s3, 1)
                for l in range(2):
                    pe.wait_ge(a_kbd, now(l))
                    mm(bank[l][0], qT[l][:, 0, :], kbd[l][:, 0:GH, :].rearrange("p a n -> p (a n)"), start=True, stop=True).then_inc(a_s1, 1)
                for l in range(2):
                    pe.wait_ge(a_d3, now(l))
                    pe.wait_ge(a_d2, now(l))
                    mm(bank[l][1][:, 0:256], qT[l][:, 1, :], kbd[l][:, GH:H, :].rearrange("p a n -> p (a n)"), start=True, stop=True).then_inc(a_s1, 1)
                for l in range(2):
                    pe.wait_ge(a_e3, now(l))
                    for p in range(NP):
                        last = pe.transpose(bank[l][2 + p // 4][:, P * (p % 4):P * (p % 4) + P], e3[l][:, p, :], ident[:, 0:P])
                    last.then_inc(a_k3p, 1)
                for l in range(2):
                    pe.wait_ge(a_k2, 2 * now(l))
                    pe.wait_ge(a_d1, first(l))
                    pe.wait_ge(a_d1, second(l))
                    for p in range(NP):
                        last = mm(bank[l][p // 3][:, (P + 1) * (p % 3):(P + 1) * (p % 3 + 1)], k2[l][:, p, :], ident[:, :], start=True, stop=True)
                    last.then_inc(a_k2p, 1)
                for l in range(2):
                    pe.wait_ge(a_k2T, now(l))
                    pe.transpose(bank[l][0][0:NP, 0:P], k2T[l][:, :, P], ident[:, 0:P]).then_inc(a_csT, 1)
                for l in range(2):
                    pe.wait_ge(a_k3T, now(l))
                    for p in range(NP):
                        last = mm(bank[l][3][:, 33 * p:33 * p + 33], k3T[l][:, p, :], v33[l][:, p, :], start=True, stop=True)
                    last.then_inc(a_up, 1)
                for l in range(2):
                    for p in range(NP):
                        last = mm(bank[l][1 + p // 4][:, P * (p % 4):P * (p % 4) + P], k2T[l][:, p, 0:P], k2T[l][:, p, 0:P], start=True, stop=True)
                    last.then_inc(a_x0, 1)
                for l in range(2):
                    pe.wait_ge(a_csb, now(l))
                    mm(bank[l][0][:, 0:NP], csb[l][:, :, :].rearrange("p a n -> p (a n)"), ident[0:NP, 0:NP], start=True, stop=True).then_inc(a_sb, 1)
                for k in range(ITERS):
                    at = lambda l: i * (2 * ITERS) + 2 * k + l + 1
                    for l in range(2):
                        pe.wait_ge(a_gbd, 2 * at(l))
                        if k == 0:
                            pe.wait_ge(a_gw, 4 * i + 2 * l + 2)
                        else:
                            pe.wait_ge(a_fix, i * (2 * ITERS) + 2 * (k - 1) + l + 1)
                        for p in range(NP):
                            last = mm(bank[l][0][:, SW * p:SW * p + SW], gbd[l][:, p, :], g[l][:, p, :], start=True, stop=True)
                        last.then_inc(a_A, 1)
                    if k == 0:
                        for l in range(2):
                            pe.wait_ge(a_e1, now(l))
                            for p in range(NP):
                                last = pe.transpose(bank[l][2 + p // 4][:, P * (p % 4):P * (p % 4) + P],
                                                    e1[l][:, 2 * p:2 * p + 2, :].rearrange("p a n -> p (a n)"), ident[:, 0:P])
                            last.then_inc(a_k1p, 1)
                    for l in range(2):
                        pe.wait_ge(a_T, 2 * at(l))
                        for p in range(NP):
                            last = mm(bank[l][1][:, SW * p:SW * p + SW], ybd[l][:, p, :], tt[l][:, p, :], start=True, stop=True)
                        last.then_inc(a_Z, 1)
                for l in range(2):
                    pe.wait_ge(a_fix, i * (2 * ITERS) + 2 * (ITERS - 1) + l + 1)
                    for p in range(NP):
                        last = mm(bank[l][0][:, D * p:D * p + D], k2[l][:, p, :], g[l][:, p, M:SW], start=True, stop=True)
                    last.then_inc(a_v0, 1)
                for l in range(2):
                    pe.wait_ge(a_wbd, 2 * now(l))
                    pe.wait_ge(a_k1T, now(l))
                    for p in range(NP):
                        last = mm(bank[l][2][:, 34 * p:34 * p + 34], k1T[l][:, p, :], wbd[l][:, p, :], start=True, stop=True)
                    last.then_inc(a_o, 1)
                for l in range(2):
                    pe.wait_ge(a_sv, now(l))
                    pe.transpose(bank[l][1][:, 0:P], sv[l][:, 0:P], ident[:, 0:P])
                    pe.transpose(bank[l][1][0:64, P:2 * P], sv[l][:, P:C], ident[:, 0:P]).then_inc(a_svp, 1)
                for l in range(2):
                    pe.wait_ge(a_svT, now(l))
                    mm(bank[l][3][:, 0:C], svT[l][:, 0, :], pT[:, 0, :], start=True, stop=False)
                    mm(bank[l][3][:, 0:C], svT[l][0:64, 1, :], pT[0:64, 1, :], start=False, stop=True).then_inc(a_pr, 1)

            pe.wait_ge(a_h1, B)
            pe.wait_ge(i_phi, 12)
            with pe.Fori(0, B // 4) as i:
                for hf in range(2):
                    now = lambda l: 4 * i + (2 * hf + l + 1)
                    for l in range(2):
                        pe.wait_ge(r_xe, 2 * now(l))
                        for a in range(2):
                            last = pe.transpose(bank[l][2][:, P * a:P * a + P], xe[l][:, P * a:P * a + P], ident[:, 0:P])
                        last.then_inc(r_xtp, 1)
                    for l in range(2):
                        pe.wait_ge(r_xth, now(l))
                        pe.wait_ge(r_xtl, now(l))
                        for a in range(2):
                            cols = slice(512 * a, 512 * a + 512)
                            mm(bank[l][a], xt_hi[l][:, 0, :], ph_hi[:, cols], start=True, stop=False)
                            mm(bank[l][a], xt_hi[l][:, 0, :], ph_lo[:, cols], start=False, stop=False)
                            mm(bank[l][a], xt_lo[l][:, 0, :], ph_hi[:, cols], start=False, stop=False)
                            mm(bank[l][a], xt_hi[l][:, 1, :], ph_st[:, cols], start=False, stop=False)
                            last = mm(bank[l][a], xt_lo[l][:, 1, :], ph_st[:, cols], start=False, stop=True)
                        last.then_inc(r_lg, 1)
                    for l in range(2):
                        pe.wait_ge(r_xel, now(l))
                        pe.wait_ge(r_dl, now(l))
                        for part, first_bank in ((0, 2), (1, 0)):
                            for a in range(2):
                                cols = slice(512 * a, 512 * a + 512)
                                chans = slice(P * part, P * part + P)
                                mm(bank[l][first_bank + a], xe_hi[l][:, chans], dw_hi[l][:, cols], start=True, stop=False)
                                mm(bank[l][first_bank + a], xe_hi[l][:, chans], dw_lo[l][:, cols], start=False, stop=False)
                                last = mm(bank[l][first_bank + a], xe_lo[l][:, chans], dw_hi[l][:, cols], start=False, stop=True)
                            last.then_inc(r_sm_p if part == 0 else r_sr_p, 1)
                    for l in range(2):
                        pe.wait_ge(r_cw, now(l))
                        pe.wait_ge(r_slm, now(l))
                        for gq in range(NG):
                            last = pe.transpose(bank[l][2 + gq // 4][:, P * (gq % 4):P * (gq % 4) + P],
                                                cw[l][:, GE * gq:GE * gq + GE, :].rearrange("p e s -> p (e s)"), ident[:, 0:P])
                        last.then_inc(r_cwp, 1)
                    pe.wait_ge(r_slr, now(1))
                    pe.wait_ge(r_cwT, now(1))

            def hidden(gr, t):
                j, k = t // HC, t % HC
                e, q = gr * GE + j, j % 2
                n = gr * (GE * HC) + t
                cols = slice(P * k, P * k + P)
                if k == 0:
                    pe.wait_ge(c_hi, 5 * e + 4)
                    pe.wait_ge(c_lo_w1, 2 * e + 2)
                    pe.wait_ge(c_lo_xs, e + 1)
                if not (isinstance(gr, int) and gr == 0 and t < 2):
                    pe.wait_ge(c_gelu, n - 1)
                dst = ps[:, t % 2, :]
                mm(dst, w1_hi[q][:, cols], xs_hi[q][:, 0, :], start=True, stop=False)
                mm(dst, w1_hi[q][:, cols], xs_lo[q][:, 0, :], start=False, stop=False)
                mm(dst, w1_lo[q][:, cols], xs_hi[q][:, 0, :], start=False, stop=False)
                mm(dst, w1_st[q][:, cols], xs_hi[q][:, 1, :], start=False, stop=False)
                mm(dst, w1_st[q][:, cols], xs_lo[q][:, 1, :], start=False, stop=True).then_inc(c_hidden, 1)

            def output(gr, t):
                j, k = t // HC, t % HC
                e, q = gr * GE + j, j % 2
                n = gr * (GE * HC) + t
                if k == 0:
                    pe.wait_ge(c_hi, 5 * e + 5)
                    pe.wait_ge(c_lo_w2, e + 1)
                pe.wait_ge(c_hlo, n + 1)
                for a in range(4):
                    rows = slice(P * a, P * a + P)
                    dst = ps[:, 2 + a, 0:C]
                    if k == 0 and not (isinstance(e, int) and e == 0):
                        pe.wait_ge(c_eo, 4 * e - 3 + a)
                    mm(ps[:, 2 + a, 0:2 * C], h_hi[t % 3][:, rows], w2_hl[q][:, k, :], start=(k == 0), stop=False)
                    last = mm(dst, h_lo[t % 3][:, rows], w2_hl[q][:, k, 0:C], start=False, stop=(k == HC - 1))
                    if k == HC - 1:
                        last.then_inc(c_output, 1)
                if k < HC - 1:
                    last.then_inc(c_output, 1)

            def combine(gr, k, par):
                if k == 0:
                    pe.wait_ge(comb_in, 16 * (gr + 1))
                    for q in range(2):
                        pe.wait_ge(eog_in[q], 128 * (gr + 1))
                pe.wait_ge(c_comb, gr * (B // 2) + (k + 1))
                for b in range(2):
                    last = mm(ps[:, 6 + k % 2, C * b:C * b + C], cwg[par][:, 2 * k + b, :], eog[par][:, 2 * k + b, :], start=True, stop=True)
                last.then_inc(c_comb_ps, 1)

            pe.wait_ge(slots_out, 32 * (B // 4))
            for l in range(2):
                pe.wait_ge(comb_out[l], 16 * (B // 2))
            hidden(0, 0)
            hidden(0, 1)

            def group(gr, last, par):
                first = isinstance(gr, int) and gr == 0
                nt = GE * HC
                for t in range(nt):
                    if t + 2 < nt:
                        hidden(gr, t + 2)
                    elif not last:
                        hidden(gr + 1, t + 2 - nt)
                    output(gr, t)
                    if not first and COMB_AT <= t < COMB_AT + B // 2:
                        combine(gr - 1, t - COMB_AT, 1 - par)

            group(0, False, 0)
            with pe.Fori(0, NG // 2 - 1) as i:
                for k in range(2):
                    group(2 * i + (k + 1), False, (k + 1) % 2)
            group(NG - 1, True, (NG - 1) % 2)
            for k in range(B // 2):
                combine(NG - 1, k, (NG - 1) % 2)


_INS = ['x', 'mask_BS_i1_0', 'L0_tok_tok_w', 'L0_tok_pos_w', 'L0_tok_type_w', 'L0_tok_gamma', 'L0_tok_beta',
        'L0_attn_w_qkv', 'L0_attn_w_proj', 'L0_attn_b_proj', 'L0_ffn_phi', 'L0_ffn_scale', 'L0_ffn_w1',
        'L0_ffn_b1', 'L0_ffn_w2', 'L0_ffn_b2']
_OUTS = [((16, 128, 192), 'float32')]


def kernel(**inputs):
    import numpy as _np
    import concourse.bacc as _bacc
    from concourse.bass_utils import run_bass_kernel_spmd as _run

    nc = _bacc.Bacc("TRN2", target_bir_lowering=False, num_devices=1)
    arrays, args = {}, []
    for name in _INS:
        a = _np.ascontiguousarray(inputs[name])
        arrays[f"in_{name}_dram"] = a
        args.append(nc.dram_tensor(f"in_{name}_dram", a.shape, mybir.dt.from_np(a.dtype), kind="ExternalInput").ap())
    for i, (shape, dtype) in enumerate(_OUTS):
        args.append(nc.dram_tensor(f"out_{i}_dram", shape, mybir.dt.from_np(_np.dtype(dtype)), kind="ExternalOutput").ap())
    build(nc, *args)
    r = _run(nc, [arrays], core_ids=[0])
    return r.results[0]["out_0_dram"]
```

```python
from contextlib import ExitStack

import concourse.bass as bass
from concourse import mybir

F32 = mybir.dt.float32
F32R = mybir.dt.float32r
I32 = mybir.dt.int32
ALU = mybir.AluOpType
ACT = mybir.ActivationFunctionType
AX = mybir.AxisListType

P = 128
LN_EPS = 1e-5
NORM_EPS2 = 1e-24


def build(nc, x, type_ids, tok_w, pos_w, type_w, gamma, beta, w_qkv, w_proj, b_proj,
          phi, scale, w1, b1, w2, b2, out):
    B, S = x.shape
    C = tok_w.shape[1]
    C0, C1 = P, C - P
    H, M = 12, 64
    D = C // H
    NP = H // 2
    GH = P // D
    E, SL = phi.shape[1], phi.shape[2]
    ES = E * SL
    HID = w1.shape[2]
    HC = HID // P
    R = B * SL
    GE = P // SL
    NG = E // GE
    ITERS = 6
    COMB_AT = 5
    SW = M + D
    MW = P
    assert S == P and B % 4 == 0 and M == 64 and C1 == 64 and R == 512

    slots_dram = nc.dram_tensor("slots_dram", [C, B // 4, E, 4 * SL], F32).ap()
    comb_dram = nc.dram_tensor("comb_dram", [NG, P, B, S], F32).ap()

    with ExitStack() as ctx:
        def sb(name, shape, dt=F32, where=ctx):
            return where.enter_context(nc.sbuf_tensor(name, shape, dt))

        h = sb("h", [P, B, C])
        ident = sb("ident", [P, P + 1])
        b1T = sb("b1T", [P, E * HC])
        w1raw = [sb(f"w1raw{q}", [P, 2, HID]) for q in range(2)]
        w2raw = [sb(f"w2raw{q}", [P, HC, C]) for q in range(2)]
        b2row = [sb(f"b2row{q}", [P, C]) for q in range(2)]

        front = ExitStack()
        fb = lambda name, shape, dt=F32: sb(name, shape, dt, front)
        ids = fb("ids", [P, B], I32)
        tids = fb("tids", [P, B], I32)
        tidf = fb("tidf", [P, B])
        pos = fb("pos", [P, C])
        ty = fb("ty", [P, 2, C])
        gam = fb("gam", [P, C])
        bet = fb("bet", [P, C])
        bpr = fb("bpr", [P, C])
        scl = fb("scl", [P, 1])
        expo = fb("expo", [P, 1])
        ones = fb("ones", [P, P])
        mask8 = fb("mask8", [P, GH, M])
        wT = fb("wT", [P, 2, 256 + 256 + C])
        pT = fb("pT", [P, 2, C])
        ph_hi = fb("ph_hi", [P, ES], F32R)
        ph_lo = fb("ph_lo", [P, ES], F32R)
        ph_st = fb("ph_st", [P, ES], F32R)

        att = ExitStack()
        two = lambda name, shape, dt=F32, w=att: [sb(f"{name}{l}", shape, dt, w) for l in range(2)]
        xn = two("xn", [P, C])
        st6 = two("st6", [P, 6])
        mv = two("mv", [P, 2])
        ve = two("ve", [P, 1])
        rs = two("rs", [P, 1])
        xT = two("xT", [P, 2, P])
        qT = two("qT", [P, 2, P])
        kk = two("kk", [P, 2, P + M])
        v33 = two("v33", [P, NP, SW])
        ql = two("ql", [P, 2, M])
        kl = two("kl", [P, 2, M])
        qbd = two("qbd", [P, H, M])
        kbd = two("kbd", [P, H, M])
        m3 = two("m3", [P, NP])
        m2 = two("m2", [P, NP])
        m1 = two("m1", [P, H])
        e3 = two("e3", [P, NP, P])
        e2 = two("e2", [P, NP, M])
        e1 = two("e1", [P, H, M])
        s2 = two("s2", [P, NP])
        r2 = two("r2", [P, NP])
        k2 = two("k2", [P, NP, P])
        k2T = two("k2T", [P, NP, P + 1])
        k3T = two("k3T", [P, NP, P])
        k1T = two("k1T", [P, NP, P])
        csm = two("csm", [NP, 2])
        csr = two("csr", [NP, 2])
        csb = two("csb", [NP, 2, M])
        r4 = two("r4", [P, NP])
        r25 = two("r25", [P, NP])
        u4 = two("u4", [P, NP])
        g = two("g", [P, NP, MW])
        gbd = two("gbd", [P, NP, P])
        ybd = two("ybd", [P, NP, P])
        tt = two("tt", [P, NP, MW])
        wf = two("wf", [P, NP, SW])
        wbd = two("wbd", [P, NP, SW])
        ro = two("ro", [P, NP, 2])
        sv = two("sv", [P, C])
        svT = two("svT", [P, 2, P])
        hb = two("hb", [P, C])
        res = two("res", [P, C])
        wn = sb("wn", [96, 8, C], F32, att)
        b1n = sb("b1n", [96, 2, P], F32, att)
        phraw = sb("phraw", [P, 2, ES], F32, att)
        phn = sb("phn", [P, ES], F32, att)
        pht = sb("pht", [P, ES], F32, att)
        att.close()

        rt = ExitStack()
        rx = two("rx", [P, C], w=rt)
        rst6 = two("rst6", [P, 6], w=rt)
        rmv = two("rmv", [P, 2], w=rt)
        rve = two("rve", [P, 1], w=rt)
        rrs = two("rrs", [P, 1], w=rt)
        rsq = two("rsq", [P, C], w=rt)
        rss = two("rss", [P, 1], w=rt)
        rsm = two("rsm", [P, 1], w=rt)
        rrn = two("rrn", [P, 1], w=rt)
        xe = two("xe", [P, 2 * P], w=rt)
        xe_hi = two("xe_hi", [P, 2 * P], F32R, rt)
        xe_lo = two("xe_lo", [P, 2 * P], F32R, rt)
        xt_hi = two("xt_hi", [P, 2, P], F32R, rt)
        xt_lo = two("xt_lo", [P, 2, P], F32R, rt)
        mx = two("mx", [P, E], w=rt)
        nm = two("nm", [P, 1], w=rt)
        fe = two("fe", [P, E], w=rt)
        ze = two("ze", [P, E], w=rt)
        rz = two("rz", [P, E], w=rt)
        zf = two("zf", [P, E], w=rt)
        zt = two("zt", [P, 1], w=rt)
        rzt = two("rzt", [P, 1], w=rt)
        fz = two("fz", [P, E], w=rt)
        lg = two("lg", [P, E, SL], w=rt)
        dw = two("dw", [P, E, SL], w=rt)
        dw_hi = two("dw_hi", [P, ES], F32R, rt)
        dw_lo = two("dw_lo", [P, ES], F32R, rt)
        cwT = two("cwT", [P, 2, NG, P], w=rt)
        slm = two("slm", [P, E, 4, SL], w=rt)
        slr = [sb(f"slr{k}", [C1, E, 4, SL], F32, rt) for k in range(2)]
        rt.close()
        front.close()

        xsm = two("xsm", [P, 2, R], w=ctx)
        w1_hi = two("w1_hi", [P, HID], F32R, ctx)
        w1_lo = two("w1_lo", [P, HID], F32R, ctx)
        w1_st = two("w1_st", [P, HID], F32R, ctx)
        w2_hl = two("w2_hl", [P, HC, 2 * C], F32R, ctx)
        eos = sb("eos", [P, 4, C])
        xs_hi = two("xs_hi", [P, 2, R], F32R, ctx)
        xs_lo = two("xs_lo", [P, 2, R], F32R, ctx)
        hraw = two("hraw", [P, R], w=ctx)
        h_hi = [sb(f"h_hi{k}", [P, R], F32R) for k in range(3)]
        h_lo = [sb(f"h_lo{k}", [P, R], F32R) for k in range(3)]
        eo = two("eo", [P, 4, C], w=ctx)
        eog = [sb(f"eog{k}", [P, B, C]) for k in range(2)]
        cwg = [sb(f"cwg{k}", [P, B, S]) for k in range(2)]

        ps = ctx.enter_context(nc.psum_tensor("ps", [P, 8, 512], F32))
        bank = [[ps[:, 4 * l + k, :] for k in range(4)] for l in range(2)]

        def sems(text):
            return [ctx.enter_context(nc.semaphore(n)) for n in text.split()]

        (ids_in, consts_in, first_tokens_in, tokens_in, phi_in, wn_in, comb_out0, comb_out1, comb_out2, comb_out3,
         slots_out, w1_in0, w1_in1, w2_in0, w2_in1, b2_in0, b2_in1, slots_in0, slots_in1, eog_in0, eog_in1,
         comb_in, y_out) = sems(
            "ids_in consts_in first_tokens_in tokens_in phi_in wn_in comb_out0 comb_out1 comb_out2 comb_out3 "
            "slots_out w1_in0 w1_in1 w2_in0 w2_in1 b2_in0 b2_in1 slots_in0 slots_in1 eog_in0 eog_in1 comb_in "
            "y_out")
        (identity_ready, masks_ready, memsets_done, type_rows_ready, weights_transposed, weights_ready, b1_ready,
         phi_squared, phi_summed, phi_sums_guarded, phi_rooted, phi_steps) = sems(
            "identity_ready masks_ready memsets_done type_rows_ready weights_transposed weights_ready b1_ready "
            "phi_squared phi_summed phi_sums_guarded phi_rooted phi_steps")
        (a_tokens_placed, a_row_stats, a_row_mean_var, a_row_var_eps, a_row_rstd, a_embedded, a_embedding_normed,
         a_rows_normed, a_rowsT_psum, a_rowsT, a_qk_psum, a_v_psum, a_queries, a_keys, a_values, a_query_landmarks,
         a_key_pairs_summed, a_query_landmarks_bd, a_key_landmarks_bd, a_key_landmarks, a_scores32_psum,
         a_scores1_psum, a_max3, a_max2, a_diff3, a_diff2, a_max1, a_diff1, a_exp3, a_exp2, a_exp1, a_sums2,
         a_inv_sums2, a_kernel2_bd, a_kernel3T_psum, a_kernel3T, a_kernel2T_psum, a_kernel2T, a_column_sums_psum,
         a_scale_max, a_scale_inverted, a_scale_rows, a_scale_psum, a_scale_spread, a_residual_bias, a_residual_v,
         a_kernel2_square_psum, a_kernel3_v_psum, a_inv_sums3, a_state_w0, a_state_X0, a_state_bd, a_state_carry,
         a_square_psum, a_square_bd, a_T, a_YT_psum, a_state, a_kernel1T_psum, a_kernel1T, a_inverse_kv_psum,
         a_inverse_kv_bd, a_attended_psum, a_inv_sums1, a_attended, a_attendedT_psum, a_attendedT,
         a_projected_psum, a_embedded_gamma, a_attention_done) = sems(
            "a_tokens_placed a_row_stats a_row_mean_var a_row_var_eps a_row_rstd a_embedded a_embedding_normed "
            "a_rows_normed a_rowsT_psum a_rowsT a_qk_psum a_v_psum a_queries a_keys a_values a_query_landmarks "
            "a_key_pairs_summed a_query_landmarks_bd a_key_landmarks_bd a_key_landmarks a_scores32_psum "
            "a_scores1_psum a_max3 a_max2 a_diff3 a_diff2 a_max1 a_diff1 a_exp3 a_exp2 a_exp1 a_sums2 "
            "a_inv_sums2 a_kernel2_bd a_kernel3T_psum a_kernel3T a_kernel2T_psum a_kernel2T a_column_sums_psum "
            "a_scale_max a_scale_inverted a_scale_rows a_scale_psum a_scale_spread a_residual_bias a_residual_v "
            "a_kernel2_square_psum a_kernel3_v_psum a_inv_sums3 a_state_w0 a_state_X0 a_state_bd a_state_carry "
            "a_square_psum a_square_bd a_T a_YT_psum a_state a_kernel1T_psum a_kernel1T a_inverse_kv_psum "
            "a_inverse_kv_bd a_attended_psum a_inv_sums1 a_attended a_attendedT_psum a_attendedT "
            "a_projected_psum a_embedded_gamma a_attention_done")
        (r_row_stats, r_row_mean_var, r_row_var_eps, r_row_rstd, r_rows_normed, r_row_squares, r_squares_guarded,
         r_inv_length, r_unit_rows, r_rowsT_psum, r_rowsT_high, r_rowsT_low, r_rows_high, r_rows_low,
         r_logits_psum, r_expert_max, r_row_max, r_exp_max, r_diffs, r_exps, r_expert_sums, r_inv_expert_sums,
         r_weighted_sums, r_row_sum, r_inv_row_sum, r_combine_factor, r_dispatch, r_dispatch_high, r_dispatch_low,
         r_slots_main_psum, r_slots_rest_psum, r_slots_main, r_slots_rest, r_combine, r_combineT_psum,
         r_combineT) = sems(
            "r_row_stats r_row_mean_var r_row_var_eps r_row_rstd r_rows_normed r_row_squares r_squares_guarded "
            "r_inv_length r_unit_rows r_rowsT_psum r_rowsT_high r_rowsT_low r_rows_high r_rows_low "
            "r_logits_psum r_expert_max r_row_max r_exp_max r_diffs r_exps r_expert_sums r_inv_expert_sums "
            "r_weighted_sums r_row_sum r_inv_row_sum r_combine_factor r_dispatch r_dispatch_high r_dispatch_low "
            "r_slots_main_psum r_slots_rest_psum r_slots_main r_slots_rest r_combine r_combineT_psum r_combineT")
        (c_high_halves, c_w1_low, c_slots_low, c_w2_low, c_hidden_psum, c_gelu, c_hidden_high, c_hidden_low,
         c_output_psum, c_output_partial, c_output, c_combined_psum, c_combined) = sems(
            "c_high_halves c_w1_low c_slots_low c_w2_low c_hidden_psum c_gelu c_hidden_high c_hidden_low "
            "c_output_psum c_output_partial c_output c_combined_psum c_combined")
        comb_out = [comb_out0, comb_out1, comb_out2, comb_out3]
        w1_in, w2_in, b2_in = [w1_in0, w1_in1], [w2_in0, w2_in1], [b2_in0, b2_in1]
        slots_in, eog_in = [slots_in0, slots_in1], [eog_in0, eog_in1]

        stage_free = ctx.enter_context(nc.semaphore("stage_free"))
        waited = ctx.enter_context(nc.semaphore("waited"))

        block = ctx.enter_context(nc.Block())

        def half(t, q):
            return t[64 * q:64 * q + 64]

        def pairs(c):
            return slice(NP // 2 * c, NP // 2 * (c + 1))

        def pA(l, c):
            return bank[l][2 * c][:, 0:NP // 2 * MW].rearrange("p (a n) -> p a n", a=NP // 2)

        def pZ(l, c):
            return bank[l][2 * c + 1][:, 0:NP // 2 * MW].rearrange("p (a n) -> p a n", a=NP // 2)

        def now(l, i):
            return 2 * i + (l + 1)

        def first(l, i):
            return 4 * i + (2 * l + 1)

        def second(l, i):
            return 4 * i + (2 * l + 2)

        def step(l, i, k, c):
            return i * (4 * ITERS) + (2 * ITERS * l + 2 * k + c + 1)

        def attention_schedule(engine, phase, start, end):
            start()
            phase(0, 0, False, True, True)
            with engine.Fori(0, B // 2 - 2) as i:
                phase(1, i, True, True, True)
                phase(0, i + 1, True, True, True)
            phase(1, B // 2 - 2, True, True, True)
            phase(0, B // 2 - 1, True, True, False)
            phase(1, B // 2 - 1, True, False, False)
            end()

        def seq(i, r):
            return 8 * i + (r + 1)

        def routing_schedule(engine, phase, start, end):
            with engine.Fori(0, B // 8) as i:
                start(i)
                for r in range(8):
                    phase(i, r)
                end(i)

        def other(a, i):
            return (1, i - 1, i) if a == 0 else (0, i, i + 1)

        OC = HC + 3

        def outputs_done(t):
            return OC * (t // HC) + (OC if t % HC == HC - 1 else t % HC + 1)

        def bc(ap, shape):
            return ap.to_broadcast(shape)

        @block.sync
        def _(sp):
            sp.dma_start(ids[:, :], x.rearrange("b s -> s b"), allow_slow_non_contiguous=True).then_inc(ids_in, 16)
            sp.dma_start(tids[:, :], type_ids.rearrange("b s -> s b"), allow_slow_non_contiguous=True).then_inc(consts_in, 16)
            sp.dma_start(pos[:, :], pos_w).then_inc(consts_in, 16)
            sp.dma_start(ty[:, :, :], type_w.rearrange("(o t) c -> o t c", o=1).to_broadcast([P, 2, C])).then_inc(consts_in, 16)
            for t, v in ((gam, gamma), (bet, beta), (bpr, b_proj)):
                sp.dma_start(t[:, :], v.rearrange("(o c) -> o c", o=1).to_broadcast([P, C])).then_inc(consts_in, 16)
            sp.dma_start(scl[:, :], scale.rearrange("(o c) -> o c", o=1).to_broadcast([P, 1])).then_inc(consts_in, 16)
            sp.dma_start(wn[:, 0:6, :], w_qkv.rearrange("(t p) c -> p t c", p=96)).then_inc(wn_in, 16)
            sp.dma_start(wn[:, 6:8, :], w_proj.rearrange("(t p) c -> p t c", p=96)).then_inc(wn_in, 16)
            sp.dma_start(b1n[:, :, :], b1.rearrange("e (c q) -> (e c) q", q=P).rearrange("(t p) q -> p t q", p=96)).then_inc(wn_in, 16)
            phv = phi.rearrange("d e s -> d (e s)")
            sp.dma_start(phraw[:, 0, :], phv[0:C0, :]).then_inc(phi_in, 16)
            for q in range(2):
                sp.dma_start(half(phraw, q)[:, 1, :], phv[C0:C, :]).then_inc(phi_in, 16)

            def load_weights(e, q):
                sp.dma_start(w1raw[q][:, 0, :], w1[bass.ds(e, 1), 0:C0, :].rearrange("o d h -> d (o h)")).then_inc(w1_in[q], 16)
                for k in range(2):
                    sp.dma_start(half(w1raw[q], k)[:, 1, :], w1[bass.ds(e, 1), C0:C, :].rearrange("o d h -> d (o h)")).then_inc(w1_in[q], 16)
                sp.dma_start(w2raw[q][:, :, :], w2[bass.ds(e, 1), :, :].rearrange("o (c p) d -> p (o c) d", p=P)).then_inc(w2_in[q], 16)

            def load_bias(e, q):
                sp.dma_start(b2row[q][:, :], b2[bass.ds(e, 1), :].to_broadcast([P, C])).then_inc(b2_in[q], 16)

            def load_slots(e, q):
                sp.dma_start(xsm[q][:, 0, :].rearrange("d (g r) -> d g r", g=B // 4),
                             slots_dram[0:C0, :, bass.ds(e, 1), :].rearrange("d g o r -> d g (o r)")).then_inc(slots_in[q], 16)
                for k in range(2):
                    sp.dma_start(half(xsm[q], k)[:, 1, :].rearrange("d (g r) -> d g r", g=B // 4),
                                 slots_dram[C0:C, :, bass.ds(e, 1), :].rearrange("d g o r -> d g (o r)")).then_inc(slots_in[q], 16)

            for q in range(2):
                load_weights(q, q)
                load_bias(q, q)

            sp.sem_inc(stage_free, 2)
            for l in range(4):
                sp.sem_inc(comb_out[l], 16)
            with sp.Fori(0, B // 8) as i:
                for r in range(8):
                    l, part = r % 2, r // 4
                    sp.wait_ge(r_combineT, seq(i, r))
                    sp.sem_inc(waited, 1)
                    sp.dma_start(comb_dram[:, :, bass.ds(8 * i + r, 1), :].rearrange("g p o l -> p g (o l)"),
                                 cwT[l][:, r // 2 % 2, :, :]).then_inc(comb_out[r % 4], 16)
                    if r % 4 == 3:
                        sp.wait_ge(r_slots_main, seq(i, r))
                        sp.wait_ge(r_slots_rest, seq(i, r))
                        sp.sem_inc(waited, 1)
                        for chans, staged in ((slice(0, C0), slm[part]), (slice(C0, C), slr[part])):
                            sp.dma_start(slots_dram[chans, bass.ds(2 * i + part, 1), :, :].rearrange("d o e r -> d (o e r)"),
                                         staged[:, :, :, :].rearrange("d e b s -> d (e b s)")).then_inc(slots_out, 16)
                        sp.wait_ge(slots_out, 32 * (2 * i + part + 1))
                        sp.sem_inc(stage_free, 1)
            sp.wait_ge(slots_out, 32 * (B // 4))
            for l in range(4):
                sp.wait_ge(comb_out[l], 16 * (B // 4) + 16)
            for q in range(2):
                load_slots(q, q)

            def prefetch(e, q):
                sp.wait_ge(c_high_halves, 5 * e + 5)
                sp.sem_inc(waited, 1)
                sp.wait_ge(c_w1_low, 2 * e + 2)
                sp.sem_inc(waited, 1)
                sp.wait_ge(c_slots_low, e + 1)
                sp.sem_inc(waited, 1)
                load_slots(e + 2, q)
                sp.wait_ge(c_w2_low, e + 1)
                sp.sem_inc(waited, 1)
                load_weights(e + 2, q)

            prefetch(0, 0)

            def group(gr, last, par):
                for j in range(GE):
                    e, q = gr * GE + j, j % 2
                    if not (last and j >= 1):
                        prefetch(gr * GE + (j + 1), (j + 1) % 2)
                    if j == 0:
                        if not (isinstance(gr, int) and gr == 0):
                            sp.wait_ge(c_combined, (gr - 1) * (B // 2) + 2)
                        sp.sem_inc(waited, 1)
                        sp.dma_start(cwg[par][:, :, :], comb_dram[bass.ds(gr, 1), :, :, :].rearrange("o p b l -> p (o b) l")).then_inc(comb_in, 16)
                    sp.wait_ge(c_output, 4 * (e + 1))
                    for k in range(4):
                        sp.dma_start(eog[par][SL * j:SL * j + SL, :, :].rearrange("p (t k) d -> p t k d", k=4)[:, :, k, :],
                                     eo[q][SL * k:SL * k + SL, :, :]).then_inc(eog_in[q], 16)
                    if not (last and j >= 2):
                        sp.sem_inc(waited, 1)
                        load_bias(e + 2, q)

            group(0, False, 0)
            with sp.Fori(0, NG // 2 - 1) as i:
                for k in range(2):
                    group(2 * i + (k + 1), False, (k + 1) % 2)
            group(NG - 1, True, (NG - 1) % 2)
            for r in range(0, B, 4):
                sp.wait_ge(c_combined, (NG - 1) * (B // 2) + (r + 4) // 2 + 2)
                sp.dma_start(out[r:r + 4].rearrange("b s c -> s b c"), h[:, r:r + 4, :]).then_inc(y_out, 16)
            sp.wait_ge(y_out, 16 * (B // 4))

        @block.gpsimd
        def _(pool):
            pool.memset(ident[:, 0:P], 0.0).then_inc(masks_ready, 1)
            pool.memset(mask8[:, :, :], 0.5).then_inc(masks_ready, 1)
            pool.memset(ones[:, :], 1.0).then_inc(memsets_done, 1)
            pool.memset(ident[:, P:P + 1], 1.0).then_inc(memsets_done, 1)
            pool.memset(expo[:, :], -0.5).then_inc(memsets_done, 1)
            pool.wait_ge(masks_ready, 2)
            pool.affine_select(out=ident[:, 0:P], in_=ident[:, 0:P], compare_op=ALU.not_equal, fill=1.0, base=0,
                               pattern=[[-1, P]], channel_multiplier=1).then_inc(identity_ready, 1)
            pool.affine_select(out=mask8[:, :, :], in_=mask8[:, :, :], compare_op=ALU.is_ge, fill=0.0, base=0,
                               pattern=[[-D, GH], [0, M]], channel_multiplier=1).then_inc(masks_ready, 1)
            pool.wait_ge(masks_ready, 3)
            pool.affine_select(out=mask8[:, :, :], in_=mask8[:, :, :], compare_op=ALU.is_ge, fill=0.0, base=D - 1,
                               pattern=[[D, GH], [0, M]], channel_multiplier=-1).then_inc(masks_ready, 1)
            pool.wait_ge(ids_in, 16)
            for b in range(B):
                pool.indirect_dma_start(h[:, b, :], None, tok_w, bass.IndirectOffsetOnAxis(ap=ids[:, b:b + 1], axis=0)).then_inc(first_tokens_in if b < 2 else tokens_in, 16)
            for l in range(2):
                for t in (k2[l], gbd[l], ybd[l]):
                    pool.memset(t[:, :, :], 0.0).then_inc(memsets_done, 1)
                for t in (g[l], tt[l]):
                    pool.memset(t[:, :, :], 0.0).then_inc(memsets_done, 1)
                pool.memset(wbd[l][:, :, :], 0.0).then_inc(memsets_done, 1)
                pool.memset(v33[l][:, :, 2 * D:SW], 1.0).then_inc(memsets_done, 1)
            for l in range(2):
                for q in range(2):
                    pool.wait_ge(memsets_done, 17 + 2 * l + q)
                    pool.memset(half(wbd[l], q)[:, :, 2 * D + q:2 * D + q + 1], 1.0).then_inc(memsets_done, 1)

            pool.wait_ge(memsets_done, 21)

            def norm_pow(l, i, count):
                pool.wait_ge(a_row_var_eps, count(l, i))
                pool.tensor_tensor(rs[l][:, :], ve[l][:, :], expo[:, :], ALU.pow).then_inc(a_row_rstd, 1)

            def landmarks(l, i):
                pool.wait_ge(a_keys, now(l, i))
                pool.tensor_tensor(kl[l][:, :, :], kk[l][:, :, 0:P:2], kk[l][:, :, 1:P:2], ALU.add).then_inc(a_key_pairs_summed, 1)
                pool.wait_ge(a_key_pairs_summed, now(l, i))
                pool.sem_inc(waited, 1)
                pool.tensor_scalar(kk[l][:, :, P:P + M], kl[l][:, :, :], 0.5, 0.0, ALU.mult, ALU.add).then_inc(a_key_landmarks, 1)
                pool.tensor_tensor(kbd[l][:, 0:GH, :], bc(kl[l][:, 0:1, :], [P, GH, M]), mask8[:, :, :], ALU.mult)
                pool.tensor_tensor(kbd[l][:, GH:H, :], bc(kl[l][:, 1:2, :], [P, H - GH, M]), mask8[:, 0:H - GH, :], ALU.mult).then_inc(a_key_landmarks_bd, 1)

            def phase(a, i, do_tail, do_front, do_norm):
                b, i_tail, i_front = other(a, i)
                if do_front:
                    landmarks(b, i_front)
                if do_norm:
                    norm_pow(a, i + 1, first)
                    norm_pow(a, i + 1, second)

            def start():
                norm_pow(0, 0, first)
                norm_pow(0, 0, second)
                landmarks(0, 0)
                norm_pow(1, 0, first)
                norm_pow(1, 0, second)

            attention_schedule(pool, phase, start, lambda: None)

            def norm_pow(i, r):
                l = r % 2
                pool.wait_ge(r_row_var_eps, seq(i, r))
                pool.tensor_tensor(rrs[l][:, :], rve[l][:, :], expo[:, :], ALU.pow).then_inc(r_row_rstd, 1)

            def length_pow(i, r):
                l = r % 2
                pool.wait_ge(r_row_squares, seq(i, r))
                pool.sem_inc(waited, 1)
                pool.tensor_scalar(rsm[l][:, :], rss[l][:, :], NORM_EPS2, 0.0, ALU.max, ALU.add).then_inc(r_squares_guarded, 1)
                pool.wait_ge(r_squares_guarded, seq(i, r))
                pool.tensor_tensor(rrn[l][:, :], rsm[l][:, :], expo[:, :], ALU.pow).then_inc(r_inv_length, 1)

            def rows_low(i, r):
                l = r % 2
                pool.wait_ge(r_rows_high, seq(i, r))
                pool.tensor_tensor(xe_lo[l][:, :], xe[l][:, :], xe_hi[l][:, :].bitcast(F32), ALU.subtract).then_inc(r_rows_low, 1)

            def combine_weights(i, r):
                l = r % 2
                pool.wait_ge(r_combine_factor, seq(i, r))
                pool.wait_ge(r_dispatch_low, seq(i, r))
                pool.tensor_tensor(dw[l][:, :, :], lg[l][:, :, :], bc(fz[l][:, :].rearrange("p (e o) -> p e o", o=1), [P, E, SL]), ALU.mult).then_inc(r_combine, 1)

            def start(i):
                for r in range(2):
                    norm_pow(i, r)
                    length_pow(i, r)

            def phase(i, r):
                if r > 0:
                    combine_weights(i, r - 1)
                rows_low(i, r)
                if r + 2 < 8:
                    norm_pow(i, r + 2)
                    length_pow(i, r + 2)

            def end(i):
                combine_weights(i, 7)

            routing_schedule(pool, phase, start, end)

            def hi(e, m, q):
                if not (isinstance(e, int) and e < 2):
                    pool.wait_ge(c_hidden_psum, HC * (e - 1))
                pool.wait_ge(w1_in[q], 48 * (m + 1))
                pool.sem_inc(waited, 1)
                pool.tensor_scalar(w1_hi[q][:, :], w1raw[q][:, 0, :], 1.0, 0.0, ALU.mult, ALU.add).then_inc(c_high_halves, 1)
                pool.tensor_scalar(w1_st[q][:, :], w1raw[q][:, 1, :], 1.0, 0.0, ALU.mult, ALU.add).then_inc(c_high_halves, 1)
                pool.wait_ge(slots_in[q], 48 * (m + 1))
                pool.sem_inc(waited, 1)
                pool.tensor_scalar(xs_hi[q][:, 0, :], xsm[q][:, 0, :], 1.0, 0.0, ALU.mult, ALU.add).then_inc(c_high_halves, 1)
                pool.tensor_scalar(xs_hi[q][:, 1, :], xsm[q][:, 1, :], 1.0, 0.0, ALU.mult, ALU.add).then_inc(c_high_halves, 1)
                if not (isinstance(e, int) and e < 2):
                    pool.wait_ge(c_output_psum, OC * (e - 1))
                pool.wait_ge(w2_in[q], 16 * (m + 1))
                pool.sem_inc(waited, 1)
                pool.tensor_scalar(w2_hl[q][:, :, 0:C], w2raw[q][:, :, :], 1.0, 0.0, ALU.mult, ALU.add).then_inc(c_high_halves, 1)

            pool.wait_ge(slots_out, 32 * (B // 4))
            for l in range(4):
                pool.wait_ge(comb_out[l], 16 * (B // 4) + 16)
            hi(0, 0, 0)

            def group(gr, last, par):
                for j in range(GE):
                    if not (last and j == GE - 1):
                        hi(gr * GE + (j + 1), gr * 2 + (j + 1) // 2, (j + 1) % 2)

            group(0, False, 0)
            with pool.Fori(0, NG // 2 - 1) as i:
                for k in range(2):
                    group(2 * i + (k + 1), False, (k + 1) % 2)
            group(NG - 1, True, (NG - 1) % 2)

        @block.scalar
        def _(act):
            act.wait_ge(phi_in, 48)
            act.activation(phn[:, :], phraw[:, 0, :], ACT.Square).then_inc(phi_squared, 1)
            act.activation(pht[0:64, :], phraw[0:64, 1, :], ACT.Square).then_inc(phi_squared, 1)
            act.wait_ge(phi_sums_guarded, 1)
            act.activation(pht[:, :], phn[:, :], ACT.Sqrt).then_inc(phi_rooted, 1)

            def copy_xT(l, i):
                act.wait_ge(a_rowsT_psum, now(l, i))
                act.activation(xT[l][:, 0, :], bank[l][0][:, 0:P], ACT.Copy)
                act.activation(xT[l][0:64, 1, :], bank[l][0][0:64, P:2 * P], ACT.Copy).then_inc(a_rowsT, 1)

            def copy_qk(l, i):
                act.wait_ge(a_qk_psum, now(l, i))
                act.activation(qT[l][:, :, :], bank[l][1][:, 0:2 * P].rearrange("p (a n) -> p a n", a=2), ACT.Copy, scale=D ** -0.5).then_inc(a_queries, 1)
                act.activation(kk[l][:, :, 0:P], bank[l][1][:, 2 * P:4 * P].rearrange("p (a n) -> p a n", a=2), ACT.Copy).then_inc(a_keys, 1)

            def copy_v(l, i):
                act.wait_ge(a_v_psum, now(l, i))
                act.activation(v33[l][:, :, 0:2 * D], bank[l][2][:, 0:C].rearrange("p (a n) -> p a n", a=NP), ACT.Copy).then_inc(a_values, 1)

            def exp2(l, i):
                act.wait_ge(a_diff2, now(l, i))
                act.activation(e2[l][:, :, :], e2[l][:, :, :], ACT.Exp).then_inc(a_exp2, 1)

            def exp3(l, i):
                act.wait_ge(a_diff3, now(l, i))
                act.activation(e3[l][:, :, :], e3[l][:, :, :], ACT.Exp).then_inc(a_exp3, 1)

            def exp1(l, i):
                act.wait_ge(a_diff1, second(l, i))
                act.activation(e1[l][:, :, :], e1[l][:, :, :], ACT.Exp).then_inc(a_exp1, 1)

            def copy_k3T(l, i):
                act.wait_ge(a_kernel3T_psum, now(l, i))
                act.activation(k3T[l][:, 0:4, :], bank[l][2].rearrange("p (a n) -> p a n", a=4), ACT.Copy)
                act.activation(k3T[l][:, 4:6, :], bank[l][3][:, 0:2 * P].rearrange("p (a n) -> p a n", a=2), ACT.Copy).then_inc(a_kernel3T, 1)

            def copy_k2T(l, i):
                act.wait_ge(a_kernel2T_psum, now(l, i))
                act.activation(k2T[l][:, :, :].rearrange("p (a q) n -> p a q n", a=2),
                               ps[:, 4 * l:4 * l + 2, 0:3 * (P + 1)].rearrange("p a (q n) -> p a q n", q=3), ACT.Copy).then_inc(a_kernel2T, 1)

            def copy_k1T(l, i):
                act.wait_ge(a_kernel1T_psum, now(l, i))
                act.activation(k1T[l][:, 0:4, :], bank[l][2].rearrange("p (a n) -> p a n", a=4), ACT.Copy)
                act.activation(k1T[l][:, 4:6, :], bank[l][3][:, 0:2 * P].rearrange("p (a n) -> p a n", a=2), ACT.Copy).then_inc(a_kernel1T, 1)

            def copy_svT(l, i):
                act.wait_ge(a_attendedT_psum, now(l, i))
                act.activation(svT[l][:, 0, :], bank[l][3][:, 0:P], ACT.Copy)
                act.activation(svT[l][0:64, 1, :], bank[l][3][0:64, P:2 * P], ACT.Copy).then_inc(a_attendedT, 1)

            def state_bd(l, i, k, c):
                if k == 0:
                    act.wait_ge(a_state_X0, 2 * now(l, i))
                else:
                    act.wait_ge(a_state, step(l, i, k - 1, c))
                for q in range(2):
                    act.activation(half(gbd[l], q)[:, pairs(c), M * q:M * q + M], half(g[l], q)[:, pairs(c), 0:M], ACT.Copy).then_inc(a_state_bd, 1)

            def square_bd(l, i, k, c):
                act.wait_ge(a_square_psum, step(l, i, k, c))
                for q in range(2):
                    act.activation(half(ybd[l], q)[:, pairs(c), M * q:M * q + M], half(pA(l, c), q)[:, :, 0:M],
                                   ACT.Copy, scale=1.0 / 256).then_inc(a_square_bd, 1)

            def phase(a, i, do_tail, do_front, do_norm):
                b, i_tail, i_front = other(a, i)
                if not do_tail:
                    state_bd(a, i, 0, 0)
                    state_bd(a, i, 0, 1)
                for c in range(2):
                    square_bd(a, i, 0, c)
                if do_front:
                    copy_qk(b, i_front)
                for c in range(2):
                    state_bd(a, i, 1, c)
                for c in range(2):
                    square_bd(a, i, 1, c)
                if do_tail:
                    copy_svT(b, i_tail)
                if do_front:
                    copy_v(b, i_front)
                for c in range(2):
                    state_bd(a, i, 2, c)
                for c in range(2):
                    square_bd(a, i, 2, c)
                for c in range(2):
                    state_bd(a, i, 3, c)
                for c in range(2):
                    square_bd(a, i, 3, c)
                if do_front:
                    exp2(b, i_front)
                for c in range(2):
                    state_bd(a, i, 4, c)
                for c in range(2):
                    square_bd(a, i, 4, c)
                if do_front:
                    exp3(b, i_front)
                    copy_k3T(b, i_front)
                for c in range(2):
                    state_bd(a, i, 5, c)
                for c in range(2):
                    square_bd(a, i, 5, c)
                if do_front:
                    exp1(b, i_front)
                    copy_k2T(b, i_front)
                    state_bd(b, i_front, 0, 0)
                    state_bd(b, i_front, 0, 1)
                if do_norm:
                    copy_xT(a, i + 1)
                copy_k1T(a, i)

            def start():
                copy_xT(0, 0)
                copy_qk(0, 0)
                copy_v(0, 0)
                exp2(0, 0)
                exp3(0, 0)
                exp1(0, 0)
                copy_k3T(0, 0)
                copy_k2T(0, 0)
                copy_xT(1, 0)

            def end():
                copy_svT(1, B // 2 - 1)

            attention_schedule(act, phase, start, end)

            def squares(i, r):
                l = r % 2
                act.wait_ge(r_rows_normed, seq(i, r))
                act.activation(rsq[l][:, :], rx[l][:, :], ACT.Square, accum_out=rss[l][:, :]).then_inc(r_row_squares, 1)

            def transposed_high(i, r):
                l = r % 2
                act.wait_ge(r_rowsT_psum, seq(i, r))
                act.activation(xt_hi[l][:, :, :], bank[l][0][:, 0:2 * P].rearrange("p (a n) -> p a n", a=2), ACT.Copy).then_inc(r_rowsT_high, 1)

            def rows_high(i, r):
                l = r % 2
                act.wait_ge(r_unit_rows, 2 * seq(i, r))
                act.activation(xe_hi[l][:, :], xe[l][:, :], ACT.Copy).then_inc(r_rows_high, 1)

            def exp_maxima(i, r):
                l = r % 2
                act.wait_ge(r_row_max, seq(i, r))
                act.activation(fe[l][:, :], mx[l][:, :], ACT.Exp, bias=nm[l][:, :]).then_inc(r_exp_max, 1)

            def exp_logits(i, r):
                l = r % 2
                act.wait_ge(r_diffs, seq(i, r))
                act.activation(lg[l][:, :, :], lg[l][:, :, :], ACT.Exp).then_inc(r_exps, 1)

            def dispatch_high(i, r):
                l = r % 2
                act.wait_ge(r_dispatch, seq(i, r))
                act.activation(dw_hi[l][:, :], dw[l][:, :, :].rearrange("p e s -> p (e s)"), ACT.Copy).then_inc(r_dispatch_high, 1)

            def stage_rest(i, r):
                l = r % 2
                act.wait_ge(r_slots_rest_psum, seq(i, r))
                act.activation(slr[r // 4][:, :, r % 4, :], ps[0:64, 4 * l + 2:4 * l + 4, :].rearrange("p a (e s) -> p (a e) s", s=SL), ACT.Copy).then_inc(r_slots_rest, 1)

            def stage_main(i, r):
                l = r % 2
                act.wait_ge(r_slots_main_psum, seq(i, r))
                if r % 4 == 0:
                    act.wait_ge(stage_free, 2 * i + (r // 4 + 1))
                act.activation(slm[r // 4][:, :, r % 4, :], ps[:, 4 * l + 2:4 * l + 4, :].rearrange("p a (e s) -> p (a e) s", s=SL), ACT.Copy).then_inc(r_slots_main, 1)

            def stage_weights(i, r):
                l = r % 2
                act.wait_ge(r_combineT_psum, seq(i, r))
                act.wait_ge(comb_out[r % 4], 16 * (2 * i + (r // 4 + 1)))
                act.activation(cwT[l][:, r // 2 % 2, :, :], ps[:, 4 * l + 2:4 * l + 4, :].rearrange("p a (g n) -> p (a g) n", n=P), ACT.Copy).then_inc(r_combineT, 1)

            def start(i):
                for r in range(2):
                    squares(i, r)
                transposed_high(i, 0)

            def phase(i, r):
                if r + 1 < 8:
                    transposed_high(i, r + 1)
                rows_high(i, r)
                exp_maxima(i, r)
                exp_logits(i, r)
                if r > 1:
                    stage_weights(i, r - 2)
                if r > 0:
                    stage_main(i, r - 1)
                if r + 2 < 8:
                    squares(i, r + 2)
                dispatch_high(i, r)
                if r > 0:
                    stage_rest(i, r - 1)

            def end(i):
                stage_weights(i, 6)
                stage_main(i, 7)
                stage_rest(i, 7)
                stage_weights(i, 7)

            routing_schedule(act, phase, start, end)

            def group(gr, last, par):
                first = isinstance(gr, int) and gr == 0
                for t in range(GE * HC):
                    n = gr * (GE * HC) + t
                    if not (first and t < 2):
                        act.wait_ge(c_hidden_low, n - 1)
                    act.wait_ge(c_hidden_psum, n + 1)
                    act.activation(hraw[t % 2][:, :], ps[:, t % 2, :], ACT.Gelu, bias=b1T[:, bass.ds(n, 1)]).then_inc(c_gelu, 1)
                    if not (first and t < 3):
                        act.wait_ge(c_output_psum, OC * (gr * GE) + outputs_done(t - 3))
                    act.wait_ge(c_gelu, n + 1)
                    act.activation(h_hi[t % 3][:, :], hraw[t % 2][:, :], ACT.Copy).then_inc(c_hidden_high, 1)

            act.wait_ge(slots_out, 32 * (B // 4))
            for l in range(4):
                act.wait_ge(comb_out[l], 16 * (B // 4) + 16)
            group(0, False, 0)
            with act.Fori(0, NG // 2 - 1) as i:
                for k in range(2):
                    group(2 * i + (k + 1), False, (k + 1) % 2)
            group(NG - 1, True, (NG - 1) % 2)

        @block.vector
        def _(dve):
            dve.wait_ge(consts_in, 16 * 7)
            dve.tensor_copy(tidf[:, :], tids[:, :]).then_inc(type_rows_ready, 1)
            dve.tensor_tensor(pos[:, :], pos[:, :], ty[:, 0, :], ALU.add).then_inc(type_rows_ready, 1)
            dve.tensor_tensor(ty[:, 1, :], ty[:, 1, :], ty[:, 0, :], ALU.subtract).then_inc(type_rows_ready, 1)
            dve.memset(wT[:, :, C:256], 0.0)
            dve.memset(wT[:, :, 256 + C:512], 0.0)
            dve.wait_ge(weights_transposed, 1)
            for k in range(2):
                rows = P if k == 0 else 64
                dve.tensor_copy(wT[0:rows, k, 0:512].rearrange("p (a n) -> p a n", a=2)[:, :, 0:C],
                                bank[0][2 * k][0:rows, 0:384].rearrange("p (a n) -> p a n", a=2)).then_inc(weights_ready, 1)
                dve.tensor_copy(wT[0:rows, k, 512:704], bank[0][2 * k + 1][0:rows, 0:C]).then_inc(weights_ready, 1)
                dve.tensor_copy(pT[0:rows, k, :], bank[0][2 * k + 1][0:rows, C:2 * C]).then_inc(weights_ready, 1)
            dve.wait_ge(weights_transposed, 2)
            dve.tensor_copy(b1T[:, :], bank[1][0][:, 0:E * HC]).then_inc(b1_ready, 1)
            dve.wait_ge(phi_summed, 1)
            dve.tensor_scalar(phn[:, :], ps[:, 5:7, :].rearrange("p a n -> p (a n)"), NORM_EPS2, 0.0, ALU.max, ALU.add).then_inc(phi_sums_guarded, 1)
            dve.wait_ge(first_tokens_in, 32)
            dve.wait_ge(type_rows_ready, 3)
            dve.wait_ge(masks_ready, 4)
            dve.wait_ge(memsets_done, 21)

            def col(ap):
                return ap.rearrange("p (a o) -> p a o", o=1)

            def hrow(l, i):
                return h[:, bass.ds(2 * i + l, 1), :].rearrange("p o c -> p (o c)")

            def embed_sum(l, i):
                dve.tensor_tensor(xn[l][:, :], hrow(l, i), pos[:, :], ALU.add).then_inc(a_tokens_placed, 1)

            def embed_stat(l, i):
                dve.wait_ge(a_tokens_placed, now(l, i))
                dve.scalar_tensor_tensor(hb[l][:, :], ty[:, 1, :], tidf[:, bass.ds(2 * i + l, 1)], xn[l][:, :], ALU.mult, ALU.add).then_inc(a_embedded, 1)
                dve.wait_ge(a_embedded, now(l, i))
                dve.sem_inc(waited, 1)
                dve.bn_stats(st6[l][:, :], hb[l][:, :]).then_inc(a_row_stats, 1)

            def embed_var(l, i):
                dve.wait_ge(a_row_stats, first(l, i))
                dve.sem_inc(waited, 1)
                dve.bn_aggr(mv[l][:, :], st6[l][:, :]).then_inc(a_row_mean_var, 1)
                dve.wait_ge(a_row_mean_var, first(l, i))
                dve.tensor_scalar(ve[l][:, :], mv[l][:, 1:2], LN_EPS, 0.0, ALU.add, ALU.add).then_inc(a_row_var_eps, 1)
                dve.scalar_tensor_tensor(xn[l][:, :], hb[l][:, :], mv[l][:, 0:1], gam[:, :], ALU.subtract, ALU.mult).then_inc(a_embedded_gamma, 1)

            def embed_norm(l, i):
                dve.wait_ge(a_row_rstd, first(l, i))
                dve.wait_ge(a_embedded_gamma, now(l, i))
                dve.scalar_tensor_tensor(hrow(l, i), xn[l][:, :], rs[l][:, :], bet[:, :], ALU.mult, ALU.add).then_inc(a_embedding_normed, 1)
                dve.wait_ge(a_embedding_normed, now(l, i))
                dve.sem_inc(waited, 1)
                dve.bn_stats(st6[l][:, :], hrow(l, i)).then_inc(a_row_stats, 1)

            def attention_var(l, i):
                dve.wait_ge(a_row_stats, second(l, i))
                dve.sem_inc(waited, 1)
                dve.bn_aggr(mv[l][:, :], st6[l][:, :]).then_inc(a_row_mean_var, 1)
                dve.wait_ge(a_row_mean_var, second(l, i))
                dve.tensor_scalar(ve[l][:, :], mv[l][:, 1:2], LN_EPS, 0.0, ALU.add, ALU.add).then_inc(a_row_var_eps, 1)

            def attention_norm(l, i):
                dve.wait_ge(a_row_rstd, second(l, i))
                dve.tensor_scalar(xn[l][:, :], hrow(l, i), mv[l][:, 0:1], rs[l][:, :], ALU.subtract, ALU.mult).then_inc(a_rows_normed, 1)

            def landmarks(l, i):
                dve.wait_ge(a_queries, now(l, i))
                dve.tensor_tensor(ql[l][:, :, :], qT[l][:, :, 0:P:2], qT[l][:, :, 1:P:2], ALU.add).then_inc(a_query_landmarks, 1)
                dve.wait_ge(a_query_landmarks, now(l, i))
                dve.tensor_tensor(qbd[l][:, 0:GH, :], bc(ql[l][:, 0:1, :], [P, GH, M]), mask8[:, :, :], ALU.mult)
                dve.tensor_tensor(qbd[l][:, GH:H, :], bc(ql[l][:, 1:2, :], [P, H - GH, M]), mask8[:, 0:H - GH, :], ALU.mult).then_inc(a_query_landmarks_bd, 1)

            def s32(l):
                return ps[:, 4 * l + 1:4 * l + 4, 0:2 * (P + M)].rearrange("p a (q c) -> p a q c", q=2)

            def maxima32(l, i):
                dve.wait_ge(a_scores32_psum, now(l, i))
                dve.tensor_reduce(m2[l][:, :], s32(l)[:, :, :, P:P + M], AX.X, ALU.max).then_inc(a_max2, 1)
                dve.tensor_reduce(m3[l][:, :], s32(l)[:, :, :, 0:P], AX.X, ALU.max).then_inc(a_max3, 1)

            def differences2(l, i):
                dve.wait_ge(a_max2, now(l, i))
                dve.tensor_tensor(e2[l][:, :, :].rearrange("p (a q) c -> p a q c", q=2), s32(l)[:, :, :, P:P + M],
                                  bc(m2[l][:, :].rearrange("p (a q o) -> p a q o", q=2, o=1), [P, 3, 2, M]), ALU.subtract).then_inc(a_diff2, 1)

            def differences3(l, i):
                dve.wait_ge(a_max3, now(l, i))
                dve.tensor_tensor(e3[l][:, :, :].rearrange("p (a q) c -> p a q c", q=2), s32(l)[:, :, :, 0:P],
                                  bc(m3[l][:, :].rearrange("p (a q o) -> p a q o", q=2, o=1), [P, 3, 2, P]), ALU.subtract).then_inc(a_diff3, 1)

            def kernel2_sums(l, i):
                dve.wait_ge(a_exp2, now(l, i))
                dve.tensor_reduce(s2[l][:, :], e2[l][:, :, :], AX.X, ALU.add).then_inc(a_sums2, 1)
                dve.wait_ge(a_sums2, now(l, i))
                dve.reciprocal(r2[l][:, :], s2[l][:, :]).then_inc(a_inv_sums2, 1)

            def kernel2(l, i):
                dve.wait_ge(a_inv_sums2, now(l, i))
                for q in range(2):
                    dve.tensor_tensor(half(k2[l], q)[:, :, M * q:M * q + M], half(e2[l], q)[:, :, :],
                                      bc(col(half(r2[l], q)[:, :]), [64, NP, M]), ALU.mult).then_inc(a_kernel2_bd, 1)

            def s1(l, k, n):
                return bank[l][k][:, 0:n * M].rearrange("p (a n) -> p a n", a=n)

            def maxima1_a(l, i):
                dve.wait_ge(a_scores1_psum, first(l, i))
                dve.tensor_reduce(m1[l][:, 0:GH], s1(l, 0, GH), AX.X, ALU.max).then_inc(a_max1, 1)

            def differences1_a(l, i):
                dve.wait_ge(a_max1, first(l, i))
                dve.tensor_tensor(e1[l][:, 0:GH, :], s1(l, 0, GH), bc(col(m1[l][:, 0:GH]), [P, GH, M]), ALU.subtract).then_inc(a_diff1, 1)

            def kernel1_b(l, i):
                dve.wait_ge(a_scores1_psum, second(l, i))
                dve.tensor_reduce(m1[l][:, GH:H], s1(l, 1, H - GH), AX.X, ALU.max).then_inc(a_max1, 1)
                dve.wait_ge(a_max1, second(l, i))
                dve.tensor_tensor(e1[l][:, GH:H, :], s1(l, 1, H - GH), bc(col(m1[l][:, GH:H]), [P, H - GH, M]), ALU.subtract).then_inc(a_diff1, 1)

            def scale_sum(l, i):
                dve.wait_ge(a_column_sums_psum, now(l, i))
                dve.tensor_reduce(csm[l][:, :], bank[l][0][0:NP, 0:P].rearrange("p (a n) -> p a n", a=2), AX.X, ALU.max).then_inc(a_scale_max, 1)
                dve.wait_ge(a_scale_max, now(l, i))
                dve.reciprocal(csr[l][:, :], csm[l][:, :]).then_inc(a_scale_inverted, 1)
                dve.wait_ge(a_scale_inverted, now(l, i))
                dve.tensor_copy(csb[l][:, :, :], bc(col(csr[l][:, :]), [NP, 2, M])).then_inc(a_scale_rows, 1)

            def scale_spread(l, i):
                dve.wait_ge(a_scale_psum, now(l, i))
                dve.tensor_scalar(r4[l][:, :], bank[l][0][:, 0:NP], 4.0, None, ALU.mult)
                dve.tensor_scalar(r25[l][:, :], bank[l][0][:, 0:NP], 0.25, None, ALU.mult).then_inc(a_scale_spread, 1)

            def state_w(l, i):
                dve.wait_ge(a_kernel3_v_psum, now(l, i))
                dve.reciprocal(u4[l][:, :], bank[l][3][:, 0:NP * SW].rearrange("p (a n) -> p a n", a=NP)[:, :, 32]).then_inc(a_inv_sums3, 1)
                dve.wait_ge(a_inv_sums3, now(l, i))
                for q in range(2):
                    dve.scalar_tensor_tensor(half(g[l], q)[:, :, M:SW],
                                             half(bank[l][3], q)[:, 0:NP * SW].rearrange("p (a n) -> p a n", a=NP)[:, :, D * q:D * q + D],
                                             4.0, bc(col(half(u4[l], q)[:, :]), [64, NP, D]), ALU.mult, ALU.mult).then_inc(a_state_w0, 1)

            def state_X(l, i):
                dve.wait_ge(a_kernel2_square_psum, now(l, i))
                dve.wait_ge(a_scale_spread, now(l, i))
                for q in range(2):
                    dve.tensor_tensor(half(g[l], q)[:, 0:4, 0:M], half(bank[l][1], q).rearrange("p (a n) -> p a n", a=4)[:, :, M * q:M * q + M],
                                      bc(col(half(r4[l], q)[:, 0:4]), [64, 4, M]), ALU.mult)
                    dve.tensor_tensor(half(g[l], q)[:, 4:6, 0:M], half(bank[l][2], q)[:, 0:2 * P].rearrange("p (a n) -> p a n", a=2)[:, :, M * q:M * q + M],
                                      bc(col(half(r4[l], q)[:, 4:6]), [64, 2, M]), ALU.mult).then_inc(a_state_X0, 1)

            def state_T(l, i, k, c):
                dve.wait_ge(a_square_bd, 2 * step(l, i, k, c))
                if k == 0:
                    dve.wait_ge(a_state_X0, 2 * now(l, i))
                    dve.wait_ge(a_state_w0, 2 * now(l, i))
                else:
                    dve.wait_ge(a_state, step(l, i, k - 1, c))
                dve.scalar_tensor_tensor(tt[l][:, pairs(c), 0:SW], g[l][:, pairs(c), 0:SW], 28.0, pA(l, c)[:, :, 0:SW], ALU.mult, ALU.subtract).then_inc(a_T, 1)

            def state_carry(l, i, k, c):
                dve.wait_ge(a_square_bd, 2 * step(l, i, k, c))
                dve.scalar_tensor_tensor(wf[l][:, pairs(c), :], g[l][:, pairs(c), 0:SW], 52.0 / 15, pA(l, c)[:, :, 0:SW], ALU.mult, ALU.subtract).then_inc(a_state_carry, 1)

            def state_next(l, i, k, c):
                dve.wait_ge(a_YT_psum, step(l, i, k, c))
                dve.wait_ge(a_state_carry, step(l, i, k, c))
                dve.scalar_tensor_tensor(g[l][:, pairs(c), 0:SW], wf[l][:, pairs(c), :], 15.0 / 16, pZ(l, c)[:, :, 0:SW], ALU.mult, ALU.add).then_inc(a_state, 1)

            def inverse_kv(l, i):
                dve.wait_ge(a_inverse_kv_psum, now(l, i))
                for q in range(2):
                    dve.tensor_tensor(half(wbd[l], q)[:, :, D * q:D * q + D], half(bank[l][1], q)[:, 0:NP * SW].rearrange("p (a n) -> p a n", a=NP)[:, :, M:SW],
                                      bc(col(half(r25[l], q)[:, :]), [64, NP, D]), ALU.mult).then_inc(a_inverse_kv_bd, 1)

            def po(l):
                return bank[l][3][:, 0:NP * SW].rearrange("p (a n) -> p a n", a=NP)

            def attended(l, i):
                dve.wait_ge(a_attended_psum, now(l, i))
                dve.reciprocal(ro[l][:, :, :], po(l)[:, :, 32:34]).then_inc(a_inv_sums1, 1)
                dve.wait_ge(a_inv_sums1, now(l, i))
                dve.tensor_tensor(sv[l][:, :].rearrange("p (a q d) -> p a q d", q=2, d=D),
                                  po(l)[:, :, 0:32].rearrange("p a (q d) -> p a q d", q=2),
                                  bc(ro[l][:, :, :].rearrange("p a (q o) -> p a q o", o=1), [P, NP, 2, D]), ALU.mult).then_inc(a_attended, 1)

            def residual_bias(l, i):
                dve.tensor_tensor(res[l][:, :], hrow(l, i), bpr[:, :], ALU.add).then_inc(a_residual_bias, 1)

            def residual_v(l, i):
                dve.wait_ge(a_residual_bias, now(l, i))
                dve.tensor_tensor(res[l][:, :].rearrange("p (a n) -> p a n", a=NP), res[l][:, :].rearrange("p (a n) -> p a n", a=NP),
                                  v33[l][:, :, 0:2 * D], ALU.add).then_inc(a_residual_v, 1)

            def residual_sum(l, i):
                dve.wait_ge(a_projected_psum, now(l, i))
                dve.wait_ge(a_residual_v, now(l, i))
                dve.tensor_tensor(hrow(l, i), res[l][:, :], bank[l][3][:, 0:C], ALU.add).then_inc(a_attention_done, 1)

            def phase(a, i, do_tail, do_front, do_norm):
                b, i_tail, i_front = other(a, i)
                for c in range(2):
                    state_T(a, i, 0, c)
                    state_carry(a, i, 0, c)
                residual_bias(a, i)
                if do_norm:
                    embed_sum(a, i + 1)
                for c in range(2):
                    state_next(a, i, 0, c)
                if do_front:
                    landmarks(b, i_front)
                if do_tail:
                    attended(b, i_tail)
                if do_norm:
                    embed_stat(a, i + 1)
                for c in range(2):
                    state_T(a, i, 1, c)
                    state_carry(a, i, 1, c)
                for c in range(2):
                    state_next(a, i, 1, c)
                if do_norm:
                    embed_var(a, i + 1)
                if do_tail:
                    residual_sum(b, i_tail)
                residual_v(a, i)
                for c in range(2):
                    state_T(a, i, 2, c)
                    state_carry(a, i, 2, c)
                if do_norm:
                    embed_norm(a, i + 1)
                for c in range(2):
                    state_next(a, i, 2, c)
                if do_front:
                    maxima32(b, i_front)
                    differences2(b, i_front)
                for c in range(2):
                    state_T(a, i, 3, c)
                    state_carry(a, i, 3, c)
                if do_front:
                    differences3(b, i_front)
                for c in range(2):
                    state_next(a, i, 3, c)
                if do_norm:
                    attention_var(a, i + 1)
                    attention_norm(a, i + 1)
                if do_front:
                    maxima1_a(b, i_front)
                for c in range(2):
                    state_T(a, i, 4, c)
                    state_carry(a, i, 4, c)
                if do_front:
                    differences1_a(b, i_front)
                    kernel2_sums(b, i_front)
                    kernel2(b, i_front)
                for c in range(2):
                    state_next(a, i, 4, c)
                if do_front:
                    kernel1_b(b, i_front)
                for c in range(2):
                    state_T(a, i, 5, c)
                    state_carry(a, i, 5, c)
                for c in range(2):
                    state_next(a, i, 5, c)
                if do_front:
                    state_w(b, i_front)
                    scale_sum(b, i_front)
                    scale_spread(b, i_front)
                    state_X(b, i_front)
                inverse_kv(a, i)

            def phi_inverse():
                dve.wait_ge(phi_rooted, 1)
                dve.reciprocal(pht[:, :], pht[:, :]).then_inc(phi_steps, 1)

            def phi_newton_a():
                for k in range(2):
                    dve.wait_ge(phi_steps, k + 1)
                    dve.tensor_tensor(phn[:, :], phn[:, :], pht[:, :], ALU.mult).then_inc(phi_steps, 1)

            def phi_newton_b():
                dve.wait_ge(phi_steps, 3)
                dve.tensor_scalar(phn[:, :], phn[:, :], -0.5, 1.5, ALU.mult, ALU.add).then_inc(phi_steps, 1)
                dve.wait_ge(phi_steps, 4)
                dve.tensor_tensor(phn[:, :], phn[:, :], pht[:, :], ALU.mult).then_inc(phi_steps, 1)

            def phi_scale():
                dve.wait_ge(phi_steps, 5)
                dve.tensor_scalar(phn[:, :], phn[:, :], scl[:, :], None, ALU.mult).then_inc(phi_steps, 1)
                dve.wait_ge(phi_steps, 6)
                dve.tensor_tensor(phraw[:, 0, :], phraw[:, 0, :], phn[:, :], ALU.mult).then_inc(phi_steps, 1)
                dve.tensor_tensor(phraw[:, 1, :], phraw[:, 1, :], phn[:, :], ALU.mult).then_inc(phi_steps, 1)

            def phi_high():
                dve.wait_ge(phi_steps, 8)
                dve.tensor_copy(ph_hi[:, :], phraw[:, 0, :]).then_inc(phi_steps, 1)
                dve.tensor_copy(ph_st[:, :], phraw[:, 1, :]).then_inc(phi_steps, 1)

            def phi_low():
                dve.wait_ge(phi_steps, 10)
                dve.tensor_tensor(ph_lo[:, :], phraw[:, 0, :], ph_hi[:, :].bitcast(F32), ALU.subtract).then_inc(phi_steps, 1)
                dve.tensor_tensor(ph_st[64:128, :], phraw[64:128, 1, :], ph_st[64:128, :].bitcast(F32), ALU.subtract).then_inc(phi_steps, 1)

            def normalised(l, i):
                embed_sum(l, i)
                embed_stat(l, i)
                embed_var(l, i)
                embed_norm(l, i)
                attention_var(l, i)
                attention_norm(l, i)

            def start():
                normalised(0, 0)
                phi_inverse()
                landmarks(0, 0)
                phi_newton_a()
                maxima32(0, 0)
                differences2(0, 0)
                differences3(0, 0)
                normalised(1, 0)
                kernel2_sums(0, 0)
                kernel2(0, 0)
                maxima1_a(0, 0)
                differences1_a(0, 0)
                kernel1_b(0, 0)
                phi_newton_b()
                state_w(0, 0)
                scale_sum(0, 0)
                phi_scale()
                scale_spread(0, 0)
                state_X(0, 0)
                phi_high()
                phi_low()
                dve.wait_ge(tokens_in, 16 * (B - 2))

            def end():
                i = B // 2 - 1
                attended(1, i)
                residual_sum(1, i)

            attention_schedule(dve, phase, start, end)

            dve.wait_ge(a_attention_done, B)
            def row_stat(i, r):
                l = r % 2
                dve.bn_stats(rst6[l][:, :], h[:, bass.ds(8 * i + r, 1), :].rearrange("p o c -> p (o c)")).then_inc(r_row_stats, 1)

            def row_var(i, r):
                l = r % 2
                dve.wait_ge(r_row_stats, seq(i, r))
                dve.sem_inc(waited, 1)
                dve.bn_aggr(rmv[l][:, :], rst6[l][:, :]).then_inc(r_row_mean_var, 1)
                dve.wait_ge(r_row_mean_var, seq(i, r))
                dve.tensor_scalar(rve[l][:, :], rmv[l][:, 1:2], LN_EPS, 0.0, ALU.add, ALU.add).then_inc(r_row_var_eps, 1)

            def row_norm(i, r):
                l = r % 2
                dve.wait_ge(r_row_rstd, seq(i, r))
                dve.tensor_scalar(rx[l][:, :], h[:, bass.ds(8 * i + r, 1), :].rearrange("p o c -> p (o c)"),
                                  rmv[l][:, 0:1], rrs[l][:, :], ALU.subtract, ALU.mult).then_inc(r_rows_normed, 1)

            def row_unit(i, r):
                l = r % 2
                dve.wait_ge(r_inv_length, seq(i, r))
                if r >= 2:
                    dve.wait_ge(r_rows_low, seq(i, r - 2))
                dve.tensor_scalar(xe[l][:, 0:C], rx[l][:, :], rrn[l][:, :], None, ALU.mult).then_inc(r_unit_rows, 1)
                dve.tensor_scalar(xe[l][:, C:2 * P], rx[l][:, C0:C], rrn[l][:, :], None, ALU.mult).then_inc(r_unit_rows, 1)

            def transposed_low(i, r):
                l = r % 2
                dve.wait_ge(r_rowsT_high, seq(i, r))
                dve.tensor_tensor(xt_lo[l][:, :, :], bank[l][0][:, 0:2 * P].rearrange("p (a n) -> p a n", a=2), xt_hi[l][:, :, :].bitcast(F32), ALU.subtract).then_inc(r_rowsT_low, 1)

            def logits(l):
                return ps[:, 4 * l:4 * l + 2, :].rearrange("p a (e s) -> p (a e) s", s=SL)

            def maxima(i, r):
                l = r % 2
                dve.wait_ge(r_logits_psum, seq(i, r))
                dve.tensor_reduce(mx[l][:, :], logits(l), AX.X, ALU.max).then_inc(r_expert_max, 1)
                if r + 1 < 8:
                    transposed_low(i, r + 1)
                dve.wait_ge(r_expert_max, seq(i, r))
                dve.tensor_reduce(nm[l][:, :], mx[l][:, :], AX.X, ALU.max, negate=True).then_inc(r_row_max, 1)
                if r >= 2:
                    dve.wait_ge(r_combine, seq(i, r - 2))
                dve.tensor_tensor(lg[l][:, :, :], logits(l), bc(col(mx[l][:, :]), [P, E, SL]), ALU.subtract).then_inc(r_diffs, 1)

            def expert_sums(i, r):
                l = r % 2
                dve.wait_ge(r_exps, seq(i, r))
                dve.tensor_reduce(ze[l][:, :], lg[l][:, :, :], AX.X, ALU.add).then_inc(r_expert_sums, 1)
                dve.wait_ge(r_expert_sums, seq(i, r))
                dve.reciprocal(rz[l][:, :], ze[l][:, :]).then_inc(r_inv_expert_sums, 1)
                dve.wait_ge(r_exp_max, seq(i, r))
                dve.tensor_tensor(zf[l][:, :], ze[l][:, :], fe[l][:, :], ALU.mult).then_inc(r_weighted_sums, 1)
                dve.wait_ge(r_inv_expert_sums, seq(i, r))
                if r >= 2:
                    dve.wait_ge(r_combineT_psum, seq(i, r - 2))
                dve.tensor_tensor(dw[l][:, :, :], lg[l][:, :, :], bc(col(rz[l][:, :]), [P, E, SL]), ALU.mult).then_inc(r_dispatch, 1)

            def row_sum(i, r):
                l = r % 2
                dve.wait_ge(r_weighted_sums, seq(i, r))
                dve.tensor_reduce(zt[l][:, :], zf[l][:, :], AX.X, ALU.add).then_inc(r_row_sum, 1)
                dve.wait_ge(r_row_sum, seq(i, r))
                dve.reciprocal(rzt[l][:, :], zt[l][:, :]).then_inc(r_inv_row_sum, 1)
                dve.wait_ge(r_inv_row_sum, seq(i, r))
                dve.tensor_scalar(fz[l][:, :], fe[l][:, :], rzt[l][:, :], None, ALU.mult).then_inc(r_combine_factor, 1)

            def dispatch_low(i, r):
                l = r % 2
                dve.wait_ge(r_dispatch_high, seq(i, r))
                dve.tensor_tensor(dw_lo[l][:, :], dw[l][:, :, :].rearrange("p e s -> p (e s)"), dw_hi[l][:, :].bitcast(F32), ALU.subtract).then_inc(r_dispatch_low, 1)

            def start(i):
                for r in range(2):
                    row_stat(i, r)
                    row_var(i, r)
                    row_norm(i, r)
                    row_unit(i, r)
                transposed_low(i, 0)

            def phase(i, r):
                maxima(i, r)
                if r > 0:
                    dispatch_low(i, r - 1)
                if r + 2 < 8:
                    row_stat(i, r + 2)
                expert_sums(i, r)
                if r + 2 < 8:
                    row_var(i, r + 2)
                row_sum(i, r)
                if r + 2 < 8:
                    row_norm(i, r + 2)
                    row_unit(i, r + 2)

            def end(i):
                dispatch_low(i, 7)

            routing_schedule(dve, phase, start, end)

            def lo(e, m, q, part):
                if part == 0:
                    dve.wait_ge(w1_in[q], 48 * (m + 1))
                    dve.wait_ge(c_high_halves, 5 * e + 2)
                    dve.tensor_tensor(w1_lo[q][:, :], w1raw[q][:, 0, :], w1_hi[q][:, :].bitcast(F32), ALU.subtract).then_inc(c_w1_low, 1)
                    dve.tensor_tensor(w1_st[q][64:128, :], w1raw[q][64:128, 1, :], w1_st[q][64:128, :].bitcast(F32), ALU.subtract).then_inc(c_w1_low, 1)
                elif part == 1:
                    dve.wait_ge(slots_in[q], 48 * (m + 1))
                    dve.wait_ge(c_high_halves, 5 * e + 4)
                    dve.tensor_tensor(xs_lo[q][:, :, :], xsm[q][:, :, :], xs_hi[q][:, :, :].bitcast(F32), ALU.subtract).then_inc(c_slots_low, 1)
                else:
                    dve.wait_ge(w2_in[q], 16 * (m + 1))
                    dve.wait_ge(c_high_halves, 5 * e + 5)
                    dve.tensor_tensor(w2_hl[q][:, :, C:2 * C], w2raw[q][:, :, :], w2_hl[q][:, :, 0:C].bitcast(F32), ALU.subtract).then_inc(c_w2_low, 1)

            def combine(gr, k):
                dve.wait_ge(c_combined_psum, gr * (B // 2) + (k + 1))
                dve.tensor_tensor(h[:, 2 * k:2 * k + 2, :], h[:, 2 * k:2 * k + 2, :],
                                  ps[:, 6 + k % 2, 0:2 * C].rearrange("p (b d) -> p b d", b=2), ALU.add).then_inc(c_combined, 1)

            def biased(e, m, q, fresh):
                dve.wait_ge(b2_in[q], 16 * (m + 1))
                if not fresh:
                    dve.wait_ge(eog_in[q], 64 * m)
                for a in range(4):
                    dve.wait_ge(c_output_psum, OC * (e + 1) - 3 + a)
                    dve.tensor_tensor(eos[:, a, :], ps[:, 2 + a, 0:C], b2row[q][:, :], ALU.add).then_inc(c_output_partial, 1)
                for a in range(4):
                    dve.wait_ge(c_output_partial, 4 * e + a + 1)
                    dve.tensor_tensor(eo[q][:, a, :], eos[:, a, :], ps[:, 2 + a, C:2 * C], ALU.add).then_inc(c_output, 1)

            dve.wait_ge(slots_out, 32 * (B // 4))
            for l in range(4):
                dve.wait_ge(comb_out[l], 16 * (B // 4) + 16)
            dve.sem_inc(c_combined, 2)
            for part in range(3):
                lo(0, 0, 0, part)

            def group(gr, last, par):
                first = isinstance(gr, int) and gr == 0
                for j in range(GE):
                    e, q = gr * GE + j, j % 2
                    for k in range(HC):
                        t = j * HC + k
                        n = gr * (GE * HC) + t
                        dve.wait_ge(c_hidden_high, n + 1)
                        dve.tensor_tensor(h_lo[t % 3][:, :], hraw[t % 2][:, :], h_hi[t % 3][:, :].bitcast(F32), ALU.subtract).then_inc(c_hidden_low, 1)
                        if k == 0 and not (first and j == 0):
                            biased(e - 1, gr * 2 + (j - 1) // 2, (j - 1) % 2, first and j - 1 < 2)
                        if not first and COMB_AT < t <= COMB_AT + B // 2:
                            combine(gr - 1, t - COMB_AT - 1)
                        if 1 <= k <= 3 and not (last and j == GE - 1):
                            lo(gr * GE + (j + 1), gr * 2 + (j + 1) // 2, (j + 1) % 2, k - 1)

            group(0, False, 0)
            with dve.Fori(0, NG // 2 - 1) as i:
                for k in range(2):
                    group(2 * i + (k + 1), False, (k + 1) % 2)
            group(NG - 1, True, (NG - 1) % 2)
            biased(E - 1, E // 2 - 1, (E - 1) % 2, False)
            for b in range(B // 2):
                combine(NG - 1, b)

        @block.tensor
        def _(pe):
            mm = pe.matmul
            pe.wait_ge(identity_ready, 1)
            pe.wait_ge(wn_in, 48)
            for k in range(2):
                rows = P if k == 0 else 64
                for t in range(8):
                    last = pe.transpose(bank[0][2 * k + t // 4][0:rows, 96 * (t % 4):96 * (t % 4) + 96], wn[:, t, P * k:P * k + rows], ident[0:96, 0:96])
            last.then_inc(weights_transposed, 1)
            for t in range(2):
                last = pe.transpose(bank[1][0][:, 96 * t:96 * t + 96], b1n[:, t, :], ident[0:96, 0:96])
            last.then_inc(weights_transposed, 1)
            pe.wait_ge(phi_squared, 2)
            pe.wait_ge(memsets_done, 1)
            for a in range(2):
                mm(bank[1][1 + a], ones[:, :], phn[:, 512 * a:512 * a + 512], start=True, stop=False)
                last = mm(bank[1][1 + a], ones[0:64, :], pht[0:64, 512 * a:512 * a + 512], start=False, stop=True)
            last.then_inc(phi_summed, 1)
            pe.wait_ge(weights_ready, 6)
            pe.wait_ge(b1_ready, 1)
            pe.wait_ge(phi_sums_guarded, 1)
            pe.wait_ge(memsets_done, 21)

            def transpose_x(l, i):
                pe.wait_ge(a_rows_normed, now(l, i))
                pe.transpose(bank[l][0][:, 0:P], xn[l][:, 0:P], ident[:, 0:P])
                pe.transpose(bank[l][0][0:64, P:2 * P], xn[l][:, P:C], ident[:, 0:P]).then_inc(a_rowsT_psum, 1)

            def project_qk(l, i):
                pe.wait_ge(a_rowsT, now(l, i))
                for t in range(4):
                    mm(bank[l][1][:, P * t:P * t + P], wT[:, 0, P * t:P * t + P], xT[l][:, 0, :], start=True, stop=False)
                    last = mm(bank[l][1][:, P * t:P * t + P], wT[0:64, 1, P * t:P * t + P], xT[l][0:64, 1, :], start=False, stop=True)
                last.then_inc(a_qk_psum, 1)

            def project_v(l, i):
                mm(bank[l][2][:, 0:C], xT[l][:, 0, :], wT[:, 0, 512:704], start=True, stop=False)
                mm(bank[l][2][:, 0:C], xT[l][0:64, 1, :], wT[0:64, 1, 512:704], start=False, stop=True).then_inc(a_v_psum, 1)

            def scores32(l, i):
                pe.wait_ge(a_query_landmarks_bd, now(l, i))
                pe.wait_ge(a_key_landmarks, now(l, i))
                pe.wait_ge(a_keys, now(l, i))
                pe.wait_ge(a_values, now(l, i))
                for p in range(NP):
                    last = mm(bank[l][1 + p // 2][:, (P + M) * (p % 2):(P + M) * (p % 2 + 1)],
                              qbd[l][:, 2 * p:2 * p + 2, :].rearrange("p a n -> p (a n)"), kk[l][:, p // 4, :], start=True, stop=True)
                last.then_inc(a_scores32_psum, 1)

            def scores1_a(l, i):
                pe.wait_ge(a_key_landmarks_bd, now(l, i))
                mm(bank[l][0], qT[l][:, 0, :], kbd[l][:, 0:GH, :].rearrange("p a n -> p (a n)"), start=True, stop=True).then_inc(a_scores1_psum, 1)

            def scores1_b(l, i):
                pe.wait_ge(a_diff3, now(l, i))
                pe.wait_ge(a_diff2, now(l, i))
                mm(bank[l][1][:, 0:256], qT[l][:, 1, :], kbd[l][:, GH:H, :].rearrange("p a n -> p (a n)"), start=True, stop=True).then_inc(a_scores1_psum, 1)

            def transpose_k3(l, i):
                pe.wait_ge(a_exp3, now(l, i))
                for p in range(NP):
                    last = pe.transpose(bank[l][2 + p // 4][:, P * (p % 4):P * (p % 4) + P], e3[l][:, p, :], ident[:, 0:P])
                last.then_inc(a_kernel3T_psum, 1)

            def transpose_k2(l, i):
                pe.wait_ge(a_kernel2_bd, 2 * now(l, i))
                pe.wait_ge(a_diff1, first(l, i))
                pe.wait_ge(a_diff1, second(l, i))
                for p in range(NP):
                    last = mm(bank[l][p // 3][:, (P + 1) * (p % 3):(P + 1) * (p % 3 + 1)], k2[l][:, p, :], ident[:, :], start=True, stop=True)
                last.then_inc(a_kernel2T_psum, 1)

            def transpose_sums(l, i):
                pe.wait_ge(a_kernel2T, now(l, i))
                pe.transpose(bank[l][0][0:NP, 0:P], k2T[l][:, :, P], ident[:, 0:P]).then_inc(a_column_sums_psum, 1)

            def kernel3_v(l, i):
                pe.wait_ge(a_kernel3T, now(l, i))
                for p in range(NP):
                    last = mm(bank[l][3][:, SW * p:SW * p + SW], k3T[l][:, p, :], v33[l][:, p, :], start=True, stop=True)
                last.then_inc(a_kernel3_v_psum, 1)

            def kernel2_square(l, i):
                for p in range(NP):
                    last = mm(bank[l][1 + p // 4][:, P * (p % 4):P * (p % 4) + P], k2T[l][:, p, 0:P], k2T[l][:, p, 0:P], start=True, stop=True)
                last.then_inc(a_kernel2_square_psum, 1)

            def spread_scale(l, i):
                pe.wait_ge(a_scale_rows, now(l, i))
                mm(bank[l][0][:, 0:NP], csb[l][:, :, :].rearrange("p a n -> p (a n)"), ident[0:NP, 0:NP], start=True, stop=True).then_inc(a_scale_psum, 1)

            def square(l, i, k, c):
                pe.wait_ge(a_state_bd, 2 * step(l, i, k, c))
                if k == 0:
                    pe.wait_ge(a_state_w0, 2 * now(l, i))
                else:
                    pe.wait_ge(a_state, step(l, i, k - 1, c))
                for p in range(NP // 2):
                    last = mm(pA(l, c)[:, p, :], gbd[l][:, NP // 2 * c + p, :], g[l][:, NP // 2 * c + p, :], start=True, stop=True)
                last.then_inc(a_square_psum, 1)

            def times_T(l, i, k, c):
                pe.wait_ge(a_T, step(l, i, k, c))
                for p in range(NP // 2):
                    last = mm(pZ(l, c)[:, p, :], ybd[l][:, NP // 2 * c + p, :], tt[l][:, NP // 2 * c + p, :], start=True, stop=True)
                last.then_inc(a_YT_psum, 1)

            def transpose_k1(l, i):
                pe.wait_ge(a_exp1, now(l, i))
                for p in range(NP):
                    last = pe.transpose(bank[l][2 + p // 4][:, P * (p % 4):P * (p % 4) + P],
                                        e1[l][:, 2 * p:2 * p + 2, :].rearrange("p a n -> p (a n)"), ident[:, 0:P])
                last.then_inc(a_kernel1T_psum, 1)

            def inverse_kv(l, i):
                pe.wait_ge(a_state, step(l, i, ITERS - 1, 1))
                for p in range(NP):
                    last = mm(bank[l][1][:, SW * p:SW * p + SW], k2[l][:, p, :], g[l][:, p, 0:SW], start=True, stop=True)
                last.then_inc(a_inverse_kv_psum, 1)

            def attended(l, i):
                pe.wait_ge(a_inverse_kv_bd, 2 * now(l, i))
                pe.wait_ge(a_kernel1T, now(l, i))
                for p in range(NP):
                    last = mm(bank[l][3][:, SW * p:SW * p + SW], k1T[l][:, p, :], wbd[l][:, p, :], start=True, stop=True)
                last.then_inc(a_attended_psum, 1)

            def transpose_attended(l, i):
                pe.wait_ge(a_attended, now(l, i))
                pe.transpose(bank[l][3][:, 0:P], sv[l][:, 0:P], ident[:, 0:P])
                pe.transpose(bank[l][3][0:64, P:2 * P], sv[l][:, P:C], ident[:, 0:P]).then_inc(a_attendedT_psum, 1)

            def project_out(l, i):
                pe.wait_ge(a_attendedT, now(l, i))
                mm(bank[l][3][:, 0:C], svT[l][:, 0, :], pT[:, 0, :], start=True, stop=False)
                mm(bank[l][3][:, 0:C], svT[l][0:64, 1, :], pT[0:64, 1, :], start=False, stop=True).then_inc(a_projected_psum, 1)

            def phase(a, i, do_tail, do_front, do_norm):
                b, i_tail, i_front = other(a, i)
                for c in range(2):
                    square(a, i, 0, c)
                if do_front:
                    if do_tail:
                        pe.wait_ge(a_inverse_kv_bd, 2 * now(b, i_tail))
                    project_qk(b, i_front)
                for c in range(2):
                    times_T(a, i, 0, c)
                if do_tail:
                    attended(b, i_tail)
                for c in range(2):
                    square(a, i, 1, c)
                if do_tail:
                    transpose_attended(b, i_tail)
                if do_front:
                    project_v(b, i_front)
                for c in range(2):
                    times_T(a, i, 1, c)
                if do_tail:
                    project_out(b, i_tail)
                for c in range(2):
                    square(a, i, 2, c)
                if do_front:
                    if do_tail:
                        pe.wait_ge(a_attention_done, now(b, i_tail))
                    scores32(b, i_front)
                for c in range(2):
                    times_T(a, i, 2, c)
                if do_front:
                    scores1_a(b, i_front)
                for c in range(2):
                    square(a, i, 3, c)
                for c in range(2):
                    times_T(a, i, 3, c)
                if do_front:
                    scores1_b(b, i_front)
                for c in range(2):
                    square(a, i, 4, c)
                if do_front:
                    transpose_k3(b, i_front)
                for c in range(2):
                    times_T(a, i, 4, c)
                if do_front:
                    kernel3_v(b, i_front)
                for c in range(2):
                    square(a, i, 5, c)
                if do_front:
                    transpose_k2(b, i_front)
                for c in range(2):
                    times_T(a, i, 5, c)
                if do_front:
                    transpose_sums(b, i_front)
                    kernel2_square(b, i_front)
                inverse_kv(a, i)
                if do_norm:
                    transpose_x(a, i + 1)
                if do_front:
                    spread_scale(b, i_front)
                transpose_k1(a, i)

            def start():
                transpose_x(0, 0)
                project_qk(0, 0)
                project_v(0, 0)
                scores32(0, 0)
                scores1_a(0, 0)
                scores1_b(0, 0)
                transpose_k3(0, 0)
                transpose_k2(0, 0)
                kernel3_v(0, 0)
                transpose_sums(0, 0)
                kernel2_square(0, 0)
                spread_scale(0, 0)
                transpose_x(1, 0)

            def end():
                i = B // 2 - 1
                attended(1, i)
                transpose_attended(1, i)
                project_out(1, i)

            attention_schedule(pe, phase, start, end)

            pe.wait_ge(a_attention_done, B)
            pe.wait_ge(phi_steps, 12)
            def transpose_rows(i, r):
                l = r % 2
                pe.wait_ge(r_unit_rows, 2 * seq(i, r))
                if r >= 2:
                    pe.wait_ge(r_diffs, seq(i, r - 2))
                for a in range(2):
                    last = pe.transpose(bank[l][0][:, P * a:P * a + P], xe[l][:, P * a:P * a + P], ident[:, 0:P])
                last.then_inc(r_rowsT_psum, 1)

            def logits(i, r):
                l = r % 2
                pe.wait_ge(r_rowsT_high, seq(i, r))
                pe.wait_ge(r_rowsT_low, seq(i, r))
                for a in range(2):
                    cols = slice(512 * a, 512 * a + 512)
                    mm(bank[l][a], xt_hi[l][:, 0, :], ph_hi[:, cols], start=True, stop=False)
                    mm(bank[l][a], xt_hi[l][:, 0, :], ph_lo[:, cols], start=False, stop=False)
                    mm(bank[l][a], xt_lo[l][:, 0, :], ph_hi[:, cols], start=False, stop=False)
                    mm(bank[l][a], xt_hi[l][:, 1, :], ph_st[:, cols], start=False, stop=False)
                    last = mm(bank[l][a], xt_lo[l][:, 1, :], ph_st[:, cols], start=False, stop=True)
                last.then_inc(r_logits_psum, 1)

            def slots(i, r, part, done):
                l = r % 2
                for a in range(2):
                    cols = slice(512 * a, 512 * a + 512)
                    chans = slice(P * part, P * part + P)
                    mm(bank[l][2 + a], xe_hi[l][:, chans], dw_hi[l][:, cols], start=True, stop=False)
                    mm(bank[l][2 + a], xe_hi[l][:, chans], dw_lo[l][:, cols], start=False, stop=False)
                    last = mm(bank[l][2 + a], xe_lo[l][:, chans], dw_hi[l][:, cols], start=False, stop=True)
                last.then_inc(done, 1)

            def slots_main(i, r):
                pe.wait_ge(r_rows_low, seq(i, r))
                pe.wait_ge(r_dispatch_low, seq(i, r))
                if r >= 2:
                    pe.wait_ge(r_combineT, seq(i, r - 2))
                slots(i, r, 0, r_slots_main_psum)

            def slots_rest(i, r):
                pe.wait_ge(r_slots_main, seq(i, r))
                slots(i, r, 1, r_slots_rest_psum)

            def transpose_weights(i, r):
                l = r % 2
                pe.wait_ge(r_combine, seq(i, r))
                pe.wait_ge(r_slots_rest, seq(i, r))
                for gq in range(NG):
                    last = pe.transpose(bank[l][2 + gq // 4][:, P * (gq % 4):P * (gq % 4) + P],
                                        dw[l][:, GE * gq:GE * gq + GE, :].rearrange("p e s -> p (e s)"), ident[:, 0:P])
                last.then_inc(r_combineT_psum, 1)

            def start(i):
                transpose_rows(i, 0)
                logits(i, 0)

            def phase(i, r):
                if r + 1 < 8:
                    transpose_rows(i, r + 1)
                if r > 1:
                    transpose_weights(i, r - 2)
                if r + 1 < 8:
                    logits(i, r + 1)
                if r > 0:
                    slots_main(i, r - 1)
                    slots_rest(i, r - 1)

            def end(i):
                transpose_weights(i, 6)
                slots_main(i, 7)
                slots_rest(i, 7)
                transpose_weights(i, 7)
                pe.wait_ge(r_combineT, seq(i, 7))

            routing_schedule(pe, phase, start, end)

            def hidden(gr, t):
                j, k = t // HC, t % HC
                e, q = gr * GE + j, j % 2
                n = gr * (GE * HC) + t
                cols = slice(P * k, P * k + P)
                if k == 0:
                    pe.wait_ge(c_high_halves, 5 * e + 4)
                    pe.wait_ge(c_w1_low, 2 * e + 2)
                    pe.wait_ge(c_slots_low, e + 1)
                if not (isinstance(gr, int) and gr == 0 and t < 2):
                    pe.wait_ge(c_gelu, n - 1)
                dst = ps[:, t % 2, :]
                mm(dst, w1_hi[q][:, cols], xs_hi[q][:, 0, :], start=True, stop=False)
                mm(dst, w1_hi[q][:, cols], xs_lo[q][:, 0, :], start=False, stop=False)
                mm(dst, w1_lo[q][:, cols], xs_hi[q][:, 0, :], start=False, stop=False)
                mm(dst, w1_st[q][:, cols], xs_hi[q][:, 1, :], start=False, stop=False)
                mm(dst, w1_st[q][:, cols], xs_lo[q][:, 1, :], start=False, stop=True).then_inc(c_hidden_psum, 1)

            def output(gr, t):
                j, k = t // HC, t % HC
                e, q = gr * GE + j, j % 2
                n = gr * (GE * HC) + t
                if k == 0:
                    pe.wait_ge(c_high_halves, 5 * e + 5)
                    pe.wait_ge(c_w2_low, e + 1)
                pe.wait_ge(c_hidden_low, n + 1)
                for a in range(4):
                    rows = slice(P * a, P * a + P)
                    dst = ps[:, 2 + a, 0:C]
                    if k == 0 and not (isinstance(e, int) and e == 0):
                        pe.wait_ge(c_output, 4 * e - 3 + a)
                    mm(ps[:, 2 + a, 0:2 * C], h_hi[t % 3][:, rows], w2_hl[q][:, k, :], start=(k == 0), stop=False)
                    last = mm(dst, h_lo[t % 3][:, rows], w2_hl[q][:, k, 0:C], start=False, stop=(k == HC - 1))
                    if k == HC - 1:
                        last.then_inc(c_output_psum, 1)
                if k < HC - 1:
                    last.then_inc(c_output_psum, 1)

            def combine(gr, k, par):
                if k == 0:
                    pe.wait_ge(comb_in, 16 * (gr + 1))
                    for q in range(2):
                        pe.wait_ge(eog_in[q], 128 * (gr + 1))
                pe.wait_ge(c_combined, gr * (B // 2) + (k + 1))
                for b in range(2):
                    last = mm(ps[:, 6 + k % 2, C * b:C * b + C], cwg[par][:, 2 * k + b, :], eog[par][:, 2 * k + b, :], start=True, stop=True)
                last.then_inc(c_combined_psum, 1)

            pe.wait_ge(slots_out, 32 * (B // 4))
            for l in range(4):
                pe.wait_ge(comb_out[l], 16 * (B // 4) + 16)
            hidden(0, 0)
            hidden(0, 1)

            def group(gr, last, par):
                first = isinstance(gr, int) and gr == 0
                nt = GE * HC
                for t in range(nt):
                    if t + 2 < nt:
                        hidden(gr, t + 2)
                    elif not last:
                        hidden(gr + 1, t + 2 - nt)
                    output(gr, t)
                    if not first and COMB_AT <= t < COMB_AT + B // 2:
                        combine(gr - 1, t - COMB_AT, 1 - par)

            group(0, False, 0)
            with pe.Fori(0, NG // 2 - 1) as i:
                for k in range(2):
                    group(2 * i + (k + 1), False, (k + 1) % 2)
            group(NG - 1, True, (NG - 1) % 2)
            for k in range(B // 2):
                combine(NG - 1, k, (NG - 1) % 2)


_INS = ['x', 'mask_BS_i1_0', 'L0_tok_tok_w', 'L0_tok_pos_w', 'L0_tok_type_w', 'L0_tok_gamma', 'L0_tok_beta',
        'L0_attn_w_qkv', 'L0_attn_w_proj', 'L0_attn_b_proj', 'L0_ffn_phi', 'L0_ffn_scale', 'L0_ffn_w1',
        'L0_ffn_b1', 'L0_ffn_w2', 'L0_ffn_b2']
_OUTS = [((16, 128, 192), 'float32')]


def kernel(**inputs):
    import numpy as _np
    import concourse.bacc as _bacc
    from concourse.bass_utils import run_bass_kernel_spmd as _run

    nc = _bacc.Bacc("TRN2", target_bir_lowering=False, num_devices=1)
    arrays, args = {}, []
    for name in _INS:
        a = _np.ascontiguousarray(inputs[name])
        arrays[f"in_{name}_dram"] = a
        args.append(nc.dram_tensor(f"in_{name}_dram", a.shape, mybir.dt.from_np(a.dtype), kind="ExternalInput").ap())
    for i, (shape, dtype) in enumerate(_OUTS):
        args.append(nc.dram_tensor(f"out_{i}_dram", shape, mybir.dt.from_np(_np.dtype(dtype)), kind="ExternalOutput").ap())
    build(nc, *args)
    r = _run(nc, [arrays], core_ids=[0])
    return r.results[0]["out_0_dram"]
```
